# Optimizing a Trainium2 kernel written in Bass

```python
import numpy as np
import jax
import jax.numpy as jnp

def _softmax(x, axis=-1):
    return jax.nn.softmax(x, axis=axis)

def _gelu(x):
    return jax.nn.gelu(x, approximate=True)

def _silu(x):
    return jax.nn.silu(x)

def _sigmoid(x):
    return jax.nn.sigmoid(x)

def _layernorm(x, axis=-1, eps=1e-05):
    m = jnp.mean(x, axis=axis, keepdims=True)
    v = jnp.var(x, axis=axis, keepdims=True)
    return (x - m) / jnp.sqrt(v + eps)

def _scatter_add(tgt, idx, src, axis=0):
    return tgt.at[idx].add(src)

def _segment_sum(src, seg, n):
    return jax.ops.segment_sum(src, seg, n)
kernel_name = 'mk_vit_tower_postln_d2_tok_img256_r4_d77a67'

def setup_inputs(seed: int=0):
    np.random.seed(seed)
    _w = jnp.asarray

    def _rec_inputs():
        import jax
        import jax.numpy as jnp
        _rk = jax.random.key(seed)
        x = 7.22013e-05 + 1.00017 * jax.random.normal(jax.random.fold_in(_rk, 1), (8, 1, 1024, 64), jnp.float32)
        return x
    x = _rec_inputs()

    def _L0_tok_setup():
        import jax, jax.numpy as jnp
        import numpy as np
        T, D_IN, D_INT, D_OUT, B = (1024, 64, 64, 64, 8)
        key = jax.random.key(seed)
        ks = jax.random.split(key, 12)
        s_in = 1.0 / np.sqrt(D_IN)
        s_int = 1.0 / np.sqrt(D_INT)
        return {'x_batched': jax.random.normal(ks[0], (B, 1, T, D_IN), dtype=jnp.float32), 'd_gamma_batched': jax.random.uniform(ks[1], (T, T), dtype=jnp.float32), 'Wq': jax.random.uniform(ks[2], (D_IN, D_INT), jnp.float32, -s_in, s_in), 'bq': jax.random.uniform(ks[3], (D_INT,), jnp.float32, -s_in, s_in), 'Wk': jax.random.uniform(ks[4], (D_IN, D_INT), jnp.float32, -s_in, s_in), 'bk': jax.random.uniform(ks[5], (D_INT,), jnp.float32, -s_in, s_in), 'Wv': jax.random.uniform(ks[6], (D_IN, D_INT), jnp.float32, -s_in, s_in), 'bv': jax.random.uniform(ks[7], (D_INT,), jnp.float32, -s_in, s_in), 'Wo': jax.random.uniform(ks[8], (D_INT, D_OUT), jnp.float32, -s_int, s_int), 'bo': jax.random.uniform(ks[9], (D_OUT,), jnp.float32, -s_int, s_int), 'prelu_a': jnp.float32(0.25)}
    _L0_tok_all = _L0_tok_setup()
    _L0_tok_in = {k: v for k, v in _L0_tok_all.items() if k in ('d_gamma_batched', 'Wq', 'bq', 'Wk', 'bk', 'Wv', 'bv', 'Wo', 'bo', 'prelu_a')}
    del _L0_tok_all

    def _L0_attn_setup():
        import jax, jax.numpy as jnp
        import numpy as np
        B_, L_, D_ = (4, 512, 64)
        E_ = 128
        N_ = 16
        R_ = 16
        K_ = 4

        def _mamba_fwd(x, in_proj_w, conv_w, conv_b, sel_w, dt_w, dt_b, A, D_param, out_w):
            silu = jax.nn.silu
            xz = jnp.einsum('bld,ed->ble', x, in_proj_w)
            x_in, z = jnp.split(xz, 2, axis=-1)
            xc = jax.lax.conv_general_dilated(jnp.swapaxes(x_in, 1, 2), conv_w, (1,), [(K_ - 1, 0)], dimension_numbers=('NCL', 'OIL', 'NCL'), feature_group_count=E_)
            xc = silu(jnp.swapaxes(xc, 1, 2) + conv_b)
            sel = jnp.einsum('ble,se->bls', xc, sel_w)
            dt_in = sel[..., :R_]
            Bm = sel[..., R_:R_ + N_]
            Cm = sel[..., R_ + N_:]
            dt = jax.nn.softplus(jnp.einsum('blr,er->ble', dt_in, dt_w) + dt_b)
            dA = jnp.exp(dt[..., None] * A)
            dBu = dt[..., None] * Bm[:, :, None, :] * xc[..., None]

            def step(h, inp):
                dA_t, dBu_t, C_t = inp
                h = dA_t * h + dBu_t
                y = jnp.einsum('ben,bn->be', h, C_t)
                return (h, y)
            h0 = jnp.zeros((x.shape[0], E_, N_), x.dtype)
            _, ys = jax.lax.scan(step, h0, (jnp.moveaxis(dA, 1, 0), jnp.moveaxis(dBu, 1, 0), jnp.moveaxis(Cm, 1, 0)))
            y = jnp.moveaxis(ys, 0, 1) + D_param * xc
            y = y * silu(z)
            return jnp.einsum('ble,de->bld', y, out_w)
        key = jax.random.key(seed)
        ks = jax.random.split(key, 8)
        s = lambda k, sh, sc: jax.random.normal(k, sh, dtype=jnp.float32) * sc
        x = s(ks[0], (B_, L_, D_), 1.0)
        in_proj_w = s(ks[1], (2 * E_, D_), 0.02)
        conv_w = s(ks[2], (E_, 1, K_), 0.1)
        conv_b = jnp.zeros((E_,), jnp.float32)
        sel_w = s(ks[3], (R_ + 2 * N_, E_), 0.02)
        dt_w = s(ks[4], (E_, R_), 0.02)
        dt_b = jnp.full((E_,), -4.0, jnp.float32)
        A = -jnp.broadcast_to(jnp.arange(1, N_ + 1, dtype=jnp.float32), (E_, N_))
        D_param = jnp.ones((E_,), jnp.float32)
        out_w = s(ks[5], (D_, E_), 0.02)
        return dict(x=x, in_proj_w=in_proj_w, conv_w=conv_w, conv_b=conv_b, sel_w=sel_w, dt_w=dt_w, dt_b=dt_b, A=A, D_param=D_param, out_w=out_w)
    _L0_attn_all = _L0_attn_setup()
    _L0_attn_in = {k: v for k, v in _L0_attn_all.items() if k in ('in_proj_w', 'conv_w', 'conv_b', 'sel_w', 'dt_w', 'dt_b', 'A', 'D_param', 'out_w')}
    del _L0_attn_all

    def _L0_ffn_setup():
        import jax, jax.numpy as jnp
        import numpy as np
        D_MODEL = 64
        N_EXPERTS = 16
        HIDDEN = 128
        SCALE = 0.02
        key = jax.random.key(seed)
        ks = jax.random.split(key, 5)
        x = jax.random.normal(ks[0], (4, 2048, D_MODEL), dtype=jnp.float32)
        gate_w = jax.random.normal(ks[1], (D_MODEL, N_EXPERTS), dtype=jnp.float32) * SCALE
        gate_b = jnp.zeros((N_EXPERTS,), dtype=jnp.float32)
        w1 = jax.random.normal(ks[2], (N_EXPERTS, D_MODEL, HIDDEN), dtype=jnp.float32) * SCALE
        w2 = jax.random.normal(ks[3], (N_EXPERTS, D_MODEL, HIDDEN), dtype=jnp.float32) * SCALE
        w3 = jax.random.normal(ks[4], (N_EXPERTS, HIDDEN, D_MODEL), dtype=jnp.float32) * SCALE
        return {'x': x, 'gate_w': gate_w, 'gate_b': gate_b, 'w1': w1, 'w2': w2, 'w3': w3}
    _L0_ffn_all = _L0_ffn_setup()
    _L0_ffn_in = {k: v for k, v in _L0_ffn_all.items() if k in ('gate_w', 'gate_b', 'w1', 'w2', 'w3')}
    del _L0_ffn_all

    def _L1_attn_setup():
        import jax, jax.numpy as jnp
        import numpy as np
        DIM = 64
        WS = 64
        H = 8
        HD = DIM // H
        SCALE = HD ** (-0.5)
        key = jax.random.key(seed)
        k1, k2, k3, k4 = jax.random.split(key, 4)
        B, L = (8, 4096)
        x = jax.random.normal(k1, (B, L, DIM), dtype=jnp.float32)
        w_qkv = jax.random.normal(k2, (3 * DIM, DIM), dtype=jnp.float32) * DIM ** (-0.5)
        w_proj = jax.random.normal(k3, (DIM, DIM), dtype=jnp.float32) * DIM ** (-0.5)
        b_proj = jnp.zeros((DIM,), dtype=jnp.float32)
        rel_bias = jax.random.normal(k4, (2 * WS - 1,), dtype=jnp.float32) * 0.02
        return {'x': x, 'w_qkv': w_qkv, 'w_proj': w_proj, 'b_proj': b_proj, 'rel_bias': rel_bias}
    _L1_attn_all = _L1_attn_setup()
    _L1_attn_in = {k: v for k, v in _L1_attn_all.items() if k in ('w_qkv', 'w_proj', 'b_proj', 'rel_bias')}
    del _L1_attn_all

    def _L1_ffn_setup():
        import jax, jax.numpy as jnp
        import numpy as np
        B, T, IN_DIM = (64, 64, 64)
        HID, OUT_DIM = (128, 64)
        N_LAYERS, N_EXPERTS, N_SHARED = (2, 16, 1)
        key = jax.random.key(seed)
        ks = jax.random.split(key, 10)
        s = 0.02
        x = jax.random.normal(ks[0], (B, T, IN_DIM), dtype=jnp.float32)
        route_id = jax.random.randint(ks[1], (B,), 0, N_EXPERTS)
        Wi = jax.random.normal(ks[2], (HID, IN_DIM), dtype=jnp.float32) * s
        bi = jnp.zeros((HID,), dtype=jnp.float32)
        Wr = jax.random.normal(ks[3], (N_LAYERS, N_EXPERTS, HID, HID), dtype=jnp.float32) * s
        br = jax.random.normal(ks[4], (N_LAYERS, N_EXPERTS, HID), dtype=jnp.float32) * s
        Ws = jax.random.normal(ks[5], (N_LAYERS, N_SHARED, HID, HID), dtype=jnp.float32) * s
        bs = jax.random.normal(ks[6], (N_LAYERS, N_SHARED, HID), dtype=jnp.float32) * s
        Wo = jax.random.normal(ks[7], (OUT_DIM, HID), dtype=jnp.float32) * s
        bo = jnp.zeros((OUT_DIM,), dtype=jnp.float32)
        return {'x': x, 'route_id': route_id, 'Wi': Wi, 'bi': bi, 'Wr': Wr, 'br': br, 'Ws': Ws, 'bs': bs, 'Wo': Wo, 'bo': bo}
    _L1_ffn_all = _L1_ffn_setup()
    _L1_ffn_in = {k: v for k, v in _L1_ffn_all.items() if k in ('route_id', 'Wi', 'bi', 'Wr', 'br', 'Ws', 'bs', 'Wo', 'bo')}
    del _L1_ffn_all
    return {'x': x, 'L0_tok_d_gamma_batched': _L0_tok_in['d_gamma_batched'], 'L0_tok_Wq': _L0_tok_in['Wq'], 'L0_tok_bq': _L0_tok_in['bq'], 'L0_tok_Wk': _L0_tok_in['Wk'], 'L0_tok_bk': _L0_tok_in['bk'], 'L0_tok_Wv': _L0_tok_in['Wv'], 'L0_tok_bv': _L0_tok_in['bv'], 'L0_tok_Wo': _L0_tok_in['Wo'], 'L0_tok_bo': _L0_tok_in['bo'], 'L0_tok_prelu_a': _L0_tok_in['prelu_a'], 'L0_attn_in_proj_w': _L0_attn_in['in_proj_w'], 'L0_attn_conv_w': _L0_attn_in['conv_w'], 'L0_attn_conv_b': _L0_attn_in['conv_b'], 'L0_attn_sel_w': _L0_attn_in['sel_w'], 'L0_attn_dt_w': _L0_attn_in['dt_w'], 'L0_attn_dt_b': _L0_attn_in['dt_b'], 'L0_attn_A': _L0_attn_in['A'], 'L0_attn_D_param': _L0_attn_in['D_param'], 'L0_attn_out_w': _L0_attn_in['out_w'], 'L0_ffn_gate_w': _L0_ffn_in['gate_w'], 'L0_ffn_gate_b': _L0_ffn_in['gate_b'], 'L0_ffn_w1': _L0_ffn_in['w1'], 'L0_ffn_w2': _L0_ffn_in['w2'], 'L0_ffn_w3': _L0_ffn_in['w3'], 'L1_attn_w_qkv': _L1_attn_in['w_qkv'], 'L1_attn_w_proj': _L1_attn_in['w_proj'], 'L1_attn_b_proj': _L1_attn_in['b_proj'], 'L1_attn_rel_bias': _L1_attn_in['rel_bias'], 'L1_ffn_route_id': _L1_ffn_in['route_id'], 'L1_ffn_Wi': _L1_ffn_in['Wi'], 'L1_ffn_bi': _L1_ffn_in['bi'], 'L1_ffn_Wr': _L1_ffn_in['Wr'], 'L1_ffn_br': _L1_ffn_in['br'], 'L1_ffn_Ws': _L1_ffn_in['Ws'], 'L1_ffn_bs': _L1_ffn_in['bs'], 'L1_ffn_Wo': _L1_ffn_in['Wo'], 'L1_ffn_bo': _L1_ffn_in['bo']}

def reference(x, L0_tok_d_gamma_batched, L0_tok_Wq, L0_tok_bq, L0_tok_Wk, L0_tok_bk, L0_tok_Wv, L0_tok_bv, L0_tok_Wo, L0_tok_bo, L0_tok_prelu_a, L0_attn_in_proj_w, L0_attn_conv_w, L0_attn_conv_b, L0_attn_sel_w, L0_attn_dt_w, L0_attn_dt_b, L0_attn_A, L0_attn_D_param, L0_attn_out_w, L0_ffn_gate_w, L0_ffn_gate_b, L0_ffn_w1, L0_ffn_w2, L0_ffn_w3, L1_attn_w_qkv, L1_attn_w_proj, L1_attn_b_proj, L1_attn_rel_bias, L1_ffn_route_id, L1_ffn_Wi, L1_ffn_bi, L1_ffn_Wr, L1_ffn_br, L1_ffn_Ws, L1_ffn_bs, L1_ffn_Wo, L1_ffn_bo):
    import jax
    import jax.numpy as jnp

    def _L0_tok_ref(x_batched, d_gamma_batched, Wq, bq, Wk, bk, Wv, bv, Wo, bo, prelu_a):
        import jax, jax.numpy as jnp
        import numpy as np
        T, D_IN, D_INT, D_OUT, B = (1024, 64, 64, 64, 8)
        x = x_batched.reshape(x_batched.shape[0], T, D_IN)
        q = x @ Wq + bq
        k = x @ Wk + bk
        v = x @ Wv + bv
        scores = jnp.einsum('btd,bsd->bts', q, k)
        retained = jnp.einsum('bts,bsd->btd', d_gamma_batched * scores, v)
        y = retained @ Wo + bo
        out = jnp.where(y >= 0, y, prelu_a * y)
        return out

    def _L0_attn_ref(x, in_proj_w, conv_w, conv_b, sel_w, dt_w, dt_b, A, D_param, out_w):
        import jax, jax.numpy as jnp
        import numpy as np
        B_, L_, D_ = (4, 512, 64)
        E_ = 128
        N_ = 16
        R_ = 16
        K_ = 4

        def _mamba_fwd(x, in_proj_w, conv_w, conv_b, sel_w, dt_w, dt_b, A, D_param, out_w):
            silu = jax.nn.silu
            xz = jnp.einsum('bld,ed->ble', x, in_proj_w)
            x_in, z = jnp.split(xz, 2, axis=-1)
            xc = jax.lax.conv_general_dilated(jnp.swapaxes(x_in, 1, 2), conv_w, (1,), [(K_ - 1, 0)], dimension_numbers=('NCL', 'OIL', 'NCL'), feature_group_count=E_)
            xc = silu(jnp.swapaxes(xc, 1, 2) + conv_b)
            sel = jnp.einsum('ble,se->bls', xc, sel_w)
            dt_in = sel[..., :R_]
            Bm = sel[..., R_:R_ + N_]
            Cm = sel[..., R_ + N_:]
            dt = jax.nn.softplus(jnp.einsum('blr,er->ble', dt_in, dt_w) + dt_b)
            dA = jnp.exp(dt[..., None] * A)
            dBu = dt[..., None] * Bm[:, :, None, :] * xc[..., None]

            def step(h, inp):
                dA_t, dBu_t, C_t = inp
                h = dA_t * h + dBu_t
                y = jnp.einsum('ben,bn->be', h, C_t)
                return (h, y)
            h0 = jnp.zeros((x.shape[0], E_, N_), x.dtype)
            _, ys = jax.lax.scan(step, h0, (jnp.moveaxis(dA, 1, 0), jnp.moveaxis(dBu, 1, 0), jnp.moveaxis(Cm, 1, 0)))
            y = jnp.moveaxis(ys, 0, 1) + D_param * xc
            y = y * silu(z)
            return jnp.einsum('ble,de->bld', y, out_w)
        return _mamba_fwd(x, in_proj_w, conv_w, conv_b, sel_w, dt_w, dt_b, A, D_param, out_w)

    def _L0_ffn_ref(x, gate_w, gate_b, w1, w2, w3):
        import jax, jax.numpy as jnp
        import numpy as np
        D_MODEL = 64
        N_EXPERTS = 16
        HIDDEN = 128
        SCALE = 0.02
        n_experts = w1.shape[0]
        logits = jnp.einsum('bsd,de->bse', x, gate_w) + gate_b
        probs = jax.nn.softmax(logits, axis=-1)
        top_probs, top_idx = jax.lax.top_k(probs, 2)
        top_probs = top_probs / jnp.sum(top_probs, axis=-1, keepdims=True)
        dispatch = jnp.sum(jax.nn.one_hot(top_idx, n_experts, dtype=x.dtype) * top_probs[..., None], axis=-2)
        h1 = jnp.einsum('bsd,edh->bseh', x, w1)
        h2 = jnp.einsum('bsd,edh->bseh', x, w2)
        hidden = jax.nn.silu(h1) * h2
        expert_out = jnp.einsum('bseh,eho->bseo', hidden, w3)
        return jnp.einsum('bseo,bse->bso', expert_out, dispatch)

    def _L1_attn_ref(x, w_qkv, w_proj, b_proj, rel_bias):
        import jax, jax.numpy as jnp
        import numpy as np
        DIM = 64
        WS = 64
        H = 8
        HD = DIM // H
        SCALE = HD ** (-0.5)
        B, L, C = x.shape
        pad_len = (WS - L % WS) % WS
        if pad_len > 0:
            x = jnp.pad(x, ((0, 0), (0, pad_len), (0, 0)))
        padded_L = x.shape[1]
        nw = padded_L // WS
        xw = x.reshape(B, nw, WS, C)
        qkv = jnp.einsum('bnwc,oc->bnwo', xw, w_qkv)
        qkv = qkv.reshape(B, nw, WS, 3, H, HD)
        q = jnp.transpose(qkv[..., 0, :, :], (0, 1, 3, 2, 4))
        k = jnp.transpose(qkv[..., 1, :, :], (0, 1, 3, 2, 4))
        v = jnp.transpose(qkv[..., 2, :, :], (0, 1, 3, 2, 4))
        attn = jnp.einsum('bnhqd,bnhkd->bnhqk', q, k) * SCALE
        pos = jnp.arange(WS)
        rel_idx = pos[None, :] - pos[:, None] + WS - 1
        attn = attn + rel_bias[rel_idx]
        attn = jax.nn.softmax(attn, axis=-1)
        out = jnp.einsum('bnhqk,bnhkd->bnhqd', attn, v)
        out = jnp.transpose(out, (0, 1, 3, 2, 4)).reshape(B, nw, WS, C)
        out = jnp.einsum('bnwc,oc->bnwo', out, w_proj) + b_proj
        out = out.reshape(B, padded_L, C)
        if pad_len > 0:
            out = out[:, :L, :]
        return out

    def _L1_ffn_ref(x, route_id, Wi, bi, Wr, br, Ws, bs, Wo, bo):
        import jax, jax.numpy as jnp
        import numpy as np
        B, T, IN_DIM = (64, 64, 64)
        HID, OUT_DIM = (128, 64)
        N_LAYERS, N_EXPERTS, N_SHARED = (2, 16, 1)
        flat = x.reshape(-1, x.shape[-1])
        n_tok = flat.shape[0]
        route = jnp.repeat(route_id, n_tok // route_id.shape[0])
        h = jax.nn.relu(flat @ Wi.T + bi)
        n_layers, n_experts = (Wr.shape[0], Wr.shape[1])
        for l in range(n_layers):
            shared = (jnp.einsum('nd,shd->snh', h, Ws[l]) + bs[l][:, None, :]).mean(axis=0)
            routed = jnp.zeros_like(h)
            for e in range(n_experts):
                ye = h @ Wr[l, e].T + br[l, e]
                routed = routed + jnp.where((route == e)[:, None], ye, 0.0)
            h = jax.nn.relu(shared + routed + h)
        out = h @ Wo.T + bo
        return out.reshape(*x.shape[:-1], out.shape[-1])
    h = _L0_tok_ref(x, L0_tok_d_gamma_batched, L0_tok_Wq, L0_tok_bq, L0_tok_Wk, L0_tok_bk, L0_tok_Wv, L0_tok_bv, L0_tok_Wo, L0_tok_bo, L0_tok_prelu_a)
    h = _layernorm(h + _L0_attn_ref(h, L0_attn_in_proj_w, L0_attn_conv_w, L0_attn_conv_b, L0_attn_sel_w, L0_attn_dt_w, L0_attn_dt_b, L0_attn_A, L0_attn_D_param, L0_attn_out_w), axis=-1)
    h = _layernorm(h + _L0_ffn_ref(h, L0_ffn_gate_w, L0_ffn_gate_b, L0_ffn_w1, L0_ffn_w2, L0_ffn_w3), axis=-1)
    h = _layernorm(h + _L1_attn_ref(h, L1_attn_w_qkv, L1_attn_w_proj, L1_attn_b_proj, L1_attn_rel_bias), axis=-1)
    h = _layernorm(h + _L1_ffn_ref(h, L1_ffn_route_id, L1_ffn_Wi, L1_ffn_bi, L1_ffn_Wr, L1_ffn_br, L1_ffn_Ws, L1_ffn_bs, L1_ffn_Wo, L1_ffn_bo), axis=-1)
    return h

_drawn_inputs = setup_inputs


def setup_inputs(seed=0):
    import zlib

    import numpy as np

    out = dict(_drawn_inputs(seed))
    spreads = {'L0_attn_conv_b': (0.0, 0.8),
     'L0_attn_dt_b': (-4.0, 0.6),
     'L0_attn_D_param': (1.0, 0.6),
     'L0_ffn_gate_b': (0.0, 0.8),
     'L1_attn_b_proj': (0.0, 0.1),
     'L1_ffn_bi': (0.0, 0.584),
     'L1_ffn_bo': (0.0, 0.1)}
    factors = {'L0_tok_bo': 8.0,
     'L0_attn_sel_w': 8.0,
     'L0_attn_dt_w': 8.0,
     'L0_attn_A': 8.0,
     'L0_ffn_gate_w': 8.0,
     'L0_ffn_w1': 8.0,
     'L0_ffn_w2': 8.0,
     'L0_ffn_w3': 8.0,
     'L1_attn_rel_bias': 8.0,
     'L1_ffn_Wi': 2.807,
     'L1_ffn_Wr': 7.667,
     'L1_ffn_br': 8.0,
     'L1_ffn_Ws': 6.857,
     'L1_ffn_bs': 8.0}
    for name, (base, spread) in spreads.items():
        noise = np.random.default_rng([zlib.crc32(name.encode()), seed]).standard_normal(out[name].shape)
        drawn = base * np.exp(spread * noise) if base else spread * noise
        out[name] = jnp.asarray(drawn.astype(out[name].dtype))
    for name, factor in factors.items():
        out[name] = (out[name] * factor).astype(out[name].dtype)
    return out
```

```python
from contextlib import ExitStack

import numpy as np

import concourse.bass as bass
from concourse import mybir

F32 = mybir.dt.float32
BF16 = mybir.dt.bfloat16
I32 = mybir.dt.int32
ALU = mybir.AluOpType
ACT = mybir.ActivationFunctionType
AX = mybir.AxisListType

P = 128
B, T, D = 8, 1024, 64
PAIRS = B // 2
NT = T // P
CH = 512
NC = T // CH
E = 128
NS = 16
NX = 16
HID = 128
WS, H, HD = 64, 8, 8
NW = T // WS
LAYERS = 2
EPS = 1e-5
WCOL = HID + 1

PER = dict(
    x_loaded=16, w_routed=16 * LAYERS * 2 * NT, stored=16,
    q_ps=NC, k_ps=NC, vw_ps=2, qk_sb=2 * NC, vw_sb=2, scores=2 * NT, masked=2 * NT, retained=2 * NT,
    y_ready=2, yT_ps=2, h0_ready=2,
    xin_ps=2, xin_sb=2, z_ps=2, z_ready=2, conv_ready=2, xc_ready=2, sel_ps=2, dt_ps=2, sel_hi=2, sel_split=2,
    dt_neg=2, dt_ln=2, dt_ready=2, u_ready=2,
    b_ps=2 * NS, c_ps=2 * NS, dA_ready=2 * NS, c_sb=2 * NS, dbu_ready=2 * NS, scanned=2 * NS, hc_ready=2 * NS,
    y_summed=2 * NS, y_read=2, gated_y=2, mamba_ps=2,
    logit_ps=1, top_diff=1, top_exp=1, hh_ps=4 * NX, silu_ready=4 * NX, hidden=4 * NX, expert_ps=4 * NX,
    gated=4 * NX, summed=4 * (NX - 1), moeT_ps=1,
    q_zero=2, aq_ps=NC, ak_ps=NC, av_ps=2, q_blocks=2 * NC, k_blocks=H, v_blocks=4, att_ps=NW, biased=NW, row_max=NW,
    shifted=NW, att_exp=NW, probT_ps=NW, probT_sb=NW, pv_ps=NW, normed=NW, outT_ps=NW // 2, outT_sb=NW // 2,
    proj_ps=NW // 2,
    f_in_ps=2, f0_ready=2, l0_ps=2, l1_ps=2, l0_first=1, l0_second=1, l1_first=1, l1_second=1, f_out_ps=1,
    r_ready=8, centred=8, squared=8, var_ps=8, ln_log=8, rstd=8, h_ready=8,
)


def build_tower(nc, i, out):
    with ExitStack() as ctx:
        def sb(name, shape, dt=F32):
            return ctx.enter_context(nc.sbuf_tensor(name, shape, dt))

        sem = {n: ctx.enter_context(nc.semaphore(n)) for n in PER}
        loaded = ctx.enter_context(nc.semaphore("loaded"))
        zeroed = ctx.enter_context(nc.semaphore("zeroed"))
        fold_ps = ctx.enter_context(nc.semaphore("fold_ps"))
        fold_sb = ctx.enter_context(nc.semaphore("fold_sb"))
        table_stored = ctx.enter_context(nc.semaphore("table_stored"))
        shared_ready = ctx.enter_context(nc.semaphore("shared_ready"))
        table_ready = ctx.enter_context(nc.semaphore("table_ready"))
        dve_chain = ctx.enter_context(nc.semaphore("dve_chain"))
        act_chain = ctx.enter_context(nc.semaphore("act_chain"))
        pair_done = ctx.enter_context(nc.semaphore("pair_done"))

        decayT = sb("decayT", [P, NT, T])
        wq_bd = sb("wq_bd", [P, P])
        wk_bd = sb("wk_bd", [P, P])
        wvo_bd = sb("wvo_bd", [P, P])
        wvT = sb("wvT", [D, D])
        wo_tok = sb("wo_tok", [D, D])
        vec = sb("vec", [P, i["vec"].shape[1]])
        rows = sb("rows", [P, i["rows"].shape[1]])
        in_proj = sb("in_proj", [P, 2 * E])
        selT = sb("selT", [P, P])
        sel_dt = sb("sel_dt", [NS, E])
        dt_wT = sb("dt_wT", [NS, E])
        w_dt = sb("w_dt", [P, E])
        out_wT = sb("out_wT", [P, D])
        gate_bd = sb("gate_bd", [P, 2 * NX])
        w1 = sb("w1", [P, NX, HID])
        w2 = sb("w2", [P, NX, HID])
        w3 = sb("w3", [P, NX, D])
        aq_bd = sb("aq_bd", [P, P])
        ak_bd = sb("ak_bd", [P, P])
        av_bd = sb("av_bd", [P, P])
        projT = sb("projT", [P, 2, D])
        fiT = sb("fiT", [P, HID])
        foT = sb("foT", [P, D])
        wsT = sb("wsT", [P, LAYERS, HID])
        table_dram = nc.dram_tensor("routed_table", (P, LAYERS, NX, WCOL), F32, kind="Internal").ap()
        consts = sb("consts", [P, i["consts"].shape[1]])
        pick = sb("pick", [P, 2 * NS, P], BF16)
        route = sb("route", [1, B * NT], I32)
        ident = consts[:, 0:P]
        centre = consts[:, P:2 * P]
        average = consts[:, 2 * P:3 * P]
        head_mask = consts[:, 3 * P:3 * P + H]
        order = consts[:, 3 * P + H:3 * P + H + NX]
        VEC = {n: k for k, n in enumerate(i["vec_names"])}

        def v(name, k=0):
            return vec[:, VEC[name] + k:VEC[name] + k + 1]

        vo_row = sb("vo_row", [P, P])
        bo_row = rows[:, 0:D]
        gate_row = rows[:, D:D + NX]
        rel_row = rows[:, D + NX:D + NX + WS]

        xT = sb("xT", [P, T])
        even, odd = sb("h_even", [P, T]), sb("h_odd", [P, T])
        h = [even, odd, even, odd, even]
        res = sb("res", [P, T])
        sq = sb("sq", [P, T])
        rs = sb("rs", [P, T])
        y_tok = sb("y_tok", [P, NT, 2, D])
        xpad = sb("xpad", [P, 2, T + 3])
        xc = sb("xc", [P, 2, T])
        zs = sb("zs", [P, 2, T])
        bc = sb("bc", [P, 2, T], BF16)
        steps = sb("steps", [P, LAYERS * 2 * NT * WCOL])
        dt = steps[:, 0:2 * T].rearrange("p (g t) -> p g t", g=2)
        u = steps[:, 2 * T:4 * T].rearrange("p (g t) -> p g t", g=2)
        scratch = sb("scratch", [P, 10, T])
        qk = dt
        vw = xc[:, 0, :].rearrange("p (a b) -> p a b", a=NT)
        y_neg = zs[:, 0, :].rearrange("p (t g d) -> p t g d", t=NT, g=2)
        w_ring = steps[:, :].rearrange("p (l g t c) -> p l g t c", l=LAYERS, g=2, t=NT)
        table = scratch[:, 0:5].rearrange("p a b -> p (a b)")[:, 0:LAYERS * NX * WCOL]\
            .rearrange("p (l e c) -> p l e c", l=LAYERS, e=NX)
        logits = sb("logits", [P, NT * 2, NX])
        logits2 = sb("logits2", [P, NT * 2, NX])
        hit = sb("hit", [P, NT * 2, NX])
        pick1 = sb("pick1", [P, NT * 2, NX])
        pick2 = sb("pick2", [P, NT * 2, NX])
        gates = sb("gates", [P, NT * 2, NX])
        m1 = sb("m1", [P, NT * 2])
        m2 = sb("m2", [P, NT * 2])
        mo = sb("mo", [P, NT * 2])
        g1 = sb("g1", [P, NT * 2])
        g2 = sb("g2", [P, NT * 2])
        acc = y_tok
        vb = sb("vb", [P, NW, H // 2, 2, 2, HD + 1])
        qb = scratch[:, 8:10].rearrange("p a (w q) -> p (a w) q", q=P)
        rmax = sb("rmax", [P, 2, H])
        rsum = sb("rsum", [P, 2, H])

        ps = ctx.enter_context(nc.psum_tensor("ps", [P, 8, CH], F32))

        def banks(k, n=2):
            return ps[:, k:k + n, :].rearrange("p a b -> p (a b)")

        block = ctx.enter_context(nc.Block())

        def att_bias(w):
            return sq[:, (w % 2) * CH:(w % 2 + 1) * CH]

        def att_shift(w):
            return rs[:, (w % 2) * CH:(w % 2 + 1) * CH]

        def att_prob(w):
            return xc[:, 0, (w % 2) * CH:(w % 2 + 1) * CH]

        def att_probT(w):
            return zs[:, 0, (w % 2) * CH:(w % 2 + 1) * CH]

        def att_out(m):
            return xc[:, 1, (m % 2) * P:(m % 2 + 1) * P]

        def att_outT(m):
            return zs[:, 1, (m % 2) * P:(m % 2 + 1) * P]

        kb = scratch[:, 0:8].rearrange("p a (w h k) -> p (a w) h k", w=2, h=H)

        def gated_out(k):
            return scratch[:, 6 + k % 2, 0:4 * D].rearrange("p (a b) -> p a b", a=4)

        def ffn_in(l, g):
            return scratch[:, 2 * l + g]

        def at(pair, name, n):
            return pair * PER[name] + n

        def link(e, chain, per_pair, pair, count, ins):
            count[0] += 1
            ins.then_inc(chain, 1)
            e.wait_ge(chain, pair * per_pair + count[0])

        @block.sync
        def _(sp):
            n = 0
            sp.wait_ge(zeroed, 5)
            for dst, src in [
                (decayT[:, :, :], i["decayT"]), (wvT[:, :], i["wvT"]), (wo_tok[:, :], i["wo_tok"]),
                (wq_bd[0:D, 0:D], i["wq"]), (wq_bd[D:P, D:P], i["wq"]),
                (wk_bd[0:D, 0:D], i["wk"]), (wk_bd[D:P, D:P], i["wk"]),
                (vec[:, :], i["vec"]), (rows[:, :], i["rows"]), (consts[:, :], i["consts"]),
                (pick[:, :, :], i["pick"]), (in_proj[0:D, :], i["in_projT"]), (in_proj[D:P, :], i["in_projT"]),
                (selT[:, :], i["selT"]), (sel_dt[:, :], i["sel_dt"]), (dt_wT[:, :], i["dt_wT"]),
                (out_wT[:, :], i["out_wT"]),
                (gate_bd[0:D, 0:NX], i["gate_w"]), (gate_bd[D:P, NX:2 * NX], i["gate_w"]),
                (w1[0:D], i["w1"]), (w1[D:P], i["w1"]), (w2[0:D], i["w2"]), (w2[D:P], i["w2"]), (w3[:, :, :], i["w3"]),
                (aq_bd[0:D, 0:D], i["aqT"]), (aq_bd[D:P, D:P], i["aqT"]),
                (ak_bd[0:D, 0:D], i["akT"]), (ak_bd[D:P, D:P], i["akT"]),
                (av_bd[0:D, 0:D], i["avT"]), (av_bd[D:P, D:P], i["avT"]),
                (projT[0:D, 0, :], i["projT"]), (projT[D:P, 1, :], i["projT"]),
                (fiT[0:D, :], i["fiT"]), (fiT[D:P, :], i["fiT"]), (foT[:, :], i["foT"]), (wsT[:, :, :], i["wsT"]),
                (table, i["table"]), (route[:, :], i["route"]),
            ]:
                sp.dma_start(dst, src).then_inc(loaded, 16)
                n += 1
            assert n == LOADS
            sp.wait_ge(table_ready, 1 + LAYERS)
            sp.dma_start(table_dram, table).then_inc(table_stored, 16)
            with sp.Fori(0, PAIRS) as pair:
                sp.wait_ge(pair_done, pair + 1)
                sp.dma_start(xT[:, :], i["xT"][:, bass.ts(pair, T)]).then_inc(sem["x_loaded"], 16)
                sp.wait_ge(table_stored, 16)
                sp.wait_ge(sem["h_ready"], at(pair, "h_ready", 2))
                for g in range(2):
                    for j in range(NT):
                        expert = sp.value_load(route[:, bass.ds(pair * (2 * NT) + (g * NT + j), 1)],
                                               min_val=0, max_val=NX - 1)
                        for l in range(LAYERS):
                            sp.dma_start(w_ring[:, l, g, j, :], table_dram[:, l, bass.ds(expert, 1), :])\
                              .then_inc(sem["w_routed"], 16)
                sp.wait_ge(sem["h_ready"], at(pair, "h_ready", 8))
                sp.dma_start(out[:, bass.ts(pair, T)], h[4][:, :]).then_inc(sem["stored"], 16)
            sp.wait_ge(sem["stored"], 16 * PAIRS)

        @block.gpsimd
        def _(pool):
            for tile in (wq_bd, wk_bd):
                pool.memset(tile[:, :], 0.0).then_inc(zeroed, 1)
            pool.memset(gate_bd[:, :], 0.0)
            pool.memset(aq_bd[:, :], 0.0)
            pool.memset(ak_bd[:, :], 0.0)
            pool.memset(av_bd[:, :], 0.0).then_inc(zeroed, 1)
            pool.memset(wvo_bd[:, :], 0.0).then_inc(zeroed, 1)
            pool.memset(projT[:, :, :], 0.0).then_inc(zeroed, 1)
            pool.memset(vb[:, :, :, :, :, :], 0.0)
            pool.memset(xpad[:, :, :], 0.0).then_inc(table_ready, 1)
            pool.wait_ge(loaded, 16 * LOADS)
            for l in range(LAYERS):
                both = wsT[:, l, :]
                pool.tensor_tensor(both, both, ident, ALU.add).then_inc(shared_ready, 1)
            pool.wait_ge(shared_ready, LAYERS)
            for l in range(LAYERS):
                t = table[:, l, :, 0:HID]
                pool.tensor_tensor(t, t, wsT[:, l, :].unsqueeze(1).to_broadcast([P, NX, HID]), ALU.add)
                t = table[:, l, :, HID]
                pool.tensor_scalar(t, t, v("bs", l), None, ALU.add).then_inc(table_ready, 1)
            with pool.Fori(0, PAIRS) as pair:
                for g in range(2):
                    for n in range(NS):
                        k = g * NS + n
                        pool.wait_ge(sem["scanned"], at(pair, "scanned", k + 1))
                        pool.wait_ge(sem["c_sb"], at(pair, "c_sb", k + 1))
                        if k >= 2:
                            pool.wait_ge(sem["y_summed"], at(pair, "y_summed", k - 1))
                        pool.tensor_tensor(scratch[:, 8 + k % 2], scratch[:, 6 + k % 2], scratch[:, 2 + k % 2],
                                           ALU.mult).then_inc(sem["hc_ready"], 1)
                for k in range(4, 4 * NX):
                    g, c = divmod(k % 4, NC)
                    pool.wait_ge(sem["gated"], at(pair, "gated", k + 1))
                    if k >= 8:
                        pool.wait_ge(sem["summed"], at(pair, "summed", k - 7))
                    a = acc[:, 4 * c:4 * c + 4, g, :]
                    pool.tensor_tensor(a, a, gated_out(k), ALU.add).then_inc(sem["summed"], 1)
                for w in range(NW):
                    pool.wait_ge(sem["row_max"], at(pair, "row_max", w + 1))
                    if w >= 2:
                        pool.wait_ge(sem["att_exp"], at(pair, "att_exp", w - 1))
                    pool.tensor_tensor(
                        att_shift(w).rearrange("p (a b) -> p a b", a=H),
                        att_bias(w).rearrange("p (a b) -> p a b", a=H),
                        rmax[:, w % 2, :].unsqueeze(2).to_broadcast([P, H, WS]),
                        ALU.subtract).then_inc(sem["shifted"], 1)

        @block.tensor
        def _(pe):
            pe.wait_ge(loaded, 16 * LOADS)
            pe.matmul(ps[0:D, 0, 0:D], wvT[:, :], wo_tok[:, :], start=True, stop=True)
            pe.matmul(ps[D:P, 0, 0:D], wvT[:, :], wo_tok[:, :], start=True, stop=True)
            pe.matmul(ps[:, 1, 0:D], v("bv")[0:D].to_broadcast([D, P]), wo_tok[:, :], start=True, stop=True)
            pe.matmul(ps[:, 2, 0:E], sel_dt[:, :], dt_wT[:, :], start=True, stop=True).then_inc(fold_ps, 1)
            pe.wait_ge(fold_sb, 1)

            with pe.Fori(0, PAIRS) as pair:
                mm = pe.matmul

                def norm(k):
                    for c in range(NC):
                        cols = slice(c * CH, (c + 1) * CH)
                        pe.wait_ge(sem["r_ready"], at(pair, "r_ready", 2 * k + 2))
                        mm(ps[:, 4 + c, :], centre, res[:, cols], start=True, stop=True).then_inc(sem["centred"], 1)
                    for c in range(NC):
                        cols = slice(c * CH, (c + 1) * CH)
                        pe.wait_ge(sem["squared"], at(pair, "squared", 2 * k + c + 1))
                        mm(ps[:, 6 + c, :], average, sq[:, cols], start=True, stop=True).then_inc(sem["var_ps"], 1)

                pe.wait_ge(pair_done, pair + 1)
                pe.wait_ge(sem["x_loaded"], at(pair, "x_loaded", 16))
                for c in range(NC):
                    mm(ps[:, c, :], wq_bd[:, :], xT[:, c * CH:(c + 1) * CH], start=True, stop=True)\
                        .then_inc(sem["q_ps"], 1)
                for c in range(NC):
                    mm(ps[:, 2 + c, :], wk_bd[:, :], xT[:, c * CH:(c + 1) * CH], start=True, stop=True)\
                        .then_inc(sem["k_ps"], 1)
                for t in range(NT):
                    m = mm(ps[:, 6 + t // 4, (t % 4) * P:(t % 4 + 1) * P], xT[:, t * P:(t + 1) * P], wvo_bd[:, :],
                           start=True, stop=True)
                    if t % 4 == 3:
                        m.then_inc(sem["vw_ps"], 1)

                def scores(k):
                    g, s = divmod(k, NT)
                    half = slice(D * g, D * g + D)
                    pe.wait_ge(sem["qk_sb"], at(pair, "qk_sb", 2 * NC))
                    if k >= 2:
                        pe.wait_ge(sem["masked"], at(pair, "masked", k - 1))
                    for c in range(NC):
                        m = mm(ps[:, 2 * (k % 2) + c, :], qk[half, 1, s * P:(s + 1) * P],
                               qk[half, 0, c * CH:(c + 1) * CH], start=True, stop=True)
                    m.then_inc(sem["scores"], 1)

                scores(0)
                for k in range(2 * NT):
                    g, s = divmod(k, NT)
                    if k + 1 < 2 * NT:
                        scores(k + 1)
                    pe.wait_ge(sem["masked"], at(pair, "masked", k + 1))
                    pe.wait_ge(sem["vw_sb"], at(pair, "vw_sb", 2))
                    for t in range(NT):
                        m = mm(ps[:, 4 + g, t * D:(t + 1) * D], scratch[:, k % 4, t * P:(t + 1) * P],
                               vw[:, s, D * g:D * g + D], start=(s == 0 and t == 0), stop=(s == NT - 1),
                               skip_group_check=True)
                    m.then_inc(sem["retained"], 1)
                for t in range(NT):
                    pe.wait_ge(sem["y_ready"], at(pair, "y_ready", 2))
                    m = pe.transpose(ps[:, 6 + t // 4, (t % 4) * P:(t % 4 + 1) * P],
                                     y_tok[:, t, :, :].rearrange("p a b -> p (a b)"), ident)
                    if t % 4 == 3:
                        m.then_inc(sem["yT_ps"], 1)

                for g in range(2):
                    half = slice(D * g, D * g + D)
                    pe.wait_ge(sem["h0_ready"], at(pair, "h0_ready", 2))
                    if g:
                        pe.wait_ge(sem["xin_sb"], at(pair, "xin_sb", 1))
                    for c in range(NC):
                        m = mm(ps[:, c, :], in_proj[half, 0:E], h[0][half, c * CH:(c + 1) * CH], start=True, stop=True)
                    m.then_inc(sem["xin_ps"], 1)
                    if g:
                        pe.wait_ge(sem["z_ready"], at(pair, "z_ready", 1))
                    for c in range(NC):
                        m = mm(ps[:, 2 + c, :], in_proj[half, E:2 * E], h[0][half, c * CH:(c + 1) * CH],
                               start=True, stop=True)
                    m.then_inc(sem["z_ps"], 1)
                for g in range(2):
                    pe.wait_ge(sem["xc_ready"], at(pair, "xc_ready", g + 1))
                    if g:
                        pe.wait_ge(sem["sel_split"], at(pair, "sel_split", 1))
                    for c in range(NC):
                        m = mm(ps[:, 4 + c, :], selT[:, :], xc[:, g, c * CH:(c + 1) * CH], start=True, stop=True)
                    m.then_inc(sem["sel_ps"], 1)
                    if g:
                        pe.wait_ge(sem["dt_neg"], at(pair, "dt_neg", 1))
                    for c in range(NC):
                        m = mm(ps[:, 6 + c, :], w_dt[:, :], xc[:, g, c * CH:(c + 1) * CH], start=True, stop=True)
                    m.then_inc(sem["dt_ps"], 1)

                def spread(k):
                    g, n = divmod(k, NS)
                    pe.wait_ge(sem["sel_split"], at(pair, "sel_split", 2))
                    pe.wait_ge(sem["z_ready"], at(pair, "z_ready", 2))
                    if k:
                        pe.wait_ge(sem["dbu_ready"], at(pair, "dbu_ready", k))
                    for c in range(NC):
                        m = mm(ps[:, 2 + c, :], pick[:, n, :], bc[:, g, c * CH:(c + 1) * CH], start=True, stop=True)
                    m.then_inc(sem["b_ps"], 1)
                    if k:
                        pe.wait_ge(sem["c_sb"], at(pair, "c_sb", k))
                    for c in range(NC):
                        m = mm(ps[:, 4 + c, :], pick[:, NS + n, :], bc[:, g, c * CH:(c + 1) * CH],
                               start=True, stop=True)
                    m.then_inc(sem["c_ps"], 1)

                spread(0)
                for k in range(2 * NS):
                    g, n = divmod(k, NS)
                    if k + 1 < 2 * NS:
                        spread(k + 1)
                    pe.wait_ge(sem["hc_ready"], at(pair, "hc_ready", k + 1))
                    if n == 0:
                        pe.wait_ge(sem["dt_neg"], at(pair, "dt_neg", 2))
                        if g:
                            pe.wait_ge(sem["y_read"], at(pair, "y_read", 1))
                    for c in range(NC):
                        m = mm(ps[:, 6 + c, :], ident, scratch[:, 8 + k % 2, c * CH:(c + 1) * CH],
                               start=(n == 0), stop=(n == NS - 1))
                    m.then_inc(sem["y_summed"], 1)
                    if k in (NS + 2, 2 * NS - 1):
                        gg = k // (2 * NS - 1)
                        pe.wait_ge(sem["gated_y"], at(pair, "gated_y", gg + 1))
                        pe.wait_ge(sem["xin_sb"], at(pair, "xin_sb", 2))
                        for c in range(NC):
                            m = mm(ps[D * gg:D * gg + D, c, :], out_wT[:, :], u[:, gg, c * CH:(c + 1) * CH],
                                   start=True, stop=True)
                        m.then_inc(sem["mamba_ps"], 1)
                norm(0)

                pe.wait_ge(sem["h_ready"], at(pair, "h_ready", 2))
                for t in range(NT):
                    m = mm(ps[:, 6, t * 2 * NX:(t + 1) * 2 * NX], h[1][:, t * P:(t + 1) * P], gate_bd[:, :],
                           start=True, stop=True)
                m.then_inc(sem["logit_ps"], 1)

                def hidden(k):
                    e, gc = divmod(k, 4)
                    g, c = divmod(gc, NC)
                    half = slice(D * g, D * g + D)
                    if k >= 2:
                        pe.wait_ge(sem["hidden"], at(pair, "hidden", k - 1))
                    cols = slice(c * CH, (c + 1) * CH)
                    mm(ps[:, k % 2, :], w1[half, e, :], h[1][half, cols], start=True, stop=True)
                    mm(ps[:, 2 + k % 2, :], w2[half, e, :], h[1][half, cols], start=True, stop=True)\
                        .then_inc(sem["hh_ps"], 1)

                hidden(0)
                for k in range(4 * NX):
                    e = k // 4
                    if k + 1 < 4 * NX:
                        hidden(k + 1)
                    pe.wait_ge(sem["hidden"], at(pair, "hidden", k + 1))
                    if k >= 2:
                        pe.wait_ge(sem["gated"], at(pair, "gated", k - 1))
                    for t in range(4):
                        m = mm(ps[:, 4 + k % 2, t * D:(t + 1) * D],
                               scratch[:, 3 + k % 3, t * P:(t + 1) * P], w3[:, e, :], start=True, stop=True)
                    m.then_inc(sem["expert_ps"], 1)
                pe.wait_ge(sem["summed"], at(pair, "summed", 4 * (NX - 1)))
                for t in range(NT):
                    m = pe.transpose(ps[:, t // 4, (t % 4) * P:(t % 4 + 1) * P],
                                     acc[:, t, :, :].rearrange("p a b -> p (a b)"), ident)
                m.then_inc(sem["moeT_ps"], 1)
                norm(1)

                pe.wait_ge(sem["h_ready"], at(pair, "h_ready", 4))
                for c in range(NC):
                    mm(ps[:, c, :], aq_bd[:, :], h[2][:, c * CH:(c + 1) * CH], start=True, stop=True)\
                        .then_inc(sem["aq_ps"], 1)
                for c in range(NC):
                    mm(ps[:, 2 + c, :], ak_bd[:, :], h[2][:, c * CH:(c + 1) * CH], start=True, stop=True)\
                        .then_inc(sem["ak_ps"], 1)
                by_parity = av_bd[:, :].rearrange("p (c a d) -> p c a d", a=2, d=HD)
                for w in range(NW):
                    for a in range(2):
                        m = mm(ps[D * a:D * a + D, 4 + w // 8, (w % 8) * D:(w % 8 + 1) * D],
                               h[2][:, w * WS:(w + 1) * WS], by_parity[:, :, a, :], start=True, stop=True)
                    if w % 8 == 7:
                        m.then_inc(sem["av_ps"], 1)

                def att_scores(w):
                    pe.wait_ge(sem["q_blocks"], at(pair, "q_blocks", 2 * NC))
                    pe.wait_ge(sem["q_zero"], at(pair, "q_zero", 2))
                    pe.wait_ge(sem["k_blocks"], at(pair, "k_blocks", H))
                    if w >= 2:
                        pe.wait_ge(sem["biased"], at(pair, "biased", w - 1))
                    mm(ps[:, w % 2, :], qb[:, w, :], kb[:, w].rearrange("p a b -> p (a b)"), start=True, stop=True)\
                        .then_inc(sem["att_ps"], 1)

                def att_turn(w):
                    pe.wait_ge(sem["att_exp"], at(pair, "att_exp", w + 1))
                    if w >= 2:
                        pe.wait_ge(sem["probT_sb"], at(pair, "probT_sb", w - 1))
                    for hp in range(H // 2):
                        m = pe.transpose(ps[:, 2 + w % 2, hp * P:(hp + 1) * P],
                                         att_prob(w)[:, hp * P:(hp + 1) * P], ident)
                    m.then_inc(sem["probT_ps"], 1)

                def att_values(w):
                    m2_, ww = divmod(w, 2)
                    pe.wait_ge(sem["probT_sb"], at(pair, "probT_sb", w + 1))
                    pe.wait_ge(sem["v_blocks"], at(pair, "v_blocks", 4))
                    if m2_ >= 2 and ww == 0:
                        pe.wait_ge(sem["outT_sb"], at(pair, "outT_sb", m2_ - 1))
                    o = ps[:, 4 + m2_ % 2, ww * 144:(ww + 1) * 144].rearrange("p (g hp r) -> p g hp r", g=2, hp=H // 2)
                    for hp in range(H // 2):
                        m = mm(o[:, :, hp, :], att_probT(w)[:, hp * P:(hp + 1) * P],
                               vb[:, w, hp].rearrange("p g a b -> p g (a b)"), start=True, stop=True)
                    m.then_inc(sem["pv_ps"], 1)

                def att_out_turn(m_):
                    pe.wait_ge(sem["normed"], at(pair, "normed", 2 * m_ + 2))
                    pe.transpose(ps[:, 4 + m_ % 2, 3 * P:4 * P], att_out(m_), ident).then_inc(sem["outT_ps"], 1)

                def att_proj(m_):
                    pe.wait_ge(sem["outT_sb"], at(pair, "outT_sb", m_ + 1))
                    for ww in range(2):
                        col = (2 * m_ + ww) * WS
                        for g in range(2):
                            m = mm(ps[D * g:D * g + D, 6 + col // CH, col % CH:col % CH + WS], projT[:, ww, :],
                                   att_outT(m_)[:, g * WS:(g + 1) * WS], start=True, stop=True)
                    m.then_inc(sem["proj_ps"], 1)

                for s in range(NW + 6):
                    if s < NW:
                        att_scores(s)
                    if 0 <= s - 2 < NW:
                        att_turn(s - 2)
                    if 0 <= s - 3 < NW:
                        att_values(s - 3)
                    if s >= 5 and (s - 5) % 2 == 0 and (s - 5) // 2 < NW // 2:
                        att_out_turn((s - 5) // 2)
                    if s >= 6 and (s - 6) % 2 == 0 and (s - 6) // 2 < NW // 2:
                        att_proj((s - 6) // 2)
                norm(2)

                pe.wait_ge(sem["h_ready"], at(pair, "h_ready", 6))
                for g in range(2):
                    half = slice(D * g, D * g + D)
                    for c in range(NC):
                        m = mm(ps[:, 2 * g + c, :], fiT[half, :], h[3][half, c * CH:(c + 1) * CH],
                               start=True, stop=True)
                    m.then_inc(sem["f_in_ps"], 1)
                pe.wait_ge(sem["w_routed"], at(pair, "w_routed", PER["w_routed"]))
                for l in range(LAYERS):
                    for g in range(2):
                        if l == 0:
                            pe.wait_ge(sem["f0_ready"], at(pair, "f0_ready", g + 1))
                        else:
                            pe.wait_ge(sem[("l0_first", "l0_second")[g]], at(pair, ("l0_first", "l0_second")[g], 1))
                        base = (4 if l == 0 else 0) + 2 * g
                        for t in range(NT):
                            m = mm(ps[:, base + t // 4, (t % 4) * P:(t % 4 + 1) * P], w_ring[:, l, g, t, 0:HID],
                                   ffn_in(l, g)[:, t * P:(t + 1) * P], start=True, stop=True)
                        m.then_inc(sem["l0_ps" if l == 0 else "l1_ps"], 1)
                for g in range(2):
                    pe.wait_ge(sem["l1_first"], at(pair, "l1_first", 1))
                    pe.wait_ge(sem["l1_second"], at(pair, "l1_second", 1))
                    for c in range(NC):
                        m = mm(ps[D * g:D * g + D, c, :], foT[:, :], ffn_in(2, g)[:, c * CH:(c + 1) * CH],
                               start=True, stop=True)
                m.then_inc(sem["f_out_ps"], 1)
                norm(3)

        @block.scalar
        def _(act):
            act.wait_ge(loaded, 16 * LOADS)
            act.wait_ge(fold_ps, 1)
            count, per = [0], ACT_CHAIN
            act.activation(wvo_bd[0:D, 0:D], ps[0:D, 0, 0:D], ACT.Copy)
            act.activation(wvo_bd[D:P, D:P], ps[D:P, 0, 0:D], ACT.Copy)
            for g in range(2):
                act.activation(vo_row[:, g * D:(g + 1) * D], ps[:, 1, 0:D], ACT.Copy)
            act.activation(w_dt[:, :], ps[:, 2, 0:E], ACT.Copy).then_inc(fold_sb, 1)
            with act.Fori(0, PAIRS) as pair:
                count[0] = 0

                def then(ins):
                    link(act, act_chain, per, pair, count, ins)

                def norm(k):
                    for c in range(NC):
                        act.wait_ge(sem["centred"], at(pair, "centred", 2 * k + c + 1))
                        act.activation(sq[:, c * CH:(c + 1) * CH], ps[:, 4 + c, :], ACT.Square)\
                           .then_inc(sem["squared"], 1)
                    for c in range(NC):
                        cols = slice(c * CH, (c + 1) * CH)
                        act.wait_ge(sem["var_ps"], at(pair, "var_ps", 2 * k + c + 1))
                        then(act.activation(rs[:, cols], ps[:, 6 + c, :], ACT.Ln, bias=v("eps")))
                        act.activation(rs[:, cols], rs[:, cols], ACT.Exp, scale=-0.5).then_inc(sem["rstd"], 1)

                act.wait_ge(pair_done, pair + 1)
                for c in range(NC):
                    act.wait_ge(sem["q_ps"], at(pair, "q_ps", c + 1))
                    act.activation(qk[:, 0, c * CH:(c + 1) * CH], ps[:, c, :], ACT.Identity, bias=v("bq"))\
                       .then_inc(sem["qk_sb"], 1)
                for c in range(NC):
                    act.wait_ge(sem["k_ps"], at(pair, "k_ps", c + 1))
                    act.activation(qk[:, 1, c * CH:(c + 1) * CH], ps[:, 2 + c, :], ACT.Identity, bias=v("bk"))\
                       .then_inc(sem["qk_sb"], 1)
                for c in range(NC):
                    act.wait_ge(sem["yT_ps"], at(pair, "yT_ps", c + 1))
                    act.activation(h[0][:, c * CH:(c + 1) * CH], ps[:, 6 + c, :], ACT.Copy)\
                       .then_inc(sem["h0_ready"], 1)

                for g in range(2):
                    act.wait_ge(sem["xin_ps"], at(pair, "xin_ps", g + 1))
                    act.activation(xpad[:, g, 3:3 + T], banks(0), ACT.Copy).then_inc(sem["xin_sb"], 1)
                    act.wait_ge(sem["z_ps"], at(pair, "z_ps", g + 1))
                    act.activation(zs[:, g, :], banks(2), ACT.Silu).then_inc(sem["z_ready"], 1)
                for g in range(2):
                    act.wait_ge(sem["conv_ready"], at(pair, "conv_ready", g + 1))
                    act.activation(xc[:, g, :], scratch[:, g], ACT.Silu, bias=v("conv_b")).then_inc(sem["xc_ready"], 1)
                for g in range(2):
                    act.wait_ge(sem["sel_ps"], at(pair, "sel_ps", g + 1))
                    act.activation(bc[:, g, :], banks(4), ACT.Copy).then_inc(sem["sel_hi"], 1)
                for g in range(2):
                    act.wait_ge(sem["dt_neg"], at(pair, "dt_neg", g + 1))
                    then(act.activation(scratch[:, 2 + g], scratch[:, 2 + g], ACT.Exp))
                    act.activation(scratch[:, 2 + g], scratch[:, 2 + g], ACT.Ln, bias=v("one")).then_inc(sem["dt_ln"], 1)
                act.wait_ge(sem["u_ready"], at(pair, "u_ready", 2))
                for k in range(2 * NS):
                    g, n = divmod(k, NS)
                    if k >= 2:
                        act.wait_ge(sem["scanned"], at(pair, "scanned", k - 1))
                    act.activation(scratch[:, k % 2], dt[:, g, :], ACT.Exp, scale=v("A", n)).then_inc(sem["dA_ready"], 1)
                    act.wait_ge(sem["c_ps"], at(pair, "c_ps", k + 1))
                    if k >= 2:
                        act.wait_ge(sem["hc_ready"], at(pair, "hc_ready", k - 1))
                    act.activation(scratch[:, 2 + k % 2], banks(4), ACT.Copy).then_inc(sem["c_sb"], 1)
                norm(0)

                act.wait_ge(sem["top_diff"], at(pair, "top_diff", 1))
                act.activation(g2[:, :], g2[:, :], ACT.Exp).then_inc(sem["top_exp"], 1)
                for k in range(4 * NX):
                    act.wait_ge(sem["hh_ps"], at(pair, "hh_ps", k + 1))
                    if k >= 2:
                        act.wait_ge(sem["hidden"], at(pair, "hidden", k - 1))
                    act.activation(scratch[:, k % 2, 0:CH], ps[:, k % 2, :], ACT.Silu).then_inc(sem["silu_ready"], 1)
                norm(1)

                for c in range(NC):
                    act.wait_ge(sem["aq_ps"], at(pair, "aq_ps", c + 1))
                    for g in range(2):
                        half = slice(D * g, D * g + D)
                        act.activation(qb[half, NW // 2 * c:NW // 2 * (c + 1), D * g:D * g + WS],
                                       ps[half, c, :].rearrange("p (a b) -> p a b", b=WS), ACT.Copy,
                                       scale=float(HD) ** -0.5).then_inc(sem["q_blocks"], 1)
                act.wait_ge(sem["ak_ps"], at(pair, "ak_ps", 2))
                for hh in range(H):
                    act.activation(kb[:, :, hh, :], banks(2).rearrange("p (a b) -> p a b", b=WS), ACT.Copy,
                                   scale=head_mask[:, hh:hh + 1]).then_inc(sem["k_blocks"], 1)
                for s in range(NW + 4):
                    if s < NW:
                        act.wait_ge(sem["shifted"], at(pair, "shifted", s + 1))
                        if s >= 2:
                            act.wait_ge(sem["probT_ps"], at(pair, "probT_ps", s - 1))
                        act.activation(att_prob(s), att_shift(s), ACT.Exp).then_inc(sem["att_exp"], 1)
                    if 0 <= s - 1 < NW:
                        w = s - 1
                        act.wait_ge(sem["probT_ps"], at(pair, "probT_ps", w + 1))
                        if w >= 2:
                            act.wait_ge(sem["pv_ps"], at(pair, "pv_ps", w - 1))
                        act.activation(att_probT(w), ps[:, 2 + w % 2, :], ACT.Copy).then_inc(sem["probT_sb"], 1)
                    if s >= 3 and (s - 3) % 2 == 0 and (s - 3) // 2 < NW // 2:
                        m_ = (s - 3) // 2
                        act.wait_ge(sem["outT_ps"], at(pair, "outT_ps", m_ + 1))
                        if m_ >= 2:
                            act.wait_ge(sem["proj_ps"], at(pair, "proj_ps", m_ - 1))
                        act.activation(att_outT(m_), ps[:, 4 + m_ % 2, 3 * P:4 * P], ACT.Copy)\
                           .then_inc(sem["outT_sb"], 1)
                norm(2)

                for g in range(2):
                    act.wait_ge(sem["f_in_ps"], at(pair, "f_in_ps", g + 1))
                    act.activation(ffn_in(0, g), banks(2 * g), ACT.Relu, bias=v("bi")).then_inc(sem["f0_ready"], 1)
                for l in range(LAYERS):
                    act.wait_ge(sem["l0_ps" if l == 0 else "l1_ps"], at(pair, "l0_ps" if l == 0 else "l1_ps", 1))
                    for t in range(NT):
                        m = act.activation(ffn_in(l + 1, 0)[:, t * P:(t + 1) * P],
                                           ps[:, (4 if l == 0 else 0) + t // 4, (t % 4) * P:(t % 4 + 1) * P],
                                           ACT.Relu, bias=w_ring[:, l, 0, t, HID:HID + 1])
                    m.then_inc(sem["l0_first" if l == 0 else "l1_first"], 1)
                norm(3)
                assert count[0] == per, count[0]

        @block.vector
        def _(dve):
            dve.wait_ge(loaded, 16 * LOADS)
            dve.wait_ge(table_ready, 1 + LAYERS)
            for a in range(2):
                dve.memset(vb[D * a:D * a + D, :, :, :, a, HD:HD + 1], 1.0)
            dve.wait_ge(table_stored, 16)
            dve.memset(m1[:, :], 0.0).then_inc(pair_done, 1)
            with dve.Fori(0, PAIRS) as pair:
                count, per = [0], DVE_CHAIN

                def then(ins):
                    link(dve, dve_chain, per, pair, count, ins)

                def norm(k):
                    for c in range(NC):
                        cols = slice(c * CH, (c + 1) * CH)
                        dve.wait_ge(sem["rstd"], at(pair, "rstd", 2 * k + c + 1))
                        m = dve.tensor_tensor(h[k + 1][:, cols], ps[:, 4 + c, :], rs[:, cols], ALU.mult)
                        m.then_inc(sem["h_ready"], 1)

                dve.wait_ge(pair_done, pair + 1)
                for c in range(2):
                    dve.wait_ge(sem["vw_ps"], at(pair, "vw_ps", c + 1))
                    dve.tensor_tensor(vw[:, 4 * c:4 * c + 4, :], ps[:, 6 + c, :].rearrange("p (a b) -> p a b", a=4),
                                      vo_row[:, :].unsqueeze(1).to_broadcast([P, 4, P]), ALU.add)\
                       .then_inc(sem["vw_sb"], 1)
                for k in range(2 * NT):
                    dve.wait_ge(sem["scores"], at(pair, "scores", k + 1))
                    if k >= 4:
                        dve.wait_ge(sem["retained"], at(pair, "retained", k - 3))
                    dve.tensor_tensor(scratch[:, k % 4], banks(2 * (k % 2)), decayT[:, k % NT, :], ALU.mult)\
                       .then_inc(sem["masked"], 1)
                for g in range(2):
                    dve.wait_ge(sem["retained"], at(pair, "retained", (g + 1) * NT))
                    y = y_tok[:, :, g, :]
                    yn = y_neg[:, :, g, :]
                    then(dve.tensor_tensor(y, ps[:, 4 + g, :].rearrange("p (a b) -> p a b", a=NT),
                                           bo_row.unsqueeze(1).to_broadcast([P, NT, D]), ALU.add))
                    then(dve.tensor_scalar(yn, y, 0.0, v("prelu"), ALU.min, ALU.mult))
                    dve.scalar_tensor_tensor(out=y, in0=y, scalar=0.0, in1=yn, op0=ALU.max, op1=ALU.add)\
                       .then_inc(sem["y_ready"], 1)

                for g in range(2):
                    dve.wait_ge(sem["xin_sb"], at(pair, "xin_sb", g + 1))
                    cv = scratch[:, g]
                    then(dve.tensor_scalar(cv, xpad[:, g, 0:T], v("conv_w", 0), None, ALU.mult))
                    for k in range(1, 4):
                        m = dve.scalar_tensor_tensor(out=cv, in0=xpad[:, g, k:k + T], scalar=v("conv_w", k), in1=cv,
                                                     op0=ALU.mult, op1=ALU.add)
                        if k < 3:
                            then(m)
                    m.then_inc(sem["conv_ready"], 1)
                for g in range(2):
                    dve.wait_ge(sem["sel_hi"], at(pair, "sel_hi", g + 1))
                    left = scratch[:, 6 + g]
                    then(dve.tensor_tensor(left[D:P], banks(4)[D:P], bc[D:P, g, :], ALU.subtract))
                    then(dve.tensor_copy(bc[D:P, g, :], left[D:P]))
                    dve.tensor_tensor(bc[96:P, g, :], left[96:P], bc[96:P, g, :], ALU.subtract)\
                       .then_inc(sem["sel_split"], 1)
                    dve.wait_ge(sem["dt_ps"], at(pair, "dt_ps", g + 1))
                    arg = scratch[:, 4 + g]
                    then(dve.tensor_scalar(arg, banks(6), v("dt_b"), None, ALU.add))
                    dve.scalar_tensor_tensor(out=scratch[:, 2 + g], in0=arg, scalar=-1.0, in1=arg,
                                             op0=ALU.mult, op1=ALU.min).then_inc(sem["dt_neg"], 1)
                for g in range(2):
                    dve.wait_ge(sem["dt_ln"], at(pair, "dt_ln", g + 1))
                    dve.scalar_tensor_tensor(out=dt[:, g, :], in0=scratch[:, 4 + g], scalar=0.0, in1=scratch[:, 2 + g],
                                             op0=ALU.max, op1=ALU.add).then_inc(sem["dt_ready"], 1)
                    dve.wait_ge(sem["dt_ready"], at(pair, "dt_ready", g + 1))
                    dve.tensor_tensor(u[:, g, :], dt[:, g, :], xc[:, g, :], ALU.mult).then_inc(sem["u_ready"], 1)
                dve.wait_ge(sem["u_ready"], at(pair, "u_ready", 2))

                def drive(k):
                    dve.wait_ge(sem["b_ps"], at(pair, "b_ps", k + 1))
                    if k >= 2:
                        dve.wait_ge(sem["scanned"], at(pair, "scanned", k - 1))
                    dve.tensor_tensor(scratch[:, 4 + k % 2], u[:, k // NS, :], banks(2), ALU.mult)\
                       .then_inc(sem["dbu_ready"], 1)

                drive(0)
                for k in range(2 * NS):
                    g, n = divmod(k, NS)
                    if k + 1 < 2 * NS:
                        drive(k + 1)
                    dve.wait_ge(sem["dA_ready"], at(pair, "dA_ready", k + 1))
                    dve.wait_ge(sem["dbu_ready"], at(pair, "dbu_ready", k + 1))
                    if k >= 2:
                        dve.wait_ge(sem["hc_ready"], at(pair, "hc_ready", k - 1))
                    dve.tensor_tensor_scan(scratch[:, 6 + k % 2], scratch[:, k % 2], scratch[:, 4 + k % 2], 0.0,
                                           ALU.mult, ALU.add).then_inc(sem["scanned"], 1)
                    if k in (NS, 2 * NS - 1):
                        gg = k // (2 * NS - 1)
                        dve.wait_ge(sem["y_summed"], at(pair, "y_summed", (gg + 1) * NS))
                        dve.scalar_tensor_tensor(out=xpad[:, gg, 3:3 + T], in0=xc[:, gg, :], scalar=v("D"),
                                                 in1=banks(6), op0=ALU.mult, op1=ALU.add).then_inc(sem["y_read"], 1)
                        dve.wait_ge(sem["y_read"], at(pair, "y_read", gg + 1))
                        dve.tensor_tensor(u[:, gg, :], xpad[:, gg, 3:3 + T], zs[:, gg, :], ALU.mult)\
                           .then_inc(sem["gated_y"], 1)
                for g in range(2):
                    half = slice(D * g, D * g + D)
                    dve.wait_ge(sem["mamba_ps"], at(pair, "mamba_ps", g + 1))
                    dve.tensor_tensor(res[half, :], h[0][half, :], banks(0)[half], ALU.add).then_inc(sem["r_ready"], 1)
                norm(0)

                dve.wait_ge(sem["logit_ps"], at(pair, "logit_ps", 1))
                G = NT * 2
                def wide(t):
                    return t[:, :].unsqueeze(2).to_broadcast([P, G, NX])
                order_b = order.unsqueeze(1).to_broadcast([P, G, NX])
                then(dve.tensor_tensor(logits[:, :, :], ps[:, 6, 0:G * NX].rearrange("p (a b) -> p a b", a=G),
                                       gate_row.unsqueeze(1).to_broadcast([P, G, NX]), ALU.add))
                then(dve.tensor_reduce(m1[:, :], logits[:, :, :], AX.X, ALU.max))
                then(dve.tensor_tensor(hit[:, :, :], logits[:, :, :], wide(m1), ALU.is_equal))
                then(dve.tensor_tensor(hit[:, :, :], hit[:, :, :], order_b, ALU.mult))
                then(dve.tensor_reduce(mo[:, :], hit[:, :, :], AX.X, ALU.max))
                then(dve.tensor_tensor(pick1[:, :, :], order_b, wide(mo), ALU.is_equal))
                then(dve.scalar_tensor_tensor(out=logits2[:, :, :], in0=pick1[:, :, :], scalar=-3.0e38,
                                              in1=logits[:, :, :], op0=ALU.mult, op1=ALU.add))
                then(dve.tensor_reduce(m2[:, :], logits2[:, :, :], AX.X, ALU.max))
                then(dve.tensor_tensor(g2[:, :], m2[:, :], m1[:, :], ALU.subtract))
                dve.tensor_copy(g1[:, :], g2[:, :]).then_inc(sem["top_diff"], 1)
                then(dve.tensor_tensor(hit[:, :, :], logits2[:, :, :], wide(m2), ALU.is_equal))
                then(dve.tensor_tensor(hit[:, :, :], hit[:, :, :], order_b, ALU.mult))
                then(dve.tensor_reduce(mo[:, :], hit[:, :, :], AX.X, ALU.max))
                then(dve.tensor_tensor(pick2[:, :, :], order_b, wide(mo), ALU.is_equal))
                dve.wait_ge(sem["top_exp"], at(pair, "top_exp", 1))
                then(dve.tensor_scalar(g1[:, :], g2[:, :], 1.0, None, ALU.add))
                then(dve.reciprocal(g1[:, :], g1[:, :]))
                then(dve.tensor_tensor(g2[:, :], g2[:, :], g1[:, :], ALU.mult))
                then(dve.tensor_tensor(pick1[:, :, :], pick1[:, :, :], wide(g1), ALU.mult))
                then(dve.tensor_tensor(pick2[:, :, :], pick2[:, :, :], wide(g2), ALU.mult))
                then(dve.tensor_tensor(gates[:, :, :], pick1[:, :, :], pick2[:, :, :], ALU.add))
                gates_v = gates[:, :, :].rearrange("p (t g) e -> p t g e", g=2)

                def gate(k):
                    e, gc = divmod(k, 4)
                    g, c = divmod(gc, NC)
                    dve.wait_ge(sem["expert_ps"], at(pair, "expert_ps", k + 1))
                    if k >= 6:
                        dve.wait_ge(sem["summed"], at(pair, "summed", k - 5))
                    dve.tensor_tensor(gated_out(k) if e else acc[:, 4 * c:4 * c + 4, g, :],
                                      ps[:, 4 + k % 2, 0:4 * D].rearrange("p (a b) -> p a b", a=4),
                                      gates_v[:, 4 * c:4 * c + 4, g, e:e + 1].to_broadcast([P, 4, D]),
                                      ALU.mult).then_inc(sem["gated"], 1)

                for k in range(4 * NX):
                    dve.wait_ge(sem["silu_ready"], at(pair, "silu_ready", k + 1))
                    if k >= 3:
                        dve.wait_ge(sem["expert_ps"], at(pair, "expert_ps", k - 2))
                    dve.tensor_tensor(scratch[:, 3 + k % 3, 0:CH], scratch[:, k % 2, 0:CH], ps[:, 2 + k % 2, :],
                                      ALU.mult).then_inc(sem["hidden"], 1)
                    if k:
                        gate(k - 1)
                gate(4 * NX - 1)
                dve.wait_ge(sem["moeT_ps"], at(pair, "moeT_ps", 1))
                for c in range(NC):
                    cols = slice(c * CH, (c + 1) * CH)
                    dve.tensor_tensor(res[:, cols], h[1][:, cols], ps[:, c, :], ALU.add).then_inc(sem["r_ready"], 1)
                norm(1)

                dve.wait_ge(sem["h_ready"], at(pair, "h_ready", 4))
                for g in range(2):
                    dve.memset(qb[D * g:D * g + D, :, D * (1 - g):D * (1 - g) + D], 0.0).then_inc(sem["q_zero"], 1)
                dve.wait_ge(sem["av_ps"], at(pair, "av_ps", 2))
                av = banks(4).rearrange("p (w g hp d) -> p w g hp d", w=NW, g=2, hp=H // 2)
                for a in range(2):
                    half = slice(D * a, D * a + D)
                    for g in range(2):
                        dve.tensor_copy(vb[half, :, :, g, a, 0:HD], av[half, :, g, :, :]).then_inc(sem["v_blocks"], 1)

                def att_norm(m_):
                    dve.wait_ge(sem["pv_ps"], at(pair, "pv_ps", 2 * m_ + 2))
                    if m_ >= 2:
                        dve.wait_ge(sem["outT_ps"], at(pair, "outT_ps", m_ - 1))
                    o = ps[:, 4 + m_ % 2, 0:288].rearrange("p (w g h d) -> p w g h d", w=2, g=2, h=H)
                    for g in range(2):
                        half = slice(D * g, D * g + D)
                        m = dve.reciprocal(rsum[half, :, :], o[half, :, g, :, HD])
                        if g:
                            then(m)
                    for g in range(2):
                        half = slice(D * g, D * g + D)
                        dve.tensor_tensor(att_out(m_)[half].rearrange("p (w h d) -> p w h d", w=2, h=H),
                                          o[half, :, g, :, 0:HD],
                                          rsum[half, :, :].unsqueeze(3).to_broadcast([D, 2, H, HD]), ALU.mult)\
                           .then_inc(sem["normed"], 1)

                for s in range(NW + 4):
                    if s < NW:
                        dve.wait_ge(sem["att_ps"], at(pair, "att_ps", s + 1))
                        if s >= 2:
                            dve.wait_ge(sem["shifted"], at(pair, "shifted", s - 1))
                        t1 = att_bias(s).rearrange("p (a b) -> p a b", a=H)
                        dve.tensor_tensor(t1, ps[:, s % 2, :].rearrange("p (a b) -> p a b", a=H),
                                          rel_row.unsqueeze(1).to_broadcast([P, H, WS]), ALU.add)\
                           .then_inc(sem["biased"], 1)
                        dve.wait_ge(sem["biased"], at(pair, "biased", s + 1))
                        dve.tensor_reduce(rmax[:, s % 2, :], t1, AX.X, ALU.max).then_inc(sem["row_max"], 1)
                    if s >= 4 and (s - 4) % 2 == 0 and (s - 4) // 2 < NW // 2:
                        att_norm((s - 4) // 2)
                dve.wait_ge(sem["proj_ps"], at(pair, "proj_ps", NW // 2))
                for c in range(NC):
                    cols = slice(c * CH, (c + 1) * CH)
                    dve.scalar_tensor_tensor(out=res[:, cols], in0=ps[:, 6 + c, :], scalar=v("b_proj"),
                                             in1=h[2][:, cols], op0=ALU.add, op1=ALU.add).then_inc(sem["r_ready"], 1)
                norm(2)

                for l in range(LAYERS):
                    dve.wait_ge(sem["l0_ps" if l == 0 else "l1_ps"], at(pair, "l0_ps" if l == 0 else "l1_ps", 2))
                    for t in range(NT):
                        m = dve.tensor_scalar(ffn_in(l + 1, 1)[:, t * P:(t + 1) * P],
                                              ps[:, (6 if l == 0 else 2) + t // 4, (t % 4) * P:(t % 4 + 1) * P],
                                              w_ring[:, l, 1, t, HID:HID + 1], 0.0, ALU.add, ALU.max)
                    m.then_inc(sem["l0_second" if l == 0 else "l1_second"], 1)
                dve.wait_ge(sem["f_out_ps"], at(pair, "f_out_ps", 1))
                for c in range(NC):
                    cols = slice(c * CH, (c + 1) * CH)
                    dve.scalar_tensor_tensor(out=res[:, cols], in0=ps[:, c, :], scalar=v("bo"),
                                             in1=h[3][:, cols], op0=ALU.add, op1=ALU.add).then_inc(sem["r_ready"], 1)
                norm(3)
                dve.wait_ge(sem["stored"], at(pair, "stored", 16))
                dve.memset(m1[:, :], 0.0).then_inc(pair_done, 1)
                assert count[0] == per, count[0]


LOADS = 38
ACT_CHAIN = 10
DVE_CHAIN = 43


def kernel(**a):
    import ml_dtypes
    import numpy as _np
    import concourse.bacc as _bacc
    from concourse import mybir as _mybir
    from concourse.bass_utils import run_bass_kernel_spmd as _run

    a = {k: _np.asarray(x) for k, x in a.items()}
    f32 = _np.float32

    def col(x):
        x = x.reshape(-1)
        return _np.concatenate([x] * (P // x.size)).reshape(P, 1)

    vecs = dict(
        bq=col(a["L0_tok_bq"]), bk=col(a["L0_tok_bk"]), bv=col(a["L0_tok_bv"]),
        prelu=_np.broadcast_to(a["L0_tok_prelu_a"], (P, 1)), conv_w=a["L0_attn_conv_w"].reshape(E, 4),
        conv_b=col(a["L0_attn_conv_b"]), dt_b=col(a["L0_attn_dt_b"]), A=a["L0_attn_A"], D=col(a["L0_attn_D_param"]),
        b_proj=col(a["L1_attn_b_proj"]), bi=col(a["L1_ffn_bi"]), bs=a["L1_ffn_bs"].reshape(LAYERS, HID).T,
        bo=col(a["L1_ffn_bo"]), eps=_np.full((P, 1), EPS, f32), one=_np.ones((P, 1), f32),
    )
    names, columns = [], []
    for n, x in vecs.items():
        names += [n] + [f"{n}_{k}" for k in range(1, x.shape[1])]
        columns.append(x)
    windows = _np.lib.stride_tricks.sliding_window_view(a["L1_attn_rel_bias"], WS)[::-1]
    rows = _np.concatenate([
        _np.broadcast_to(a["L0_tok_bo"], (P, D)), _np.broadcast_to(a["L0_ffn_gate_b"], (P, NX)),
        _np.concatenate([windows, windows])], axis=1)
    part = _np.arange(P)
    same = (part[:, None] // D == part[None, :] // D).astype(f32)
    head = (part[:, None] % D // HD == _np.arange(H)[None, :]).astype(f32)
    consts = _np.concatenate([
        _np.eye(P, dtype=f32), _np.eye(P, dtype=f32) - same / D, same / D, head,
        _np.broadcast_to(NX - _np.arange(NX, dtype=f32), (P, NX))], axis=1)
    pick = _np.zeros((P, 2 * NS, P), ml_dtypes.bfloat16)
    for q in (0, 2, 3):
        pick[32 * q + _np.arange(2 * NS), _np.arange(2 * NS), :] = 1
    sel = a["L0_attn_sel_w"]
    qkv = a["L1_attn_w_qkv"]
    wr = a["L1_ffn_Wr"].transpose(3, 0, 1, 2)
    br = a["L1_ffn_br"].transpose(2, 0, 1)[..., None]
    arrays = dict(
        xT=a["x"].reshape(2, PAIRS, T, D).transpose(0, 3, 1, 2).reshape(P, PAIRS * T),
        decayT=a["L0_tok_d_gamma_batched"].T.reshape(NT, P, T).transpose(1, 0, 2),
        wq=a["L0_tok_Wq"], wk=a["L0_tok_Wk"], wvT=a["L0_tok_Wv"].T, wo_tok=a["L0_tok_Wo"],
        vec=_np.concatenate(columns, axis=1), rows=rows, consts=consts, pick=pick,
        in_projT=a["L0_attn_in_proj_w"].T, selT=_np.concatenate([sel[NS:]] * 4).T, sel_dt=sel[:NS],
        dt_wT=a["L0_attn_dt_w"].T, out_wT=a["L0_attn_out_w"].T, gate_w=a["L0_ffn_gate_w"],
        w1=a["L0_ffn_w1"].transpose(1, 0, 2), w2=a["L0_ffn_w2"].transpose(1, 0, 2), w3=a["L0_ffn_w3"].transpose(1, 0, 2),
        aqT=qkv[0:D].T, akT=qkv[D:2 * D].T, avT=qkv[2 * D:3 * D].T, projT=a["L1_attn_w_proj"].T,
        fiT=a["L1_ffn_Wi"].T, foT=a["L1_ffn_Wo"].T, wsT=a["L1_ffn_Ws"].reshape(LAYERS, HID, HID).transpose(2, 0, 1),
        table=_np.concatenate([wr, br], axis=3), route=a["L1_ffn_route_id"].reshape(2, PAIRS, NT)
        .transpose(1, 0, 2).reshape(1, B * NT),
    )
    nc = _bacc.Bacc("TRN2", target_bir_lowering=False, num_devices=1)
    maps, ins = {}, {}
    for name, x in arrays.items():
        x = _np.ascontiguousarray(x)
        maps[f"in_{name}"] = x
        ins[name] = nc.dram_tensor(f"in_{name}", x.shape, _mybir.dt.from_np(x.dtype), kind="ExternalInput").ap()
    ins["vec_names"] = names
    out = nc.dram_tensor("out_0", (P, PAIRS * T), F32, kind="ExternalOutput").ap()
    build_tower(nc, ins, out)
    r = _run(nc, [maps], core_ids=[0])
    y = r.results[0]["out_0"]
    return y.reshape(2, D, PAIRS, T).transpose(0, 2, 3, 1).reshape(B, T, D)
```

```python
from contextlib import ExitStack

import numpy as np

import concourse.bass as bass
from concourse import mybir

F32 = mybir.dt.float32
BF16 = mybir.dt.bfloat16
I32 = mybir.dt.int32
ALU = mybir.AluOpType
ACT = mybir.ActivationFunctionType
AX = mybir.AxisListType

P = 128
B, T, D = 8, 1024, 64
PAIRS = B // 2
NT = T // P
CH = 512
NC = T // CH
E = 128
NS = 16
NX = 16
HID = 128
WS, H, HD = 64, 8, 8
NW = T // WS
LAYERS = 2
EPS = 1e-5
WCOL = HID + 1

PER = dict(
    x_loaded=16, w_routed=16 * LAYERS * 2 * NT, stored=16,
    q_ps=NC, k_ps=NC, vw_ps=2, qk_sb=2 * NC, vw_sb=2, scores=2 * NT, masked=2 * NT, retained=2 * NT,
    y_ready=2, yT_ps=2, h0_ready=2,
    xin_ps=2, xin_sb=2, z_ps=2, z_ready=2, conv_ready=2, xc_ready=2, sel_ps=2, dt_ps=2, sel_hi=2, sel_split=2,
    dt_neg=2, dt_ln=2, dt_ready=2, u_ready=2,
    b_ps=2 * NS, c_ps=2 * NS, dA_ready=2 * NS, c_sb=2 * NS, dbu_ready=2 * NS, scanned=2 * NS, hc_ready=2 * NS,
    y_summed=2 * NS, y_read=2, gated_y=2, mamba_ps=2,
    logit_ps=1, x_split=1, top_diff=1, top_exp=1, hh_ps=4 * NX, silu_ready=4 * NX, hidden=4 * NX, expert_ps=4 * NX,
    gated=4 * NX, summed=4 * (NX - 1), moeT_ps=1,
    q_zero=2, aq_ps=NC, ak_ps=NC, av_ps=2, q_blocks=2 * NC, k_blocks=H, v_blocks=4, att_ps=NW, biased=NW, row_max=NW,
    shifted=NW, att_exp=NW, probT_ps=NW, probT_sb=NW, pv_ps=NW, normed=NW, outT_ps=NW // 2, outT_sb=NW // 2,
    proj_ps=NW // 2,
    f_in_ps=2, f0_ready=2, l0_ps=2, l1_ps=2, l0_first=1, l0_second=1, l1_first=1, l1_second=1, f_out_ps=1,
    r_ready=8, centred=8, squared=8, var_ps=8, ln_log=8, rstd=8, h_ready=8,
)


def build_tower(nc, i, out):
    with ExitStack() as ctx:
        def sb(name, shape, dt=F32):
            return ctx.enter_context(nc.sbuf_tensor(name, shape, dt))

        sem = {n: ctx.enter_context(nc.semaphore(n)) for n in PER}
        loaded = ctx.enter_context(nc.semaphore("loaded"))
        zeroed = ctx.enter_context(nc.semaphore("zeroed"))
        fold_ps = ctx.enter_context(nc.semaphore("fold_ps"))
        fold_sb = ctx.enter_context(nc.semaphore("fold_sb"))
        mix_loaded = ctx.enter_context(nc.semaphore("mix_loaded"))
        decay_loaded = ctx.enter_context(nc.semaphore("decay_loaded"))
        table_loaded = ctx.enter_context(nc.semaphore("table_loaded"))
        w12_loaded = ctx.enter_context(nc.semaphore("w12_loaded"))
        w12_split = ctx.enter_context(nc.semaphore("w12_split"))
        padded = ctx.enter_context(nc.semaphore("padded"))
        table_stored = ctx.enter_context(nc.semaphore("table_stored"))
        shared_ready = ctx.enter_context(nc.semaphore("shared_ready"))
        table_ready = ctx.enter_context(nc.semaphore("table_ready"))
        dve_chain = ctx.enter_context(nc.semaphore("dve_chain"))
        act_chain = ctx.enter_context(nc.semaphore("act_chain"))
        pair_done = ctx.enter_context(nc.semaphore("pair_done"))

        decayT = sb("decayT", [P, NT, T])
        wq_bd = sb("wq_bd", [P, P])
        wk_bd = sb("wk_bd", [P, P])
        wvo_bd = sb("wvo_bd", [P, P])
        wvT = sb("wvT", [D, D])
        wo_tok = sb("wo_tok", [D, D])
        vec = sb("vec", [P, i["vec"].shape[1]])
        rows = sb("rows", [P, i["rows"].shape[1]])
        in_proj = sb("in_proj", [P, 2 * E])
        selT = sb("selT", [P, P])
        sel_dt = sb("sel_dt", [NS, E])
        dt_wT = sb("dt_wT", [NS, E])
        w_dt = sb("w_dt", [P, E])
        out_wT = sb("out_wT", [P, D])
        gate_bd = sb("gate_bd", [P, 2 * NX])
        w_a = sb("w_a", [P, 2, NX, HID], BF16)
        w_b = sb("w_b", [P, 2, NX, HID], BF16)
        w_c = [sb(f"w_c{g}", [P, 2, NX, HID], BF16) for g in range(2)]
        w3 = sb("w3", [P, NX, D])
        aq_bd = sb("aq_bd", [P, P])
        ak_bd = sb("ak_bd", [P, P])
        av_bd = sb("av_bd", [P, P])
        projT = sb("projT", [P, 2, D])
        fiT = sb("fiT", [P, HID])
        foT = sb("foT", [P, D])
        table_dram = nc.dram_tensor("routed_table", (P, LAYERS, NX, WCOL), F32, kind="Internal").ap()
        consts = sb("consts", [P, i["consts"].shape[1]])
        pick = sb("pick", [P, 2 * NS], BF16)
        route = sb("route", [1, B * NT], I32)
        ident = consts[:, 0:P]
        centre = consts[:, P:2 * P]
        average = consts[:, 2 * P:3 * P]
        head_mask = consts[:, 3 * P:3 * P + H]
        order = consts[:, 3 * P + H:3 * P + H + NX]
        VEC = {n: k for k, n in enumerate(i["vec_names"])}

        def v(name, k=0):
            return vec[:, VEC[name] + k:VEC[name] + k + 1]

        vo_row = sb("vo_row", [P, P])
        bo_row = rows[:, 0:D]
        gate_row = rows[:, D:D + NX]
        rel_row = rows[:, D + NX:D + NX + WS]

        bc = sb("bc", [P, 2, T], BF16)
        xT = bc[:, :, :].bitcast(F32).rearrange("p a b -> p (a b)")
        even, odd = sb("h_even", [P, T]), sb("h_odd", [P, T])
        h = [even, odd, even, odd, even]
        work = sb("work", [P, 4 * T + 32])
        res, sq, rs = [work[:, k * T:(k + 1) * T] for k in range(3)]
        y_tok = work[:, 3 * T:4 * T].rearrange("p (t g d) -> p t g d", t=NT, g=2)
        xpad = sb("xpad", [P, 2, T + 3])
        xc = sb("xc", [P, 2, T])
        zs = sb("zs", [P, 2, T])
        steps = sb("steps", [P, LAYERS * 2 * NT * WCOL])
        dt = steps[:, 0:2 * T].rearrange("p (g t) -> p g t", g=2)
        u = steps[:, 2 * T:4 * T].rearrange("p (g t) -> p g t", g=2)
        scratch = sb("scratch", [P, 12, T])
        qk = dt
        vw = xc[:, 0, :].rearrange("p (a b) -> p a b", a=NT)
        y_neg = zs[:, 0, :].rearrange("p (t g d) -> p t g d", t=NT, g=2)
        w_ring = steps[:, :].rearrange("p (l g t c) -> p l g t c", l=LAYERS, g=2, t=NT)
        table = work[:, 0:LAYERS * NX * WCOL].rearrange("p (l e c) -> p l e c", l=LAYERS, e=NX)
        wsT = scratch[:, 6, 0:LAYERS * HID].rearrange("p (l c) -> p l c", l=LAYERS)
        w12 = [u, scratch[:, 8:10]]
        x_a = xc[:, 0, :].bitcast(BF16).rearrange("p (g t) -> p g t", g=2)
        x_b = xc[:, 1, :].bitcast(BF16).rearrange("p (g t) -> p g t", g=2)
        x_part = zs[:, 0, :].bitcast(BF16).rearrange("p (k t) -> p k t", k=2)
        x_left = zs[:, 1, :]
        logits, logits2, hit, pick1, pick2, gates = [
            scratch[:, 8 + k // 4, (k % 4) * 256:(k % 4 + 1) * 256].rearrange("p (g e) -> p g e", e=NX)
            for k in range(6)]
        m1 = sb("m1", [P, NT * 2])
        m2 = sb("m2", [P, NT * 2])
        mo = sb("mo", [P, NT * 2])
        g1 = sb("g1", [P, NT * 2])
        g2 = sb("g2", [P, NT * 2])
        acc = y_tok
        vb = sb("vb", [P, NW, H // 2, 2, 2, HD + 1])
        qb = scratch[:, 8:10].rearrange("p a (w q) -> p (a w) q", q=P)
        rmax = sb("rmax", [P, 2, H])
        rsum = sb("rsum", [P, 2, H])

        ps = ctx.enter_context(nc.psum_tensor("ps", [P, 8, CH], F32))

        def banks(k, n=2):
            return ps[:, k:k + n, :].rearrange("p a b -> p (a b)")

        block = ctx.enter_context(nc.Block())

        def att_bias(w):
            return sq[:, (w % 2) * CH:(w % 2 + 1) * CH]

        def att_shift(w):
            return rs[:, (w % 2) * CH:(w % 2 + 1) * CH]

        def att_prob(w):
            return xc[:, 0, (w % 2) * CH:(w % 2 + 1) * CH]

        def att_probT(w):
            return zs[:, 0, (w % 2) * CH:(w % 2 + 1) * CH]

        def att_out(m):
            return xc[:, 1, (m % 2) * P:(m % 2 + 1) * P]

        def att_outT(m):
            return zs[:, 1, (m % 2) * P:(m % 2 + 1) * P]

        kb = scratch[:, 0:8].rearrange("p a (w h k) -> p (a w) h k", w=2, h=H)

        def dA_slot(k):
            return scratch[:, k % 2]

        def dbu_slot(k):
            return scratch[:, 2 + k % 2]

        def c_slot(k):
            return scratch[:, 4 + k % 2]

        def hs_slot(k):
            return scratch[:, 6 + k % 3]

        def hc_slot(k):
            return scratch[:, 9 + k % 3]

        def gated_out(k):
            return scratch[:, 6 + k % 2, 0:4 * D].rearrange("p (a b) -> p a b", a=4)

        def ffn_in(l, g):
            return scratch[:, 2 * l + g]

        def at(pair, name, n):
            return pair * PER[name] + n

        def link(e, chain, per_pair, pair, count, ins):
            count[0] += 1
            ins.then_inc(chain, 1)
            e.wait_ge(chain, pair * per_pair + count[0])

        @block.sync
        def _(sp):
            sp.wait_ge(zeroed, 1)
            for dst, src in [(wq_bd[0:D, 0:D], i["wq"]), (wq_bd[D:P, D:P], i["wq"]),
                             (wk_bd[0:D, 0:D], i["wk"]), (wk_bd[D:P, D:P], i["wk"]),
                             (vec[:, :], i["vec"]), (rows[:, :], i["rows"]),
                             (wvT[:, :], i["wvT"]), (wo_tok[:, :], i["wo_tok"]),
                             (sel_dt[:, :], i["sel_dt"]), (dt_wT[:, :], i["dt_wT"])]:
                sp.dma_start(dst, src).then_inc(mix_loaded, 16)
            for s in range(NT):
                sp.dma_start(decayT[:, s, :], i["decayT"][:, s, :]).then_inc(decay_loaded, 16)
            for dst, src in [
                (in_proj[0:D, :], i["in_projT"]), (in_proj[D:P, :], i["in_projT"]), (selT[:, :], i["selT"]),
                (pick[:, :], i["pick"]), (out_wT[:, :], i["out_wT"]), (w3[:, :, :], i["w3"]),
                (foT[:, :], i["foT"]), (fiT[0:D, :], i["fiT"]), (fiT[D:P, :], i["fiT"]),
                (gate_bd[0:D, 0:NX], i["gate_w"]), (gate_bd[D:P, NX:2 * NX], i["gate_w"]),
                (aq_bd[0:D, 0:D], i["aqT"]), (aq_bd[D:P, D:P], i["aqT"]),
                (ak_bd[0:D, 0:D], i["akT"]), (ak_bd[D:P, D:P], i["akT"]),
                (av_bd[0:D, 0:D], i["avT"]), (av_bd[D:P, D:P], i["avT"]),
                (projT[0:D, 0, :], i["projT"]), (projT[D:P, 1, :], i["projT"]), (route[:, :], i["route"]),
            ]:
                sp.dma_start(dst, src).then_inc(loaded, 16)
            sp.wait_ge(table_ready, LAYERS)
            sp.dma_start(table_dram, table).then_inc(table_stored, 16)
            with sp.Fori(0, PAIRS) as pair:
                sp.wait_ge(pair_done, pair + 1)
                sp.wait_ge(mix_loaded, 16 * MIX_LOADS)
                sp.dma_start(xT[:, :], i["xT"][:, bass.ts(pair, T)]).then_inc(sem["x_loaded"], 16)
                sp.wait_ge(table_stored, 16)
                sp.wait_ge(sem["h_ready"], at(pair, "h_ready", 2))
                for g in range(2):
                    for j in range(NT):
                        expert = sp.value_load(route[:, bass.ds(pair * (2 * NT) + (g * NT + j), 1)],
                                               min_val=0, max_val=NX - 1)
                        for l in range(LAYERS):
                            sp.dma_start(w_ring[:, l, g, j, :], table_dram[:, l, bass.ds(expert, 1), :])\
                              .then_inc(sem["w_routed"], 16)
                sp.wait_ge(sem["h_ready"], at(pair, "h_ready", 8))
                sp.dma_start(out[:, bass.ts(pair, T)], h[4][:, :]).then_inc(sem["stored"], 16)
            sp.wait_ge(sem["stored"], 16 * PAIRS)

        @block.gpsimd
        def _(pool):
            pool.memset(wq_bd[:, :], 0.0)
            pool.memset(wk_bd[:, :], 0.0)
            pool.memset(gate_bd[:, :], 0.0)
            pool.memset(aq_bd[:, :], 0.0)
            pool.memset(ak_bd[:, :], 0.0)
            pool.memset(av_bd[:, :], 0.0)
            pool.memset(projT[:, :, :], 0.0)
            pool.memset(wvo_bd[:, :], 0.0).then_inc(zeroed, 1)
            pool.memset(vb[:, :, :, :, :, :], 0.0)
            pool.memset(xpad[:, :, :], 0.0).then_inc(padded, 1)
            pool.wait_ge(table_loaded, 16 * 3)
            for l in range(LAYERS):
                pool.tensor_tensor(wsT[:, l, :], wsT[:, l, :], ident, ALU.add).then_inc(shared_ready, 1)
            pool.wait_ge(mix_loaded, 16 * MIX_LOADS)
            pool.wait_ge(shared_ready, LAYERS)
            for l in range(LAYERS):
                t = table[:, l, :, 0:HID]
                pool.tensor_tensor(t, t, wsT[:, l, :].unsqueeze(1).to_broadcast([P, NX, HID]), ALU.add)
                t = table[:, l, :, HID]
                pool.tensor_scalar(t, t, v("bs", l), None, ALU.add).then_inc(table_ready, 1)
            pool.wait_ge(table_ready, LAYERS)
            pool.wait_ge(w12_loaded, 16 * 4)
            for m in range(2):
                w = w12[m].rearrange("p a b -> p (a b)").rearrange("p (e c) -> p e c", e=NX)
                left = scratch[:, 10:12].rearrange("p a b -> p (a b)").rearrange("p (e c) -> p e c", e=NX)
                pool.tensor_scalar(w_a[:, m], w, 1.0, 1.0, ALU.mult, ALU.mult).then_inc(w12_split, 1)
                pool.wait_ge(w12_split, 5 * m + 1)
                pool.tensor_tensor(left, w, w_a[:, m], ALU.subtract).then_inc(w12_split, 1)
                pool.wait_ge(w12_split, 5 * m + 2)
                pool.tensor_scalar(w_b[:, m], left, 1.0, 1.0, ALU.mult, ALU.mult).then_inc(w12_split, 1)
                pool.wait_ge(w12_split, 5 * m + 3)
                pool.tensor_tensor(w_c[0][0:D, m], left[0:D], w_b[0:D, m], ALU.subtract)
                pool.tensor_scalar(w_c[1][0:D, m], w_a[0:D, m], 1.0, 1.0, ALU.mult, ALU.mult).then_inc(w12_split, 1)
                pool.wait_ge(w12_split, 5 * m + 4)
                pool.tensor_tensor(w_c[1][D:P, m], left[D:P], w_b[D:P, m], ALU.subtract)
                pool.tensor_scalar(w_c[0][D:P, m], w_a[D:P, m], 1.0, 1.0, ALU.mult, ALU.mult).then_inc(w12_split, 1)
                pool.wait_ge(w12_split, 5 * m + 5)
            with pool.Fori(0, PAIRS) as pair:
                for g in range(2):
                    for n in range(NS):
                        k = g * NS + n
                        pool.wait_ge(sem["scanned"], at(pair, "scanned", k + 1))
                        pool.wait_ge(sem["c_sb"], at(pair, "c_sb", k + 1))
                        if k >= 3:
                            pool.wait_ge(sem["y_summed"], at(pair, "y_summed", k - 2))
                        pool.tensor_tensor(hc_slot(k), hs_slot(k), c_slot(k),
                                           ALU.mult).then_inc(sem["hc_ready"], 1)
                for k in range(4, 4 * NX):
                    g, c = divmod(k % 4, NC)
                    pool.wait_ge(sem["gated"], at(pair, "gated", k + 1))
                    if k >= 8:
                        pool.wait_ge(sem["summed"], at(pair, "summed", k - 7))
                    a = acc[:, 4 * c:4 * c + 4, g, :]
                    pool.tensor_tensor(a, a, gated_out(k), ALU.add).then_inc(sem["summed"], 1)
                for w in range(NW):
                    pool.wait_ge(sem["row_max"], at(pair, "row_max", w + 1))
                    if w >= 2:
                        pool.wait_ge(sem["att_exp"], at(pair, "att_exp", w - 1))
                    pool.tensor_tensor(
                        att_shift(w).rearrange("p (a b) -> p a b", a=H),
                        att_bias(w).rearrange("p (a b) -> p a b", a=H),
                        rmax[:, w % 2, :].unsqueeze(2).to_broadcast([P, H, WS]),
                        ALU.subtract).then_inc(sem["shifted"], 1)

        @block.tensor
        def _(pe):
            pe.wait_ge(mix_loaded, 16 * MIX_LOADS)
            pe.matmul(ps[0:D, 0, 0:D], wvT[:, :], wo_tok[:, :], start=True, stop=True)
            pe.matmul(ps[D:P, 0, 0:D], wvT[:, :], wo_tok[:, :], start=True, stop=True)
            pe.matmul(ps[:, 1, 0:D], v("bv")[0:D].to_broadcast([D, P]), wo_tok[:, :], start=True, stop=True)
            pe.matmul(ps[:, 2, 0:E], sel_dt[:, :], dt_wT[:, :], start=True, stop=True).then_inc(fold_ps, 1)
            pe.wait_ge(fold_sb, 1)

            with pe.Fori(0, PAIRS) as pair:
                mm = pe.matmul

                def norm(k):
                    for c in range(NC):
                        cols = slice(c * CH, (c + 1) * CH)
                        pe.wait_ge(sem["r_ready"], at(pair, "r_ready", 2 * k + 2))
                        mm(ps[:, 4 + c, :], centre, res[:, cols], start=True, stop=True).then_inc(sem["centred"], 1)
                    for c in range(NC):
                        cols = slice(c * CH, (c + 1) * CH)
                        pe.wait_ge(sem["squared"], at(pair, "squared", 2 * k + c + 1))
                        mm(ps[:, 6 + c, :], average, sq[:, cols], start=True, stop=True).then_inc(sem["var_ps"], 1)

                pe.wait_ge(pair_done, pair + 1)
                pe.wait_ge(sem["x_loaded"], at(pair, "x_loaded", 16))
                for c in range(NC):
                    mm(ps[:, c, :], wq_bd[:, :], xT[:, c * CH:(c + 1) * CH], start=True, stop=True)\
                        .then_inc(sem["q_ps"], 1)
                for c in range(NC):
                    mm(ps[:, 2 + c, :], wk_bd[:, :], xT[:, c * CH:(c + 1) * CH], start=True, stop=True)\
                        .then_inc(sem["k_ps"], 1)
                for t in range(NT):
                    m = mm(ps[:, 6 + t // 4, (t % 4) * P:(t % 4 + 1) * P], xT[:, t * P:(t + 1) * P], wvo_bd[:, :],
                           start=True, stop=True)
                    if t % 4 == 3:
                        m.then_inc(sem["vw_ps"], 1)

                def scores(k):
                    g, s = divmod(k, NT)
                    half = slice(D * g, D * g + D)
                    pe.wait_ge(sem["qk_sb"], at(pair, "qk_sb", 2 * NC))
                    if k >= 2:
                        pe.wait_ge(sem["masked"], at(pair, "masked", k - 1))
                    for c in range(NC):
                        m = mm(ps[:, 2 * (k % 2) + c, :], qk[half, 1, s * P:(s + 1) * P],
                               qk[half, 0, c * CH:(c + 1) * CH], start=True, stop=True)
                    m.then_inc(sem["scores"], 1)

                scores(0)
                for k in range(2 * NT):
                    g, s = divmod(k, NT)
                    if k + 1 < 2 * NT:
                        scores(k + 1)
                    pe.wait_ge(sem["masked"], at(pair, "masked", k + 1))
                    pe.wait_ge(sem["vw_sb"], at(pair, "vw_sb", 2))
                    for t in range(NT):
                        m = mm(ps[:, 4 + g, t * D:(t + 1) * D], scratch[:, k % 4, t * P:(t + 1) * P],
                               vw[:, s, D * g:D * g + D], start=(s == 0 and t == 0), stop=(s == NT - 1),
                               skip_group_check=True)
                    m.then_inc(sem["retained"], 1)
                pe.wait_ge(table_loaded, 16 * 3)
                for t in range(NT):
                    pe.wait_ge(sem["y_ready"], at(pair, "y_ready", 2))
                    m = pe.transpose(ps[:, 6 + t // 4, (t % 4) * P:(t % 4 + 1) * P],
                                     y_tok[:, t, :, :].rearrange("p a b -> p (a b)"), ident)
                    if t % 4 == 3:
                        m.then_inc(sem["yT_ps"], 1)

                pe.wait_ge(loaded, 16 * LOADS)
                for g in range(2):
                    half = slice(D * g, D * g + D)
                    pe.wait_ge(sem["h0_ready"], at(pair, "h0_ready", 2))
                    if g:
                        pe.wait_ge(sem["xin_sb"], at(pair, "xin_sb", 1))
                    for c in range(NC):
                        m = mm(ps[:, c, :], in_proj[half, 0:E], h[0][half, c * CH:(c + 1) * CH], start=True, stop=True)
                    m.then_inc(sem["xin_ps"], 1)
                    if g:
                        pe.wait_ge(sem["z_ready"], at(pair, "z_ready", 1))
                    for c in range(NC):
                        m = mm(ps[:, 2 + c, :], in_proj[half, E:2 * E], h[0][half, c * CH:(c + 1) * CH],
                               start=True, stop=True)
                    m.then_inc(sem["z_ps"], 1)
                for g in range(2):
                    pe.wait_ge(sem["xc_ready"], at(pair, "xc_ready", g + 1))
                    if g:
                        pe.wait_ge(sem["sel_split"], at(pair, "sel_split", 1))
                    for c in range(NC):
                        m = mm(ps[:, 4 + c, :], selT[:, :], xc[:, g, c * CH:(c + 1) * CH], start=True, stop=True)
                    m.then_inc(sem["sel_ps"], 1)
                    if g:
                        pe.wait_ge(sem["dt_neg"], at(pair, "dt_neg", 1))
                    for c in range(NC):
                        m = mm(ps[:, 6 + c, :], w_dt[:, :], xc[:, g, c * CH:(c + 1) * CH], start=True, stop=True)
                    m.then_inc(sem["dt_ps"], 1)

                def spread_b(k):
                    g, n = divmod(k, NS)
                    pe.wait_ge(sem["sel_split"], at(pair, "sel_split", 2))
                    pe.wait_ge(sem["z_ready"], at(pair, "z_ready", 2))
                    if k >= 2:
                        pe.wait_ge(sem["dbu_ready"], at(pair, "dbu_ready", k - 1))
                    for c in range(NC):
                        m = mm(ps[:, 2 * (k % 2) + c, :], pick[:, n:n + 1].to_broadcast([P, P]),
                               bc[:, g, c * CH:(c + 1) * CH], start=True, stop=True)
                    m.then_inc(sem["b_ps"], 1)

                def spread_c(k):
                    g, n = divmod(k, NS)
                    if k:
                        pe.wait_ge(sem["c_sb"], at(pair, "c_sb", k))
                    for c in range(NC):
                        m = mm(ps[:, 4 + c, :], pick[:, NS + n:NS + n + 1].to_broadcast([P, P]),
                               bc[:, g, c * CH:(c + 1) * CH], start=True, stop=True)
                    m.then_inc(sem["c_ps"], 1)

                def sum_states(k):
                    g, n = divmod(k, NS)
                    pe.wait_ge(sem["hc_ready"], at(pair, "hc_ready", k + 1))
                    if n == 0:
                        pe.wait_ge(sem["dt_neg"], at(pair, "dt_neg", 2))
                        if g:
                            pe.wait_ge(sem["y_read"], at(pair, "y_read", 1))
                    for c in range(NC):
                        m = mm(ps[:, 6 + c, :], ident, hc_slot(k)[:, c * CH:(c + 1) * CH],
                               start=(n == 0), stop=(n == NS - 1))
                    m.then_inc(sem["y_summed"], 1)

                LAG = 2
                spread_b(0)
                for k in range(2 * NS + LAG):
                    if k + 1 < 2 * NS:
                        spread_b(k + 1)
                    if k < 2 * NS:
                        spread_c(k)
                    if k >= LAG:
                        sum_states(k - LAG)
                for g in range(2):
                    pe.wait_ge(sem["gated_y"], at(pair, "gated_y", g + 1))
                    for c in range(NC):
                        m = mm(ps[D * g:D * g + D, c, :], out_wT[:, :], u[:, g, c * CH:(c + 1) * CH],
                               start=True, stop=True)
                    m.then_inc(sem["mamba_ps"], 1)
                norm(0)

                pe.wait_ge(sem["h_ready"], at(pair, "h_ready", 2))
                for t in range(NT):
                    m = mm(ps[:, 6, t * 2 * NX:(t + 1) * 2 * NX], h[1][:, t * P:(t + 1) * P], gate_bd[:, :],
                           start=True, stop=True)
                m.then_inc(sem["logit_ps"], 1)

                def hidden(k):
                    e, gc = divmod(k, 4)
                    g, c = divmod(gc, NC)
                    if k >= 2:
                        pe.wait_ge(sem["hidden"], at(pair, "hidden", k - 1))
                    cols = slice(c * CH, (c + 1) * CH)
                    for m in range(2):
                        for part, (w, x) in enumerate(((w_a, x_a), (w_b, x_a), (w_c[g], x_b))):
                            last = mm(ps[:, 2 * m + k % 2, :], w[:, m, e, :], x[:, g, cols],
                                      start=(part == 0), stop=(part == 2))
                    last.then_inc(sem["hh_ps"], 1)

                pe.wait_ge(w12_split, 10)
                pe.wait_ge(sem["x_split"], at(pair, "x_split", 1))
                hidden(0)
                for k in range(4 * NX):
                    e = k // 4
                    if k + 1 < 4 * NX:
                        hidden(k + 1)
                    pe.wait_ge(sem["hidden"], at(pair, "hidden", k + 1))
                    if k >= 2:
                        pe.wait_ge(sem["gated"], at(pair, "gated", k - 1))
                    for t in range(4):
                        m = mm(ps[:, 4 + k % 2, t * D:(t + 1) * D],
                               scratch[:, 3 + k % 3, t * P:(t + 1) * P], w3[:, e, :], start=True, stop=True)
                    m.then_inc(sem["expert_ps"], 1)
                pe.wait_ge(sem["summed"], at(pair, "summed", 4 * (NX - 1)))
                for t in range(NT):
                    m = pe.transpose(ps[:, t // 4, (t % 4) * P:(t % 4 + 1) * P],
                                     acc[:, t, :, :].rearrange("p a b -> p (a b)"), ident)
                m.then_inc(sem["moeT_ps"], 1)
                norm(1)

                pe.wait_ge(sem["h_ready"], at(pair, "h_ready", 4))
                for c in range(NC):
                    mm(ps[:, c, :], aq_bd[:, :], h[2][:, c * CH:(c + 1) * CH], start=True, stop=True)\
                        .then_inc(sem["aq_ps"], 1)
                for c in range(NC):
                    mm(ps[:, 2 + c, :], ak_bd[:, :], h[2][:, c * CH:(c + 1) * CH], start=True, stop=True)\
                        .then_inc(sem["ak_ps"], 1)
                by_parity = av_bd[:, :].rearrange("p (c a d) -> p c a d", a=2, d=HD)
                for w in range(NW):
                    for a in range(2):
                        m = mm(ps[D * a:D * a + D, 4 + w // 8, (w % 8) * D:(w % 8 + 1) * D],
                               h[2][:, w * WS:(w + 1) * WS], by_parity[:, :, a, :], start=True, stop=True)
                    if w % 8 == 7:
                        m.then_inc(sem["av_ps"], 1)

                def att_scores(w):
                    pe.wait_ge(sem["q_blocks"], at(pair, "q_blocks", 2 * NC))
                    pe.wait_ge(sem["q_zero"], at(pair, "q_zero", 2))
                    pe.wait_ge(sem["k_blocks"], at(pair, "k_blocks", H))
                    if w >= 2:
                        pe.wait_ge(sem["biased"], at(pair, "biased", w - 1))
                    mm(ps[:, w % 2, :], qb[:, w, :], kb[:, w].rearrange("p a b -> p (a b)"), start=True, stop=True)\
                        .then_inc(sem["att_ps"], 1)

                def att_turn(w):
                    pe.wait_ge(sem["att_exp"], at(pair, "att_exp", w + 1))
                    if w >= 2:
                        pe.wait_ge(sem["probT_sb"], at(pair, "probT_sb", w - 1))
                    for hp in range(H // 2):
                        m = pe.transpose(ps[:, 2 + w % 2, hp * P:(hp + 1) * P],
                                         att_prob(w)[:, hp * P:(hp + 1) * P], ident)
                    m.then_inc(sem["probT_ps"], 1)

                def att_values(w):
                    m2_, ww = divmod(w, 2)
                    pe.wait_ge(sem["probT_sb"], at(pair, "probT_sb", w + 1))
                    pe.wait_ge(sem["v_blocks"], at(pair, "v_blocks", 4))
                    if m2_ >= 2 and ww == 0:
                        pe.wait_ge(sem["outT_sb"], at(pair, "outT_sb", m2_ - 1))
                    o = ps[:, 4 + m2_ % 2, ww * 144:(ww + 1) * 144].rearrange("p (g hp r) -> p g hp r", g=2, hp=H // 2)
                    for hp in range(H // 2):
                        m = mm(o[:, :, hp, :], att_probT(w)[:, hp * P:(hp + 1) * P],
                               vb[:, w, hp].rearrange("p g a b -> p g (a b)"), start=True, stop=True)
                    m.then_inc(sem["pv_ps"], 1)

                def att_out_turn(m_):
                    pe.wait_ge(sem["normed"], at(pair, "normed", 2 * m_ + 2))
                    pe.transpose(ps[:, 4 + m_ % 2, 3 * P:4 * P], att_out(m_), ident).then_inc(sem["outT_ps"], 1)

                def att_proj(m_):
                    pe.wait_ge(sem["outT_sb"], at(pair, "outT_sb", m_ + 1))
                    for ww in range(2):
                        col = (2 * m_ + ww) * WS
                        for g in range(2):
                            m = mm(ps[D * g:D * g + D, 6 + col // CH, col % CH:col % CH + WS], projT[:, ww, :],
                                   att_outT(m_)[:, g * WS:(g + 1) * WS], start=True, stop=True)
                    m.then_inc(sem["proj_ps"], 1)

                for s in range(NW + 6):
                    if s < NW:
                        att_scores(s)
                    if 0 <= s - 2 < NW:
                        att_turn(s - 2)
                    if 0 <= s - 3 < NW:
                        att_values(s - 3)
                    if s >= 5 and (s - 5) % 2 == 0 and (s - 5) // 2 < NW // 2:
                        att_out_turn((s - 5) // 2)
                    if s >= 6 and (s - 6) % 2 == 0 and (s - 6) // 2 < NW // 2:
                        att_proj((s - 6) // 2)
                norm(2)

                pe.wait_ge(sem["h_ready"], at(pair, "h_ready", 6))
                for g in range(2):
                    half = slice(D * g, D * g + D)
                    for c in range(NC):
                        m = mm(ps[:, 2 * g + c, :], fiT[half, :], h[3][half, c * CH:(c + 1) * CH],
                               start=True, stop=True)
                    m.then_inc(sem["f_in_ps"], 1)
                pe.wait_ge(sem["w_routed"], at(pair, "w_routed", PER["w_routed"]))
                for l in range(LAYERS):
                    for g in range(2):
                        if l == 0:
                            pe.wait_ge(sem["f0_ready"], at(pair, "f0_ready", g + 1))
                        else:
                            pe.wait_ge(sem[("l0_first", "l0_second")[g]], at(pair, ("l0_first", "l0_second")[g], 1))
                        base = (4 if l == 0 else 0) + 2 * g
                        for t in range(NT):
                            m = mm(ps[:, base + t // 4, (t % 4) * P:(t % 4 + 1) * P], w_ring[:, l, g, t, 0:HID],
                                   ffn_in(l, g)[:, t * P:(t + 1) * P], start=True, stop=True)
                        m.then_inc(sem["l0_ps" if l == 0 else "l1_ps"], 1)
                for g in range(2):
                    pe.wait_ge(sem["l1_first"], at(pair, "l1_first", 1))
                    pe.wait_ge(sem["l1_second"], at(pair, "l1_second", 1))
                    for c in range(NC):
                        m = mm(ps[D * g:D * g + D, c, :], foT[:, :], ffn_in(2, g)[:, c * CH:(c + 1) * CH],
                               start=True, stop=True)
                m.then_inc(sem["f_out_ps"], 1)
                norm(3)

        @block.scalar
        def _(act):
            for dst, src in [(consts[:, :], i["consts"]), (wsT, i["wsT"]), (table, i["table"])]:
                act.dma_start(dst, src).then_inc(table_loaded, 16)
            for m, name in enumerate(("w1", "w2")):
                for a in range(2):
                    act.dma_start(w12[m][D * a:D * a + D], i[name]).then_inc(w12_loaded, 16)
            act.wait_ge(fold_ps, 1)
            count, per = [0], ACT_CHAIN
            act.activation(wvo_bd[0:D, 0:D], ps[0:D, 0, 0:D], ACT.Copy)
            act.activation(wvo_bd[D:P, D:P], ps[D:P, 0, 0:D], ACT.Copy)
            for g in range(2):
                act.activation(vo_row[:, g * D:(g + 1) * D], ps[:, 1, 0:D], ACT.Copy)
            act.activation(w_dt[:, :], ps[:, 2, 0:E], ACT.Copy).then_inc(fold_sb, 1)
            with act.Fori(0, PAIRS) as pair:
                count[0] = 0

                def then(ins):
                    link(act, act_chain, per, pair, count, ins)

                def norm(k):
                    for c in range(NC):
                        act.wait_ge(sem["centred"], at(pair, "centred", 2 * k + c + 1))
                        act.activation(sq[:, c * CH:(c + 1) * CH], ps[:, 4 + c, :], ACT.Square)\
                           .then_inc(sem["squared"], 1)
                    for c in range(NC):
                        cols = slice(c * CH, (c + 1) * CH)
                        act.wait_ge(sem["var_ps"], at(pair, "var_ps", 2 * k + c + 1))
                        then(act.activation(rs[:, cols], ps[:, 6 + c, :], ACT.Ln, bias=v("eps")))
                        act.activation(rs[:, cols], rs[:, cols], ACT.Exp, scale=-0.5).then_inc(sem["rstd"], 1)

                act.wait_ge(pair_done, pair + 1)
                for c in range(NC):
                    act.wait_ge(sem["q_ps"], at(pair, "q_ps", c + 1))
                    act.activation(qk[:, 0, c * CH:(c + 1) * CH], ps[:, c, :], ACT.Identity, bias=v("bq"))\
                       .then_inc(sem["qk_sb"], 1)
                for c in range(NC):
                    act.wait_ge(sem["k_ps"], at(pair, "k_ps", c + 1))
                    act.activation(qk[:, 1, c * CH:(c + 1) * CH], ps[:, 2 + c, :], ACT.Identity, bias=v("bk"))\
                       .then_inc(sem["qk_sb"], 1)
                for c in range(NC):
                    act.wait_ge(sem["yT_ps"], at(pair, "yT_ps", c + 1))
                    act.activation(h[0][:, c * CH:(c + 1) * CH], ps[:, 6 + c, :], ACT.Copy)\
                       .then_inc(sem["h0_ready"], 1)

                for g in range(2):
                    act.wait_ge(sem["xin_ps"], at(pair, "xin_ps", g + 1))
                    act.activation(xpad[:, g, 3:3 + T], banks(0), ACT.Copy).then_inc(sem["xin_sb"], 1)
                    act.wait_ge(sem["z_ps"], at(pair, "z_ps", g + 1))
                    act.activation(zs[:, g, :], banks(2), ACT.Silu).then_inc(sem["z_ready"], 1)
                for g in range(2):
                    act.wait_ge(sem["conv_ready"], at(pair, "conv_ready", g + 1))
                    act.activation(xc[:, g, :], scratch[:, g], ACT.Silu, bias=v("conv_b")).then_inc(sem["xc_ready"], 1)
                for g in range(2):
                    act.wait_ge(sem["sel_ps"], at(pair, "sel_ps", g + 1))
                    act.activation(bc[:, g, :], banks(4), ACT.Copy).then_inc(sem["sel_hi"], 1)
                act.preload_act_table_set("natural_log_exp_and_others")
                for g in range(2):
                    act.wait_ge(sem["dt_neg"], at(pair, "dt_neg", g + 1))
                    then(act.activation(scratch[:, 2 + g], scratch[:, 2 + g], ACT.Exp))
                    act.activation(scratch[:, 2 + g], scratch[:, 2 + g], ACT.Ln, bias=v("one")).then_inc(sem["dt_ln"], 1)
                act.wait_ge(sem["u_ready"], at(pair, "u_ready", 2))
                for k in range(2 * NS):
                    g, n = divmod(k, NS)
                    if k >= 2:
                        act.wait_ge(sem["scanned"], at(pair, "scanned", k - 1))
                    act.activation(dA_slot(k), dt[:, g, :], ACT.Exp, scale=v("A", n)).then_inc(sem["dA_ready"], 1)
                    act.wait_ge(sem["c_ps"], at(pair, "c_ps", k + 1))
                    if k >= 2:
                        act.wait_ge(sem["hc_ready"], at(pair, "hc_ready", k - 1))
                    act.activation(c_slot(k), banks(4), ACT.Copy).then_inc(sem["c_sb"], 1)
                norm(0)

                act.wait_ge(sem["top_diff"], at(pair, "top_diff", 1))
                act.activation(g2[:, :], g2[:, :], ACT.Exp).then_inc(sem["top_exp"], 1)
                for k in range(4 * NX):
                    act.wait_ge(sem["hh_ps"], at(pair, "hh_ps", k + 1))
                    if k >= 2:
                        act.wait_ge(sem["hidden"], at(pair, "hidden", k - 1))
                    act.activation(scratch[:, k % 2, 0:CH], ps[:, k % 2, :], ACT.Silu).then_inc(sem["silu_ready"], 1)
                act.preload_act_table_set("natural_log_exp_and_others")
                norm(1)

                for c in range(NC):
                    act.wait_ge(sem["aq_ps"], at(pair, "aq_ps", c + 1))
                    for g in range(2):
                        half = slice(D * g, D * g + D)
                        act.activation(qb[half, NW // 2 * c:NW // 2 * (c + 1), D * g:D * g + WS],
                                       ps[half, c, :].rearrange("p (a b) -> p a b", b=WS), ACT.Copy,
                                       scale=float(HD) ** -0.5).then_inc(sem["q_blocks"], 1)
                act.wait_ge(sem["ak_ps"], at(pair, "ak_ps", 2))
                for hh in range(H):
                    act.activation(kb[:, :, hh, :], banks(2).rearrange("p (a b) -> p a b", b=WS), ACT.Copy,
                                   scale=head_mask[:, hh:hh + 1]).then_inc(sem["k_blocks"], 1)
                for s in range(NW + 4):
                    if s < NW:
                        act.wait_ge(sem["shifted"], at(pair, "shifted", s + 1))
                        if s >= 2:
                            act.wait_ge(sem["probT_ps"], at(pair, "probT_ps", s - 1))
                        act.activation(att_prob(s), att_shift(s), ACT.Exp).then_inc(sem["att_exp"], 1)
                    if 0 <= s - 1 < NW:
                        w = s - 1
                        act.wait_ge(sem["probT_ps"], at(pair, "probT_ps", w + 1))
                        if w >= 2:
                            act.wait_ge(sem["pv_ps"], at(pair, "pv_ps", w - 1))
                        act.activation(att_probT(w), ps[:, 2 + w % 2, :], ACT.Copy).then_inc(sem["probT_sb"], 1)
                    if s >= 3 and (s - 3) % 2 == 0 and (s - 3) // 2 < NW // 2:
                        m_ = (s - 3) // 2
                        act.wait_ge(sem["outT_ps"], at(pair, "outT_ps", m_ + 1))
                        if m_ >= 2:
                            act.wait_ge(sem["proj_ps"], at(pair, "proj_ps", m_ - 1))
                        act.activation(att_outT(m_), ps[:, 4 + m_ % 2, 3 * P:4 * P], ACT.Copy)\
                           .then_inc(sem["outT_sb"], 1)
                norm(2)

                for g in range(2):
                    act.wait_ge(sem["f_in_ps"], at(pair, "f_in_ps", g + 1))
                    act.activation(ffn_in(0, g), banks(2 * g), ACT.Relu, bias=v("bi")).then_inc(sem["f0_ready"], 1)
                for l in range(LAYERS):
                    act.wait_ge(sem["l0_ps" if l == 0 else "l1_ps"], at(pair, "l0_ps" if l == 0 else "l1_ps", 1))
                    for t in range(NT):
                        m = act.activation(ffn_in(l + 1, 0)[:, t * P:(t + 1) * P],
                                           ps[:, (4 if l == 0 else 0) + t // 4, (t % 4) * P:(t % 4 + 1) * P],
                                           ACT.Relu, bias=w_ring[:, l, 0, t, HID:HID + 1])
                    m.then_inc(sem["l0_first" if l == 0 else "l1_first"], 1)
                norm(3)
                assert count[0] == per, count[0]

        @block.vector
        def _(dve):
            dve.wait_ge(padded, 1)
            for a in range(2):
                dve.memset(vb[D * a:D * a + D, :, :, :, a, HD:HD + 1], 1.0)
            dve.memset(m1[:, :], 0.0).then_inc(pair_done, 1)
            dve.wait_ge(mix_loaded, 16 * MIX_LOADS)
            with dve.Fori(0, PAIRS) as pair:
                count, per = [0], DVE_CHAIN

                def then(ins):
                    link(dve, dve_chain, per, pair, count, ins)

                def norm(k):
                    for c in range(NC):
                        cols = slice(c * CH, (c + 1) * CH)
                        dve.wait_ge(sem["rstd"], at(pair, "rstd", 2 * k + c + 1))
                        m = dve.tensor_tensor(h[k + 1][:, cols], ps[:, 4 + c, :], rs[:, cols], ALU.mult)
                        m.then_inc(sem["h_ready"], 1)

                dve.wait_ge(pair_done, pair + 1)
                for c in range(2):
                    dve.wait_ge(sem["vw_ps"], at(pair, "vw_ps", c + 1))
                    dve.tensor_tensor(vw[:, 4 * c:4 * c + 4, :], ps[:, 6 + c, :].rearrange("p (a b) -> p a b", a=4),
                                      vo_row[:, :].unsqueeze(1).to_broadcast([P, 4, P]), ALU.add)\
                       .then_inc(sem["vw_sb"], 1)
                for k in range(2 * NT):
                    dve.wait_ge(decay_loaded, 16 * (min(k, NT - 1) + 1))
                    dve.wait_ge(sem["scores"], at(pair, "scores", k + 1))
                    if k >= 4:
                        dve.wait_ge(sem["retained"], at(pair, "retained", k - 3))
                    dve.tensor_tensor(scratch[:, k % 4], banks(2 * (k % 2)), decayT[:, k % NT, :], ALU.mult)\
                       .then_inc(sem["masked"], 1)
                dve.wait_ge(table_stored, 16)
                for g in range(2):
                    dve.wait_ge(sem["retained"], at(pair, "retained", (g + 1) * NT))
                    y = y_tok[:, :, g, :]
                    yn = y_neg[:, :, g, :]
                    then(dve.tensor_tensor(y, ps[:, 4 + g, :].rearrange("p (a b) -> p a b", a=NT),
                                           bo_row.unsqueeze(1).to_broadcast([P, NT, D]), ALU.add))
                    then(dve.tensor_scalar(yn, y, 0.0, v("prelu"), ALU.min, ALU.mult))
                    dve.scalar_tensor_tensor(out=y, in0=y, scalar=0.0, in1=yn, op0=ALU.max, op1=ALU.add)\
                       .then_inc(sem["y_ready"], 1)

                for g in range(2):
                    dve.wait_ge(sem["xin_sb"], at(pair, "xin_sb", g + 1))
                    cv = scratch[:, g]
                    then(dve.tensor_scalar(cv, xpad[:, g, 0:T], v("conv_w", 0), None, ALU.mult))
                    for k in range(1, 4):
                        m = dve.scalar_tensor_tensor(out=cv, in0=xpad[:, g, k:k + T], scalar=v("conv_w", k), in1=cv,
                                                     op0=ALU.mult, op1=ALU.add)
                        if k < 3:
                            then(m)
                    m.then_inc(sem["conv_ready"], 1)
                for g in range(2):
                    dve.wait_ge(sem["sel_hi"], at(pair, "sel_hi", g + 1))
                    left = scratch[:, 6 + g]
                    then(dve.tensor_tensor(left[D:P], banks(4)[D:P], bc[D:P, g, :], ALU.subtract))
                    then(dve.tensor_copy(bc[D:P, g, :], left[D:P]))
                    dve.tensor_tensor(bc[96:P, g, :], left[96:P], bc[96:P, g, :], ALU.subtract)\
                       .then_inc(sem["sel_split"], 1)
                    dve.wait_ge(sem["dt_ps"], at(pair, "dt_ps", g + 1))
                    arg = scratch[:, 4 + g]
                    then(dve.tensor_scalar(arg, banks(6), v("dt_b"), None, ALU.add))
                    dve.scalar_tensor_tensor(out=scratch[:, 2 + g], in0=arg, scalar=-1.0, in1=arg,
                                             op0=ALU.mult, op1=ALU.min).then_inc(sem["dt_neg"], 1)
                for g in range(2):
                    dve.wait_ge(sem["dt_ln"], at(pair, "dt_ln", g + 1))
                    dve.scalar_tensor_tensor(out=dt[:, g, :], in0=scratch[:, 4 + g], scalar=0.0, in1=scratch[:, 2 + g],
                                             op0=ALU.max, op1=ALU.add).then_inc(sem["dt_ready"], 1)
                    dve.wait_ge(sem["dt_ready"], at(pair, "dt_ready", g + 1))
                    dve.wait_ge(w12_split, 10)
                    dve.tensor_tensor(u[:, g, :], dt[:, g, :], xc[:, g, :], ALU.mult).then_inc(sem["u_ready"], 1)
                dve.wait_ge(sem["u_ready"], at(pair, "u_ready", 2))

                def drive(k):
                    dve.wait_ge(sem["b_ps"], at(pair, "b_ps", k + 1))
                    if k >= 2:
                        dve.wait_ge(sem["scanned"], at(pair, "scanned", k - 1))
                    dve.tensor_tensor(dbu_slot(k), u[:, k // NS, :], banks(2 * (k % 2)), ALU.mult)\
                       .then_inc(sem["dbu_ready"], 1)

                drive(0)
                for k in range(2 * NS):
                    g, n = divmod(k, NS)
                    if k + 1 < 2 * NS:
                        drive(k + 1)
                    dve.wait_ge(sem["dA_ready"], at(pair, "dA_ready", k + 1))
                    dve.wait_ge(sem["dbu_ready"], at(pair, "dbu_ready", k + 1))
                    if k >= 3:
                        dve.wait_ge(sem["hc_ready"], at(pair, "hc_ready", k - 2))
                    dve.tensor_tensor_scan(hs_slot(k), dA_slot(k), dbu_slot(k), 0.0,
                                           ALU.mult, ALU.add).then_inc(sem["scanned"], 1)
                    if k in (NS + 1, 2 * NS - 1):
                        gg = k // (2 * NS - 1)
                        dve.wait_ge(sem["y_summed"], at(pair, "y_summed", (gg + 1) * NS))
                        dve.scalar_tensor_tensor(out=xpad[:, gg, 3:3 + T], in0=xc[:, gg, :], scalar=v("D"),
                                                 in1=banks(6), op0=ALU.mult, op1=ALU.add).then_inc(sem["y_read"], 1)
                        dve.wait_ge(sem["y_read"], at(pair, "y_read", gg + 1))
                        dve.tensor_tensor(u[:, gg, :], xpad[:, gg, 3:3 + T], zs[:, gg, :], ALU.mult)\
                           .then_inc(sem["gated_y"], 1)
                for g in range(2):
                    half = slice(D * g, D * g + D)
                    dve.wait_ge(sem["mamba_ps"], at(pair, "mamba_ps", g + 1))
                    dve.tensor_tensor(res[half, :], h[0][half, :], banks(0)[half], ALU.add).then_inc(sem["r_ready"], 1)
                norm(0)

                dve.wait_ge(sem["h_ready"], at(pair, "h_ready", 2))
                then(dve.tensor_copy(x_part[:, 0, :], h[1][:, :]))
                then(dve.tensor_tensor(x_left, h[1][:, :], x_part[:, 0, :], ALU.subtract))
                then(dve.tensor_copy(x_part[:, 1, :], x_left))
                for g in range(2):
                    own, other = slice(D * g, D * g + D), slice(D * (1 - g), D * (1 - g) + D)
                    dve.tensor_copy(x_a[own, g, :], x_part[own, 0, :])
                    dve.tensor_copy(x_b[own, g, :], x_part[own, 0, :])
                    dve.tensor_copy(x_a[other, g, :], x_part[own, 1, :])
                    m = dve.tensor_tensor(x_b[other, g, :], x_left[own], x_part[own, 1, :], ALU.subtract)
                m.then_inc(sem["x_split"], 1)
                dve.wait_ge(sem["logit_ps"], at(pair, "logit_ps", 1))
                G = NT * 2
                def wide(t):
                    return t[:, :].unsqueeze(2).to_broadcast([P, G, NX])
                order_b = order.unsqueeze(1).to_broadcast([P, G, NX])
                then(dve.tensor_tensor(logits[:, :, :], ps[:, 6, 0:G * NX].rearrange("p (a b) -> p a b", a=G),
                                       gate_row.unsqueeze(1).to_broadcast([P, G, NX]), ALU.add))
                then(dve.tensor_reduce(m1[:, :], logits[:, :, :], AX.X, ALU.max))
                then(dve.tensor_tensor(hit[:, :, :], logits[:, :, :], wide(m1), ALU.is_equal))
                then(dve.tensor_tensor(hit[:, :, :], hit[:, :, :], order_b, ALU.mult))
                then(dve.tensor_reduce(mo[:, :], hit[:, :, :], AX.X, ALU.max))
                then(dve.tensor_tensor(pick1[:, :, :], order_b, wide(mo), ALU.is_equal))
                then(dve.scalar_tensor_tensor(out=logits2[:, :, :], in0=pick1[:, :, :], scalar=-3.0e38,
                                              in1=logits[:, :, :], op0=ALU.mult, op1=ALU.add))
                then(dve.tensor_reduce(m2[:, :], logits2[:, :, :], AX.X, ALU.max))
                then(dve.tensor_tensor(g2[:, :], m2[:, :], m1[:, :], ALU.subtract))
                dve.tensor_copy(g1[:, :], g2[:, :]).then_inc(sem["top_diff"], 1)
                then(dve.tensor_tensor(hit[:, :, :], logits2[:, :, :], wide(m2), ALU.is_equal))
                then(dve.tensor_tensor(hit[:, :, :], hit[:, :, :], order_b, ALU.mult))
                then(dve.tensor_reduce(mo[:, :], hit[:, :, :], AX.X, ALU.max))
                then(dve.tensor_tensor(pick2[:, :, :], order_b, wide(mo), ALU.is_equal))
                dve.wait_ge(sem["top_exp"], at(pair, "top_exp", 1))
                then(dve.tensor_scalar(g1[:, :], g2[:, :], 1.0, None, ALU.add))
                then(dve.reciprocal(g1[:, :], g1[:, :]))
                then(dve.tensor_tensor(g2[:, :], g2[:, :], g1[:, :], ALU.mult))
                then(dve.tensor_tensor(pick1[:, :, :], pick1[:, :, :], wide(g1), ALU.mult))
                then(dve.tensor_tensor(pick2[:, :, :], pick2[:, :, :], wide(g2), ALU.mult))
                then(dve.tensor_tensor(gates[:, :, :], pick1[:, :, :], pick2[:, :, :], ALU.add))
                gates_v = gates[:, :, :].rearrange("p (t g) e -> p t g e", g=2)

                def gate(k):
                    e, gc = divmod(k, 4)
                    g, c = divmod(gc, NC)
                    dve.wait_ge(sem["expert_ps"], at(pair, "expert_ps", k + 1))
                    if k >= 6:
                        dve.wait_ge(sem["summed"], at(pair, "summed", k - 5))
                    dve.tensor_tensor(gated_out(k) if e else acc[:, 4 * c:4 * c + 4, g, :],
                                      ps[:, 4 + k % 2, 0:4 * D].rearrange("p (a b) -> p a b", a=4),
                                      gates_v[:, 4 * c:4 * c + 4, g, e:e + 1].to_broadcast([P, 4, D]),
                                      ALU.mult).then_inc(sem["gated"], 1)

                for k in range(4 * NX):
                    dve.wait_ge(sem["silu_ready"], at(pair, "silu_ready", k + 1))
                    if k >= 3:
                        dve.wait_ge(sem["expert_ps"], at(pair, "expert_ps", k - 2))
                    dve.tensor_tensor(scratch[:, 3 + k % 3, 0:CH], scratch[:, k % 2, 0:CH], ps[:, 2 + k % 2, :],
                                      ALU.mult).then_inc(sem["hidden"], 1)
                    if k:
                        gate(k - 1)
                gate(4 * NX - 1)
                dve.wait_ge(sem["moeT_ps"], at(pair, "moeT_ps", 1))
                for c in range(NC):
                    cols = slice(c * CH, (c + 1) * CH)
                    dve.tensor_tensor(res[:, cols], h[1][:, cols], ps[:, c, :], ALU.add).then_inc(sem["r_ready"], 1)
                norm(1)

                dve.wait_ge(sem["h_ready"], at(pair, "h_ready", 4))
                for g in range(2):
                    dve.memset(qb[D * g:D * g + D, :, D * (1 - g):D * (1 - g) + D], 0.0).then_inc(sem["q_zero"], 1)
                dve.wait_ge(sem["av_ps"], at(pair, "av_ps", 2))
                av = banks(4).rearrange("p (w g hp d) -> p w g hp d", w=NW, g=2, hp=H // 2)
                for a in range(2):
                    half = slice(D * a, D * a + D)
                    for g in range(2):
                        dve.tensor_copy(vb[half, :, :, g, a, 0:HD], av[half, :, g, :, :]).then_inc(sem["v_blocks"], 1)

                def att_norm(m_):
                    dve.wait_ge(sem["pv_ps"], at(pair, "pv_ps", 2 * m_ + 2))
                    if m_ >= 2:
                        dve.wait_ge(sem["outT_ps"], at(pair, "outT_ps", m_ - 1))
                    o = ps[:, 4 + m_ % 2, 0:288].rearrange("p (w g h d) -> p w g h d", w=2, g=2, h=H)
                    for g in range(2):
                        half = slice(D * g, D * g + D)
                        m = dve.reciprocal(rsum[half, :, :], o[half, :, g, :, HD])
                        if g:
                            then(m)
                    for g in range(2):
                        half = slice(D * g, D * g + D)
                        dve.tensor_tensor(att_out(m_)[half].rearrange("p (w h d) -> p w h d", w=2, h=H),
                                          o[half, :, g, :, 0:HD],
                                          rsum[half, :, :].unsqueeze(3).to_broadcast([D, 2, H, HD]), ALU.mult)\
                           .then_inc(sem["normed"], 1)

                for s in range(NW + 4):
                    if s < NW:
                        dve.wait_ge(sem["att_ps"], at(pair, "att_ps", s + 1))
                        if s >= 2:
                            dve.wait_ge(sem["shifted"], at(pair, "shifted", s - 1))
                        t1 = att_bias(s).rearrange("p (a b) -> p a b", a=H)
                        dve.tensor_tensor(t1, ps[:, s % 2, :].rearrange("p (a b) -> p a b", a=H),
                                          rel_row.unsqueeze(1).to_broadcast([P, H, WS]), ALU.add)\
                           .then_inc(sem["biased"], 1)
                        dve.wait_ge(sem["biased"], at(pair, "biased", s + 1))
                        dve.tensor_reduce(rmax[:, s % 2, :], t1, AX.X, ALU.max).then_inc(sem["row_max"], 1)
                    if s >= 4 and (s - 4) % 2 == 0 and (s - 4) // 2 < NW // 2:
                        att_norm((s - 4) // 2)
                dve.wait_ge(sem["proj_ps"], at(pair, "proj_ps", NW // 2))
                for c in range(NC):
                    cols = slice(c * CH, (c + 1) * CH)
                    dve.scalar_tensor_tensor(out=res[:, cols], in0=ps[:, 6 + c, :], scalar=v("b_proj"),
                                             in1=h[2][:, cols], op0=ALU.add, op1=ALU.add).then_inc(sem["r_ready"], 1)
                norm(2)

                for l in range(LAYERS):
                    dve.wait_ge(sem["l0_ps" if l == 0 else "l1_ps"], at(pair, "l0_ps" if l == 0 else "l1_ps", 2))
                    for t in range(NT):
                        m = dve.tensor_scalar(ffn_in(l + 1, 1)[:, t * P:(t + 1) * P],
                                              ps[:, (6 if l == 0 else 2) + t // 4, (t % 4) * P:(t % 4 + 1) * P],
                                              w_ring[:, l, 1, t, HID:HID + 1], 0.0, ALU.add, ALU.max)
                    m.then_inc(sem["l0_second" if l == 0 else "l1_second"], 1)
                dve.wait_ge(sem["f_out_ps"], at(pair, "f_out_ps", 1))
                for c in range(NC):
                    cols = slice(c * CH, (c + 1) * CH)
                    dve.scalar_tensor_tensor(out=res[:, cols], in0=ps[:, c, :], scalar=v("bo"),
                                             in1=h[3][:, cols], op0=ALU.add, op1=ALU.add).then_inc(sem["r_ready"], 1)
                norm(3)
                dve.wait_ge(sem["stored"], at(pair, "stored", 16))
                dve.memset(m1[:, :], 0.0).then_inc(pair_done, 1)
                assert count[0] == per, count[0]


MIX_LOADS = 10
LOADS = 20
ACT_CHAIN = 10
DVE_CHAIN = 46


def kernel(**a):
    import ml_dtypes
    import numpy as _np
    import concourse.bacc as _bacc
    from concourse import mybir as _mybir
    from concourse.bass_utils import run_bass_kernel_spmd as _run

    a = {k: _np.asarray(x) for k, x in a.items()}
    f32 = _np.float32

    def col(x):
        x = x.reshape(-1)
        return _np.concatenate([x] * (P // x.size)).reshape(P, 1)

    vecs = dict(
        bq=col(a["L0_tok_bq"]), bk=col(a["L0_tok_bk"]), bv=col(a["L0_tok_bv"]),
        prelu=_np.broadcast_to(a["L0_tok_prelu_a"], (P, 1)), conv_w=a["L0_attn_conv_w"].reshape(E, 4),
        conv_b=col(a["L0_attn_conv_b"]), dt_b=col(a["L0_attn_dt_b"]), A=a["L0_attn_A"], D=col(a["L0_attn_D_param"]),
        b_proj=col(a["L1_attn_b_proj"]), bi=col(a["L1_ffn_bi"]), bs=a["L1_ffn_bs"].reshape(LAYERS, HID).T,
        bo=col(a["L1_ffn_bo"]), eps=_np.full((P, 1), EPS, f32), one=_np.ones((P, 1), f32),
    )
    names, columns = [], []
    for n, x in vecs.items():
        names += [n] + [f"{n}_{k}" for k in range(1, x.shape[1])]
        columns.append(x)
    windows = _np.lib.stride_tricks.sliding_window_view(a["L1_attn_rel_bias"], WS)[::-1]
    rows = _np.concatenate([
        _np.broadcast_to(a["L0_tok_bo"], (P, D)), _np.broadcast_to(a["L0_ffn_gate_b"], (P, NX)),
        _np.concatenate([windows, windows])], axis=1)
    part = _np.arange(P)
    same = (part[:, None] // D == part[None, :] // D).astype(f32)
    head = (part[:, None] % D // HD == _np.arange(H)[None, :]).astype(f32)
    consts = _np.concatenate([
        _np.eye(P, dtype=f32), _np.eye(P, dtype=f32) - same / D, same / D, head,
        _np.broadcast_to(NX - _np.arange(NX, dtype=f32), (P, NX))], axis=1)
    pick = _np.zeros((P, 2 * NS), ml_dtypes.bfloat16)
    for q in (0, 2, 3):
        pick[32 * q + _np.arange(2 * NS), _np.arange(2 * NS)] = 1
    sel = a["L0_attn_sel_w"]
    qkv = a["L1_attn_w_qkv"]
    wr = a["L1_ffn_Wr"].transpose(3, 0, 1, 2)
    br = a["L1_ffn_br"].transpose(2, 0, 1)[..., None]
    arrays = dict(
        xT=a["x"].reshape(2, PAIRS, T, D).transpose(0, 3, 1, 2).reshape(P, PAIRS * T),
        decayT=a["L0_tok_d_gamma_batched"].T.reshape(NT, P, T).transpose(1, 0, 2),
        wq=a["L0_tok_Wq"], wk=a["L0_tok_Wk"], wvT=a["L0_tok_Wv"].T, wo_tok=a["L0_tok_Wo"],
        vec=_np.concatenate(columns, axis=1), rows=rows, consts=consts, pick=pick,
        in_projT=a["L0_attn_in_proj_w"].T, selT=_np.concatenate([sel[NS:]] * 4).T, sel_dt=sel[:NS],
        dt_wT=a["L0_attn_dt_w"].T, out_wT=a["L0_attn_out_w"].T, gate_w=a["L0_ffn_gate_w"],
        w1=a["L0_ffn_w1"].transpose(1, 0, 2).reshape(D, 2, T), w2=a["L0_ffn_w2"].transpose(1, 0, 2).reshape(D, 2, T),
        w3=a["L0_ffn_w3"].transpose(1, 0, 2),
        aqT=qkv[0:D].T, akT=qkv[D:2 * D].T, avT=qkv[2 * D:3 * D].T, projT=a["L1_attn_w_proj"].T,
        fiT=a["L1_ffn_Wi"].T, foT=a["L1_ffn_Wo"].T, wsT=a["L1_ffn_Ws"].reshape(LAYERS, HID, HID).transpose(2, 0, 1),
        table=_np.concatenate([wr, br], axis=3), route=a["L1_ffn_route_id"].reshape(2, PAIRS, NT)
        .transpose(1, 0, 2).reshape(1, B * NT),
    )
    nc = _bacc.Bacc("TRN2", target_bir_lowering=False, num_devices=1)
    maps, ins = {}, {}
    for name, x in arrays.items():
        x = _np.ascontiguousarray(x)
        maps[f"in_{name}"] = x
        ins[name] = nc.dram_tensor(f"in_{name}", x.shape, _mybir.dt.from_np(x.dtype), kind="ExternalInput").ap()
    ins["vec_names"] = names
    out = nc.dram_tensor("out_0", (P, PAIRS * T), F32, kind="ExternalOutput").ap()
    build_tower(nc, ins, out)
    r = _run(nc, [maps], core_ids=[0])
    y = r.results[0]["out_0"]
    return y.reshape(2, D, PAIRS, T).transpose(0, 2, 3, 1).reshape(B, T, D)
```

```python
from contextlib import ExitStack

import numpy as np

import concourse.bass as bass
from concourse import mybir

F32 = mybir.dt.float32
BF16 = mybir.dt.bfloat16
I32 = mybir.dt.int32
ALU = mybir.AluOpType
ACT = mybir.ActivationFunctionType
AX = mybir.AxisListType

P = 128
B, T, D = 8, 1024, 64
PAIRS = B // 2
NT = T // P
CH = 512
NC = T // CH
HT = NT // NC
NCH = 256
NN = T // NCH
E = 128
NS = 16
NX = 16
HID = 128
WS, H, HD = 64, 8, 8
NW = T // WS
LAYERS = 2
LEAD = 5
HIDDEN_RING = 2 * LEAD + 2
CATCH_UP = (2 * NX - 6, 2 * NX - 4, 2 * NX - 2)
STEPS = 2 * NX + LEAD - len(CATCH_UP)
OUT_DONE = [max(0, j - LEAD) + sum(x < j for x in CATCH_UP) for j in range(STEPS + 1)]
OUT_STEPS = [range(OUT_DONE[j], OUT_DONE[j + 1]) for j in range(STEPS)]
MIDDLE_LATE = 3
LOW_LATE = (5, 7)
DT_LATE = (4, 6, 8, 10)
U_LATE = (7, 9, 11, 13)
Y_LATE = (NS + 4, NS + 6)
Y_GATED = (NS + 8, NS + 10)
K_SPLIT = 3
EPS = 1e-5
SUM_STEPS = 6
WCOL = HID + 1

PER = dict(
    x_loaded=16, w_routed=16 * LAYERS * 2 * NT, stored=16,
    q_ps=NC, k_ps=NC, vw_ps=2, qk_sb=2 * NC, k_late=NC, k_zero=2, vw_sb=2, scores=2 * NT, masked=2 * NT, retained=2 * NT * NC,
    y_pos=2 * NC, y_neg=2 * NC, h0_ready=2 * NC, taps_ready=4,
    xin_ps=2, z_ps=2, z_ready=2, xc_ready=2, sel_ps=2, dt_ps=2, sel_hi=2, sel_read=2, sel_split=1 + NC,
    dt_read=2, dt_exp=2, dt_ln=2, dt_ready=1, dt_late=NN, u_ready=1, u_late=NN,
    b_ps=2 * NS, c_ps=2 * NS, dA_ready=2 * NS, c_sb=2 * NS, dbu_ready=2 * NS, scanned=2 * NS, hc_ready=2 * NS + 1,
    y_summed=2 * NS + 1, y_copied=1, y_read=2 * NC, gated_y=2 * NC,
    logit_ps=1, x_high=NN, x_rest=NN, x_low=1, x_split=1, x_copied=1, x_third=4, top_diff=1, top_silu=1,
    gates_ready=1, gatesT_ps=1, gates_hi=1, gates_split=1,
    hh_ps=4 * NX, silu_ready=4 * NX, hidden=4 * NX, expert_ps=4 * NX, gate_ps=4 * NX, gate_sb=4 * NX, gated=4 * NX,
    summed=4 * NX,
    q_zero=2, aq_ps=NC, ak_ps=NC, av_ps=2, k_copied=NC, q_blocks=2 * NC, k_blocks=NC * K_SPLIT, k_blocks_dve=NC * (H - K_SPLIT), v_blocks=4, att_ps=NW, biased=NW, row_max=NW,
    shifted=NW, att_exp=NW, probT_ps=NW, probT_sb=NW, pv_ps=NW, normed=NW, outT_ps=NW // 2, outT_sb=NW // 2,
    proj_ps=NW // 2,
    f_in_ps=2 * NC, f0_first=NC, f0_second=NC, l0_ps=2 * NC, l1_ps=2 * NC, l0_first=NC, l0_second=NC,
    l1_first=NC, l1_second=NC,
    r_ready=2 * NC, squared=4 * NN, var_ps=4 * NN, rstd=4 * NN, h_ready=4 * NN,
)


def build_tower(nc, i, out):
    with ExitStack() as ctx:
        def sb(name, shape, dt=F32):
            return ctx.enter_context(nc.sbuf_tensor(name, shape, dt))

        sem = {n: ctx.enter_context(nc.semaphore(n)) for n in PER}
        loaded = ctx.enter_context(nc.semaphore("loaded"))
        zeroed = ctx.enter_context(nc.semaphore("zeroed"))
        fold_ps = ctx.enter_context(nc.semaphore("fold_ps"))
        fold_sb = ctx.enter_context(nc.semaphore("fold_sb"))
        mix_loaded = ctx.enter_context(nc.semaphore("mix_loaded"))
        decay_loaded = [ctx.enter_context(nc.semaphore(f"decay_loaded{s}")) for s in range(NT)]
        table_loaded = ctx.enter_context(nc.semaphore("table_loaded"))
        w12_loaded = ctx.enter_context(nc.semaphore("w12_loaded"))
        w12_split = ctx.enter_context(nc.semaphore("w12_split"))
        padded = ctx.enter_context(nc.semaphore("padded"))
        conv_folded = ctx.enter_context(nc.semaphore("conv_folded"))
        out_centred = ctx.enter_context(nc.semaphore("out_centred"))
        shared_ready = ctx.enter_context(nc.semaphore("shared_ready"))
        table_ready = ctx.enter_context(nc.semaphore("table_ready"))
        dve_chain = ctx.enter_context(nc.semaphore("dve_chain"))
        act_chain = ctx.enter_context(nc.semaphore("act_chain"))
        pair_done = ctx.enter_context(nc.semaphore("pair_done"))

        decayT = sb("decayT", [P, NT, T])
        wq_bd = sb("wq_bd", [P, P])
        wk_bd = sb("wk_bd", [P, P])
        wvo_bd = sb("wvo_bd", [P, P])
        wvT = sb("wvT", [D, D])
        wo_tok = sb("wo_tok", [D, D])
        vec = sb("vec", [P, i["vec"].shape[1]])
        rows = sb("rows", [P, i["rows"].shape[1]])
        in_z = sb("in_z", [P, 2, E])
        in_x = sb("in_x", [P, 2, 2, E])
        selT = sb("selT", [P, P])
        sel_dt = sb("sel_dt", [NS, E])
        dt_wT = sb("dt_wT", [NS, E])
        w_dt = sb("w_dt", [P, E])
        gate_bd = sb("gate_bd", [P, 2 * NX])
        w_a = sb("w_a", [P, 2, NX, HID], BF16)
        w_b = sb("w_b", [P, 2, NX, HID], BF16)
        w_c = [sb(f"w_c{g}", [P, 2, NX, HID], BF16) for g in range(2)]
        to_model = sb("to_model", [P, NX + 4, D])
        w3 = to_model[:, 0:NX]
        foT, out_wT = to_model[:, NX], to_model[:, NX + 1]
        projT = to_model[:, NX + 2:NX + 4]
        out_bias = sb("out_bias", [P, 2])
        aq_bd = sb("aq_bd", [P, P])
        ak_bd = sb("ak_bd", [P, P])
        av_bd = sb("av_bd", [P, P])
        fiT = sb("fiT", [P, 2, HID])
        table_dram = nc.dram_tensor("routed_table", (P, LAYERS, NX, WCOL), F32, kind="Internal").ap()
        consts = sb("consts", [P, i["consts"].shape[1]])
        pick = sb("pick", [P, 2 * NS], BF16)
        route = sb("route", [1, B * NT], I32)
        ident = consts[:, 0:P]
        centre = consts[:, P:2 * P]
        average = consts[:, 2 * P:3 * P]
        head_mask = consts[:, 3 * P:3 * P + H]
        order = consts[:, 3 * P + H:3 * P + H + NX]
        VEC = {n: k for k, n in enumerate(i["vec_names"])}

        def v(name, k=0):
            return vec[:, VEC[name] + k:VEC[name] + k + 1]

        vo_row = sb("vo_row", [P, P])
        gate_row = rows[:, 0:NX]
        rel_row = rows[:, NX:NX + WS]

        bc = sb("bc", [P, 2, T], BF16)
        xT = bc[:, :, :].bitcast(F32).rearrange("p a b -> p (a b)")
        even, odd = sb("h_even", [P, T]), sb("h_odd", [P, T])
        h = [even, odd, even, odd, even]
        work = sb("work", [P, 4 * T + 32])
        y_sum = work[:, 0:T]
        k_sb = work[:, 0:T]
        sq, rs = [work[:, k * T:(k + 1) * T] for k in (1, 2)]
        acc = work[:, 3 * T:4 * T]
        taps = sb("taps", [P, 2, T + 3])
        xc = sb("xc", [P, 2, T])
        zs = sb("zs", [P, 2, T])
        steps = sb("steps", [P, LAYERS * 2 * NT * WCOL])
        dt = steps[:, 0:2 * T].rearrange("p (g t) -> p g t", g=2)
        u = steps[:, 2 * T:4 * T].rearrange("p (g t) -> p g t", g=2)
        scratch = sb("scratch", [P, 12, T])
        q_tok = steps[:, 0:T]
        k_tok = [steps[:, (1 + g) * T:(2 + g) * T] for g in range(2)]
        vw = xc[:, 0, :].rearrange("p (a b) -> p a b", a=NT)
        y_pos, y_neg = zs[:, 0, :], zs[:, 1, :]
        w_ring = steps[:, :].rearrange("p (l g t c) -> p l g t c", l=LAYERS, g=2, t=NT)
        table = work[:, 0:LAYERS * NX * WCOL].rearrange("p (l e c) -> p l e c", l=LAYERS, e=NX)
        wsT = scratch[:, 6, 0:LAYERS * HID].rearrange("p (l c) -> p l c", l=LAYERS)
        in_src = scratch[:, 10, 0:E]
        out_sum = scratch[:, 7, 0:(NX + 4) * D // 2].rearrange("p (a b) -> p a b", a=NX + 4)
        w12 = [scratch[:, 4:6], scratch[:, 8:10]]
        x_a = xc[:, 0, :].bitcast(BF16).rearrange("p (g t) -> p g t", g=2)
        x_b = xc[:, 1, :].bitcast(BF16).rearrange("p (g t) -> p g t", g=2)
        x_part = zs[:, 0, :].bitcast(BF16).rearrange("p (k t) -> p k t", k=2)
        x_left = zs[:, 1, :]
        logits, logits2, hit, pick1, pick2, gates = [
            scratch[:, 8 + k // 4, (k % 4) * 256:(k % 4 + 1) * 256].rearrange("p (g e) -> p g e", e=NX)
            for k in range(6)]
        m1 = sb("m1", [P, NT * 2])
        m2 = sb("m2", [P, NT * 2])
        mo = sb("mo", [P, NT * 2])
        g1 = sb("g1", [P, NT * 2])
        g2 = sb("g2", [P, NT * 2])
        gates4 = scratch[:, 10, :].rearrange("p (t r x) -> p t r x", t=NT, r=4)
        gatesT = scratch[:, 11, 0:CH].bitcast(BF16)
        gates_left = scratch[:, 1, :]
        vb = sb("vb", [P, NW, H // 2, 2, 2, HD + 1])
        qb = scratch[:, 8:10].rearrange("p a (w q) -> p (a w) q", q=P)
        rmax = sb("rmax", [P, 2, H])
        rsum = sb("rsum", [P, 2, H])

        ps = ctx.enter_context(nc.psum_tensor("ps", [P, 8, CH], F32))

        def banks(k, n=2):
            return ps[:, k:k + n, :].rearrange("p a b -> p (a b)")

        block = ctx.enter_context(nc.Block())

        def att_bias(w):
            return sq[:, (w % 2) * CH:(w % 2 + 1) * CH]

        def att_shift(w):
            return rs[:, (w % 2) * CH:(w % 2 + 1) * CH]

        def att_prob(w):
            return xc[:, 0, (w % 2) * CH:(w % 2 + 1) * CH]

        def att_probT(w):
            return zs[:, 0, (w % 2) * CH:(w % 2 + 1) * CH]

        def att_out(m):
            return xc[:, 1, (m % 2) * P:(m % 2 + 1) * P]

        def att_outT(m):
            return zs[:, 1, (m % 2) * P:(m % 2 + 1) * P]

        kb = scratch[:, 0:8].rearrange("p a (w h k) -> p (a w) h k", w=2, h=H)

        def dA_slot(k):
            return scratch[:, k % 2]

        def dbu_slot(k):
            return scratch[:, 2 + k % 2]

        def c_slot(k):
            return scratch[:, 4 + k % 2]

        def hs_slot(k):
            return scratch[:, 6 + k % 3]

        def hc_slot(k):
            return scratch[:, 9 + k % 3]

        def dt_pos(g):
            return rs if g else scratch[:, 4]

        def dt_neg(g):
            return sq if g else scratch[:, 2]

        def hidden_slot(k):
            k = k % HIDDEN_RING
            return scratch[:, 2 + k // 2, (k % 2) * CH:(k % 2 + 1) * CH]

        def gate_slot(j):
            return scratch[:, 1, (j % 2) * CH:(j % 2 + 1) * CH]

        def gated_out(j):
            return work[:, (j % 2) * CH:(j % 2 + 1) * CH]

        def ffn_in(l, g):
            return scratch[:, 2 * l + g]

        SEL_BANK, DT_BANK = (0, 6), (2, 4)
        RES_BANK = (0, None, 6, 4)
        VAR_BANKS = ((2, 3, 4, 5), (2, 3, 4, 5), (0, 1, 2, 3), (6, 7, 2, 3))

        def norm_chunk(bank, c):
            return banks(bank)[:, c * NCH:(c + 1) * NCH]

        def res_chunk(k, c):
            return acc[:, c * NCH:(c + 1) * NCH] if k == 1 else norm_chunk(RES_BANK[k], c)

        def res_bias(k):
            return (None, None, out_bias[:, 0:1], out_bias[:, 1:2])[k]

        R_COUNT = (0, None, None, NC)

        def at(pair, name, n):
            return pair * PER[name] + n

        def link(e, chain, per_pair, pair, count, ins):
            count[0] += 1
            ins.then_inc(chain, 1)
            e.wait_ge(chain, pair * per_pair + count[0])

        @block.sync
        def _(sp):
            sp.wait_ge(zeroed, 1)
            for dst, src in [(wq_bd[0:D, 0:D], i["wq"]), (wq_bd[D:P, D:P], i["wq"]),
                             (wk_bd[0:D, 0:D], i["wk"]), (wk_bd[D:P, D:P], i["wk"]),
                             (vec[:, :], i["vec"]), (rows[:, :], i["rows"]),
                             (wvT[:, :], i["wvT"]), (wo_tok[:, :], i["wo_tok"]),
                             (sel_dt[:, :], i["sel_dt"]), (dt_wT[:, :], i["dt_wT"]), (consts[:, :], i["consts"])]:
                sp.dma_start(dst, src).then_inc(mix_loaded, 16)
            sp.dma_start(xT[:, :], i["x_first"]).then_inc(sem["x_loaded"], 16)
            sp.wait_ge(zeroed, 2)
            for s in range(NT):
                sp.dma_start(decayT[:, s, :], i["decayT"][:, s, :]).then_inc(decay_loaded[s], 16)
            for dst, src in [
                (in_src[0:D, :], i["in_xT"]), (in_src[D:P, :], i["in_xT"]), (in_x[:, :, :, :], i["taps"]), (in_z[0:D, 0, :], i["in_zT"]), (in_z[D:P, 1, :], i["in_zT"]), (selT[:, :], i["selT"]),
                (pick[:, :], i["pick"]), (out_wT, i["out_wT"]), (w3, i["w3"]),
                (foT, i["foT"]), (fiT[0:D, 0, :], i["fiT"]), (fiT[D:P, 1, :], i["fiT"]),
                (gate_bd[0:D, 0:NX], i["gate_w"]), (gate_bd[D:P, NX:2 * NX], i["gate_w"]),
                (aq_bd[0:D, 0:D], i["aqT"]), (aq_bd[D:P, D:P], i["aqT"]),
                (ak_bd[0:D, 0:D], i["akT"]), (ak_bd[D:P, D:P], i["akT"]),
                (av_bd[0:D, 0:D], i["avT"]), (av_bd[D:P, D:P], i["avT"]),
                (projT[0:D, 0, :], i["projT"]), (projT[D:P, 1, :], i["projT"]), (route[:, :], i["route"]),
            ]:
                sp.dma_start(dst, src).then_inc(loaded, 16)
            sp.wait_ge(table_ready, LAYERS)
            sp.dma_start(table_dram, table).then_inc(sem["stored"], 16)
            def move(pair, more):
                sp.wait_ge(sem["h_ready"], at(pair, "h_ready", NN))
                sp.wait_ge(sem["stored"], 16)
                if more:
                    sp.dma_start(xT[:, :], i["x_next"][:, bass.ts(pair, T)]).then_inc(sem["x_loaded"], 16)
                for g in range(2):
                    for j in range(NT):
                        expert = sp.value_load(route[:, bass.ds(pair * (2 * NT) + (g * NT + j), 1)],
                                               min_val=0, max_val=NX - 1)
                        for l in range(LAYERS):
                            sp.dma_start(w_ring[:, l, g, j, :], table_dram[:, l, bass.ds(expert, 1), :])\
                              .then_inc(sem["w_routed"], 16)
                sp.wait_ge(sem["h_ready"], at(pair, "h_ready", 4 * NN))
                sp.dma_start(out[:, bass.ts(pair, T)], h[4][:, :]).then_inc(sem["stored"], 16)

            with sp.Fori(0, PAIRS - 1) as pair:
                move(pair, True)
            move(PAIRS - 1, False)
            sp.wait_ge(sem["stored"], 16 * (PAIRS + 1))

        @block.gpsimd
        def _(pool):
            pool.memset(wq_bd[:, :], 0.0)
            pool.memset(wk_bd[:, :], 0.0)
            pool.memset(wvo_bd[:, :], 0.0).then_inc(zeroed, 1)
            pool.memset(gate_bd[:, :], 0.0)
            pool.memset(aq_bd[:, :], 0.0)
            pool.memset(ak_bd[:, :], 0.0)
            pool.memset(av_bd[:, :], 0.0)
            pool.memset(projT, 0.0)
            pool.memset(in_z[:, :, :], 0.0)
            pool.memset(fiT[:, :, :], 0.0).then_inc(zeroed, 1)
            pool.memset(vb[:, :, :, :, :, :], 0.0)
            pool.memset(taps[:, :, :], 0.0).then_inc(padded, 1)
            pool.wait_ge(table_loaded, 16 * 2)
            pool.wait_ge(mix_loaded, 16 * MIX_LOADS)
            for l in range(LAYERS):
                pool.tensor_tensor(wsT[:, l, :], wsT[:, l, :], ident, ALU.add).then_inc(shared_ready, 1)
            pool.wait_ge(mix_loaded, 16 * MIX_LOADS)
            pool.wait_ge(shared_ready, LAYERS)
            for l in range(LAYERS):
                t = table[:, l, :, 0:HID]
                pool.tensor_tensor(t, t, wsT[:, l, :].unsqueeze(1).to_broadcast([P, NX, HID]), ALU.add)
                t = table[:, l, :, HID]
                pool.tensor_scalar(t, t, v("bs", l), None, ALU.add).then_inc(table_ready, 1)
            pool.wait_ge(loaded, 16 * LOADS)
            pool.tensor_tensor(in_x[:, :, :, :].rearrange("p a b e -> p (a b) e"),
                               in_x[:, :, :, :].rearrange("p a b e -> p (a b) e"),
                               in_src[:, :].unsqueeze(1).to_broadcast([P, 4, E]), ALU.mult).then_inc(conv_folded, 1)
            half = D // 2
            pool.tensor_tensor(out_sum, to_model[:, :, 0:half], to_model[:, :, half:D],
                               ALU.add).then_inc(out_centred, 1)
            for k in range(1, SUM_STEPS):
                half //= 2
                pool.wait_ge(out_centred, k)
                pool.tensor_tensor(out_sum[:, :, 0:half], out_sum[:, :, 0:half], out_sum[:, :, half:2 * half],
                                   ALU.add).then_inc(out_centred, 1)
            pool.wait_ge(out_centred, SUM_STEPS)
            pool.tensor_scalar(out_sum[:, :, 0], out_sum[:, :, 0], 1.0 / D, 1.0, ALU.mult, ALU.mult)\
                .then_inc(out_centred, 1)
            pool.wait_ge(out_centred, SUM_STEPS + 1)
            pool.tensor_tensor(to_model[:, :, :], to_model[:, :, :],
                               out_sum[:, :, 0:1].to_broadcast([P, NX + 4, D]),
                               ALU.subtract).then_inc(out_centred, 1)
            pool.wait_ge(table_ready, LAYERS)
            pool.wait_ge(w12_loaded, 16 * 4)
            for m in range(2):
                w = w12[m].rearrange("p a b -> p (a b)").rearrange("p (e c) -> p e c", e=NX)
                left = scratch[:, 10:12].rearrange("p a b -> p (a b)").rearrange("p (e c) -> p e c", e=NX)
                pool.tensor_scalar(w_a[:, m], w, 1.0, 1.0, ALU.mult, ALU.mult).then_inc(w12_split, 1)
                pool.wait_ge(w12_split, 5 * m + 1)
                pool.tensor_tensor(left, w, w_a[:, m], ALU.subtract).then_inc(w12_split, 1)
                pool.wait_ge(w12_split, 5 * m + 2)
                pool.tensor_scalar(w_b[:, m], left, 1.0, 1.0, ALU.mult, ALU.mult).then_inc(w12_split, 1)
                pool.wait_ge(w12_split, 5 * m + 3)
                pool.tensor_tensor(w_c[0][0:D, m], left[0:D], w_b[0:D, m], ALU.subtract)
                pool.tensor_scalar(w_c[1][0:D, m], w_a[0:D, m], 1.0, 1.0, ALU.mult, ALU.mult).then_inc(w12_split, 1)
                pool.wait_ge(w12_split, 5 * m + 4)
                pool.tensor_tensor(w_c[1][D:P, m], left[D:P], w_b[D:P, m], ALU.subtract)
                pool.tensor_scalar(w_c[0][D:P, m], w_a[D:P, m], 1.0, 1.0, ALU.mult, ALU.mult).then_inc(w12_split, 1)
                pool.wait_ge(w12_split, 5 * m + 5)
            with pool.Fori(0, PAIRS) as pair:
                for g in range(2):
                    for n in range(NS):
                        k = g * NS + n
                        if k in U_LATE:
                            c = U_LATE.index(k)
                            cols = slice(c * NCH, (c + 1) * NCH)
                            pool.wait_ge(sem["dt_late"], at(pair, "dt_late", c + 1))
                            pool.tensor_tensor(u[:, 1, cols], dt[:, 1, cols], xc[:, 1, cols],
                                               ALU.mult).then_inc(sem["u_late"], 1)
                        pool.wait_ge(sem["scanned"], at(pair, "scanned", k + 1))
                        pool.wait_ge(sem["c_sb"], at(pair, "c_sb", k + 1))
                        if k >= 3:
                            pool.wait_ge(sem["y_summed"], at(pair, "y_summed", k - 2))
                        if k < 2 * NS - 1:
                            pool.tensor_tensor(hc_slot(k), hs_slot(k), c_slot(k), ALU.mult).then_inc(sem["hc_ready"], 1)
                for c in range(NC):
                    cols = slice(c * CH, (c + 1) * CH)
                    pool.tensor_tensor(hc_slot(k)[:, cols], hs_slot(k)[:, cols], c_slot(k)[:, cols],
                                       ALU.mult).then_inc(sem["hc_ready"], 1)
                pool.wait_ge(sem["x_low"], at(pair, "x_low", 1))
                for c in range(NC):
                    cols = slice(c * CH, (c + 1) * CH)
                    for g in range(2):
                        own, other = slice(D * g, D * g + D), slice(D * (1 - g), D * (1 - g) + D)
                        n = 2 * c + g
                        if n:
                            pool.wait_ge(sem["x_third"], at(pair, "x_third", n))
                        pool.tensor_tensor(x_b[other, g, cols], x_left[own, cols], x_part[own, 1, cols],
                                           ALU.subtract).then_inc(sem["x_third"], 1)
                for j in range(2 * NX - 2):
                    cols = slice((j % 2) * CH, (j % 2 + 1) * CH)
                    pool.wait_ge(sem["gated"], at(pair, "gated", 2 * (j + 1)))
                    if j >= 2:
                        pool.wait_ge(sem["summed"], at(pair, "summed", 2 * (j - 1)))
                    pool.tensor_tensor(acc[:, cols], gated_out(j), acc[:, cols] if j >= 2 else h[1][:, cols],
                                       ALU.add).then_inc(sem["summed"], 2)
                for w in range(NW):
                    pool.wait_ge(sem["row_max"], at(pair, "row_max", w + 1))
                    if w >= 2:
                        pool.wait_ge(sem["att_exp"], at(pair, "att_exp", w - 1))
                    pool.tensor_tensor(
                        att_shift(w).rearrange("p (a b) -> p a b", a=H),
                        att_bias(w).rearrange("p (a b) -> p a b", a=H),
                        rmax[:, w % 2, :].unsqueeze(2).to_broadcast([P, H, WS]),
                        ALU.subtract).then_inc(sem["shifted"], 1)

        @block.tensor
        def _(pe):
            pe.wait_ge(mix_loaded, 16 * MIX_LOADS)
            pe.matmul(ps[0:D, 4, 0:D], wvT[:, :], wo_tok[:, :], start=True, stop=True)
            pe.matmul(ps[D:P, 4, 0:D], wvT[:, :], wo_tok[:, :], start=True, stop=True)
            pe.matmul(ps[:, 5, 0:D], v("bv")[0:D].to_broadcast([D, P]), wo_tok[:, :], start=True, stop=True)
            pe.matmul(ps[:, 6, 0:2], centre, vec[:, VEC["b_proj"]:VEC["b_proj"] + 2], start=True, stop=True)
            pe.matmul(ps[:, 7, 0:E], sel_dt[:, :], dt_wT[:, :], start=True, stop=True).then_inc(fold_ps, 1)

            with pe.Fori(0, PAIRS) as pair:
                mm = pe.matmul

                def norm(k):
                    for c in range(NN):
                        pe.wait_ge(sem["squared"], at(pair, "squared", NN * k + c + 1))
                        mm(ps[:, VAR_BANKS[k][c], 0:NCH], average, sq[:, c * NCH:(c + 1) * NCH], start=True, stop=True)\
                            .then_inc(sem["var_ps"], 1)

                pe.wait_ge(sem["x_loaded"], at(pair, "x_loaded", 16))
                for c in range(NC):
                    mm(ps[:, c, :], wq_bd[:, :], xT[:, c * CH:(c + 1) * CH], start=True, stop=True)\
                        .then_inc(sem["q_ps"], 1)
                pe.wait_ge(pair_done, pair + 1)
                for c in range(NC):
                    mm(ps[:, 2 + c, :], wk_bd[:, :], xT[:, c * CH:(c + 1) * CH], start=True, stop=True)\
                        .then_inc(sem["k_ps"], 1)
                pe.wait_ge(fold_sb, 1)
                for t in range(NT):
                    m = mm(ps[:, 6 + t // 4, (t % 4) * P:(t % 4 + 1) * P], xT[:, t * P:(t + 1) * P], wvo_bd[:, :],
                           start=True, stop=True)
                    if t % 4 == 3:
                        m.then_inc(sem["vw_ps"], 1)

                def scores(k):
                    g, s = divmod(k, NT)
                    pe.wait_ge(sem["qk_sb"], at(pair, "qk_sb", 2 * NC))
                    pe.wait_ge(sem["k_late"], at(pair, "k_late", NC))
                    pe.wait_ge(sem["k_zero"], at(pair, "k_zero", 2))
                    if k >= 2:
                        pe.wait_ge(sem["masked"], at(pair, "masked", k - 1))
                    for c in range(NC):
                        m = mm(ps[:, 2 * (k % 2) + c, :], k_tok[g][:, s * P:(s + 1) * P],
                               q_tok[:, c * CH:(c + 1) * CH], start=True, stop=True)
                    m.then_inc(sem["scores"], 1)

                scores(0)
                for k in range(2 * NT):
                    g, s = divmod(k, NT)
                    half = slice(D * g, D * g + D)
                    if k + 1 < 2 * NT:
                        scores(k + 1)
                    pe.wait_ge(sem["masked"], at(pair, "masked", k + 1))
                    pe.wait_ge(sem["vw_sb"], at(pair, "vw_sb", 2))
                    for c in range(NC):
                        m = mm(ps[half, 4 + c, :], vw[:, s, half], scratch[:, k % 4, c * CH:(c + 1) * CH],
                               start=(s == 0), stop=(s == NT - 1))
                        m.then_inc(sem["retained"], 1)

                pe.wait_ge(loaded, 16 * LOADS)
                pe.wait_ge(conv_folded, 1)
                for g in range(2):
                    pe.wait_ge(sem["taps_ready"], at(pair, "taps_ready", 2 * g + 2))
                    for c in range(NC):
                        for lag in range(2):
                            m = mm(ps[:, 2 * g + c, :], in_x[:, g, lag, :],
                                   taps[:, g, c * CH + 3 - 2 * lag:c * CH + 3 - 2 * lag + CH],
                                   start=(lag == 0), stop=(lag == 1))
                    m.then_inc(sem["xin_ps"], 1)
                    pe.wait_ge(sem["h0_ready"], at(pair, "h0_ready", 2 * NC))
                    for c in range(NC):
                        m = mm(ps[:, 4 + 2 * g + c, :], in_z[:, g, :], h[0][:, c * CH:(c + 1) * CH],
                               start=True, stop=True)
                    m.then_inc(sem["z_ps"], 1)
                for g in range(2):
                    pe.wait_ge(sem["xc_ready"], at(pair, "xc_ready", 2))
                    if g:
                        pe.wait_ge(sem["z_ready"], at(pair, "z_ready", 2))
                    for c in range(NC):
                        m = mm(ps[:, SEL_BANK[g] + c, :], selT[:, :], xc[:, g, c * CH:(c + 1) * CH], start=True, stop=True)
                    m.then_inc(sem["sel_ps"], 1)
                    for c in range(NC):
                        m = mm(ps[:, DT_BANK[g] + c, :], w_dt[:, :], xc[:, g, c * CH:(c + 1) * CH],
                               start=True, stop=True)
                    m.then_inc(sem["dt_ps"], 1)

                def spread_b(k):
                    g, n = divmod(k, NS)
                    pe.wait_ge(sem["sel_split"], at(pair, "sel_split", 1 + NC * g))
                    pe.wait_ge(sem["dt_read"], at(pair, "dt_read", 1))
                    if k >= 2:
                        pe.wait_ge(sem["dbu_ready"], at(pair, "dbu_ready", k - 1))
                    for c in range(NC):
                        m = mm(ps[:, 2 * (k % 2) + c, :], pick[:, n:n + 1].to_broadcast([P, P]),
                               bc[:, g, c * CH:(c + 1) * CH], start=True, stop=True)
                    m.then_inc(sem["b_ps"], 1)

                def spread_c(k):
                    g, n = divmod(k, NS)
                    if k == 0:
                        pe.wait_ge(sem["dt_read"], at(pair, "dt_read", 2))
                    if k:
                        pe.wait_ge(sem["c_sb"], at(pair, "c_sb", k))
                    for c in range(NC):
                        m = mm(ps[:, 4 + c, :], pick[:, NS + n:NS + n + 1].to_broadcast([P, P]),
                               bc[:, g, c * CH:(c + 1) * CH], start=True, stop=True)
                    m.then_inc(sem["c_ps"], 1)

                def sum_states(k):
                    g, n = divmod(k, NS)
                    pe.wait_ge(sem["hc_ready"], at(pair, "hc_ready", k + 1))
                    if n == 0:
                        pe.wait_ge(sem["sel_read"], at(pair, "sel_read", 2))
                        if g:
                            pe.wait_ge(sem["y_copied"], at(pair, "y_copied", 1))
                    for c in range(NC):
                        if k == 2 * NS - 1 and c:
                            m.then_inc(sem["y_summed"], 1)
                            pe.wait_ge(sem["hc_ready"], at(pair, "hc_ready", 2 * NS + 1))
                        m = mm(ps[:, 6 + c, :], ident, hc_slot(k)[:, c * CH:(c + 1) * CH],
                               start=(n == 0), stop=(n == NS - 1))
                    m.then_inc(sem["y_summed"], 1)

                LAG = 2
                spread_b(0)
                for k in range(2 * NS + LAG):
                    if k + 1 < 2 * NS:
                        spread_b(k + 1)
                    if k < 2 * NS:
                        spread_c(k)
                    if k == 2 * NS:
                        pe.wait_ge(sem["dbu_ready"], at(pair, "dbu_ready", 2 * NS))
                        for c in range(NC):
                            mm(ps[:, c, :], centre, h[0][:, c * CH:(c + 1) * CH], start=True, stop=True)
                    if k >= LAG:
                        sum_states(k - LAG)
                pe.wait_ge(out_centred, SUM_STEPS + 2)
                pe.wait_ge(sem["gated_y"], at(pair, "gated_y", NC))
                for c in range(NC):
                    mm(ps[0:D, c, :], out_wT, u[:, 0, c * CH:(c + 1) * CH], start=False, stop=True,
                       skip_group_check=True)
                for c in range(NC):
                    pe.wait_ge(sem["gated_y"], at(pair, "gated_y", NC + 1 + c))
                    mm(ps[D:P, c, :], out_wT, u[:, 1, c * CH:(c + 1) * CH], start=False, stop=True,
                       skip_group_check=True).then_inc(sem["r_ready"], 1)
                norm(0)

                for t in range(NT):
                    pe.wait_ge(sem["h_ready"], at(pair, "h_ready", t * P // NCH + 1))
                    m = mm(ps[:, 6, t * 2 * NX:(t + 1) * 2 * NX], h[1][:, t * P:(t + 1) * P], gate_bd[:, :],
                           start=True, stop=True)
                m.then_inc(sem["logit_ps"], 1)

                def hidden(k):
                    e, c, g = k // 4, k // 2 % 2, k % 2
                    if k == 0:
                        pe.wait_ge(sem["x_split"], at(pair, "x_split", 1))
                    if k == 2:
                        pe.wait_ge(sem["x_copied"], at(pair, "x_copied", 1))
                    if k < 4:
                        pe.wait_ge(sem["x_third"], at(pair, "x_third", k + 1))
                    if k >= 2:
                        pe.wait_ge(sem["hidden"], at(pair, "hidden", k - 1))
                    cols = slice(c * CH, (c + 1) * CH)
                    for m in range(2):
                        for part, (w, x) in enumerate(((w_a, x_a), (w_b, x_a), (w_c[g], x_b))):
                            last = mm(ps[:, 2 * m + k % 2, :], w[:, m, e, :], x[:, g, cols],
                                      start=(part == 0), stop=(part == 2))
                    last.then_inc(sem["hh_ps"], 1)

                def expert_out(j):
                    e = j // 2
                    pe.wait_ge(sem["hidden"], at(pair, "hidden", 2 * j + 2))
                    if j >= 2:
                        pe.wait_ge(sem["gated"], at(pair, "gated", 2 * (j - 1)))
                    for g in range(2):
                        mm(ps[D * g:D * g + D, 4 + j % 2, :], w3[:, e, :], hidden_slot(2 * j + g),
                           start=True, stop=True).then_inc(sem["expert_ps"], 1)
                    if j == 0:
                        pe.wait_ge(sem["gates_split"], at(pair, "gates_split", 1))
                    if j >= 2:
                        pe.wait_ge(sem["gate_sb"], at(pair, "gate_sb", 2 * (j - 1)))
                    cols = slice((j % 2) * CH, (j % 2 + 1) * CH)
                    for g in range(2):
                        r = g * NX + e
                        mm(ps[D * g:D * g + D, 6 + j % 2, :], pick[:, r:r + 1].to_broadcast([P, D]),
                           gatesT[:, cols], start=True, stop=True).then_inc(sem["gate_ps"], 1)

                pe.wait_ge(w12_split, 10)
                for j in range(STEPS):
                    if j < 2 * NX:
                        hidden(2 * j)
                        hidden(2 * j + 1)
                    if j == LEAD - 2:
                        pe.wait_ge(sem["gates_ready"], at(pair, "gates_ready", 1))
                        for t in range(NT):
                            m = pe.transpose(ps[:, 6 + t // 4, (t % 4) * P:(t % 4 + 1) * P],
                                             gates4[:, t].rearrange("p r x -> p (r x)"), ident)
                        m.then_inc(sem["gatesT_ps"], 1)
                    for o_ in OUT_STEPS[j]:
                        expert_out(o_)
                norm(1)

                for c in range(NC):
                    pe.wait_ge(sem["h_ready"], at(pair, "h_ready", NN + NN // NC * (c + 1)))
                    mm(ps[:, 2 + c, :], ak_bd[:, :], h[2][:, c * CH:(c + 1) * CH], start=True, stop=True)\
                        .then_inc(sem["ak_ps"], 1)
                    mm(ps[:, c, :], aq_bd[:, :], h[2][:, c * CH:(c + 1) * CH], start=True, stop=True)\
                        .then_inc(sem["aq_ps"], 1)
                def att_scores(w):
                    c = w // (NW // NC)
                    pe.wait_ge(sem["q_blocks"], at(pair, "q_blocks", 2 * NC if w else 2))
                    pe.wait_ge(sem["q_zero"], at(pair, "q_zero", 2))
                    pe.wait_ge(sem["k_blocks"], at(pair, "k_blocks", K_SPLIT * (c + 1)))
                    pe.wait_ge(sem["k_blocks_dve"], at(pair, "k_blocks_dve", (H - K_SPLIT) * (c + 1)))
                    if w >= 2:
                        pe.wait_ge(sem["biased"], at(pair, "biased", w - 1))
                    mm(ps[:, w % 2, :], qb[:, w, :], kb[:, w].rearrange("p a b -> p (a b)"), start=True, stop=True)\
                        .then_inc(sem["att_ps"], 1)

                def att_turn(w):
                    if w == 1:
                        pe.wait_ge(sem["k_blocks"], at(pair, "k_blocks", 2 * K_SPLIT))
                    pe.wait_ge(sem["att_exp"], at(pair, "att_exp", w + 1))
                    if w >= 2:
                        pe.wait_ge(sem["probT_sb"], at(pair, "probT_sb", w - 1))
                    for hp in range(H // 2):
                        m = pe.transpose(ps[:, 2 + w % 2, hp * P:(hp + 1) * P],
                                         att_prob(w)[:, hp * P:(hp + 1) * P], ident)
                    m.then_inc(sem["probT_ps"], 1)

                def att_values(w):
                    m2_, ww = divmod(w, 2)
                    pe.wait_ge(sem["probT_sb"], at(pair, "probT_sb", w + 1))
                    pe.wait_ge(sem["v_blocks"], at(pair, "v_blocks", 4))
                    if m2_ >= 2 and ww == 0:
                        pe.wait_ge(sem["outT_sb"], at(pair, "outT_sb", m2_ - 1))
                    o = ps[:, 4 + m2_ % 2, ww * 144:(ww + 1) * 144].rearrange("p (g hp r) -> p g hp r", g=2, hp=H // 2)
                    for hp in range(H // 2):
                        m = mm(o[:, :, hp, :], att_probT(w)[:, hp * P:(hp + 1) * P],
                               vb[:, w, hp].rearrange("p g a b -> p g (a b)"), start=True, stop=True)
                    m.then_inc(sem["pv_ps"], 1)

                def att_out_turn(m_):
                    pe.wait_ge(sem["normed"], at(pair, "normed", 2 * m_ + 2))
                    pe.transpose(ps[:, 4 + m_ % 2, 3 * P:4 * P], att_out(m_), ident).then_inc(sem["outT_ps"], 1)

                def att_proj(m_):
                    pe.wait_ge(sem["outT_sb"], at(pair, "outT_sb", m_ + 1))
                    for ww in range(2):
                        col = (2 * m_ + ww) * WS
                        for g in range(2):
                            m = mm(ps[D * g:D * g + D, 6 + col // CH, col % CH:col % CH + WS], projT[:, ww, :],
                                   att_outT(m_)[:, g * WS:(g + 1) * WS], start=False, stop=True,
                                   skip_group_check=True)
                    m.then_inc(sem["proj_ps"], 1)

                att_scores(0)
                att_scores(1)
                by_parity = av_bd[:, :].rearrange("p (c a d) -> p c a d", a=2, d=HD)
                for w in range(NW):
                    for a in range(2):
                        m = mm(ps[D * a:D * a + D, 4 + w // 8, (w % 8) * D:(w % 8 + 1) * D],
                               h[2][:, w * WS:(w + 1) * WS], by_parity[:, :, a, :], start=True, stop=True)
                    if w % 8 == 7:
                        m.then_inc(sem["av_ps"], 1)

                for s in range(2, NW + 6):
                    if s < NW:
                        att_scores(s)
                    if 0 <= s - 2 < NW:
                        att_turn(s - 2)
                    if s == 2:
                        for c in range(NC):
                            mm(ps[:, 6 + c, :], ident, h[2][:, c * CH:(c + 1) * CH], start=True, stop=True)
                    if 0 <= s - 3 < NW:
                        att_values(s - 3)
                    if s >= 5 and (s - 5) % 2 == 0 and (s - 5) // 2 < NW // 2:
                        att_out_turn((s - 5) // 2)
                    if s >= 6 and (s - 6) % 2 == 0 and (s - 6) // 2 < NW // 2:
                        att_proj((s - 6) // 2)
                norm(2)

                for c in range(NC):
                    pe.wait_ge(sem["h_ready"], at(pair, "h_ready", 2 * NN + NN // NC * (c + 1)))
                    for g in range(2):
                        mm(ps[:, 2 * g + c, :], fiT[:, g, :], h[3][:, c * CH:(c + 1) * CH],
                           start=True, stop=True).then_inc(sem["f_in_ps"], 1)
                pe.wait_ge(sem["w_routed"], at(pair, "w_routed", PER["w_routed"]))
                for l in range(LAYERS):
                    for c in range(NC):
                        for g in range(2):
                            name = ("f0_first", "f0_second", "l0_first", "l0_second")[2 * l + g]
                            pe.wait_ge(sem[name], at(pair, name, c + 1))
                            base = (4 if l == 0 else 0) + 2 * g
                            for t in range(c * HT, (c + 1) * HT):
                                m = mm(ps[:, base + c, (t % HT) * P:(t % HT + 1) * P], w_ring[:, l, g, t, 0:HID],
                                       ffn_in(l, g)[:, t * P:(t + 1) * P], start=True, stop=True)
                            m.then_inc(sem["l0_ps" if l == 0 else "l1_ps"], 1)
                for c in range(NC):
                    mm(ps[:, 4 + c, :], ident, h[3][:, c * CH:(c + 1) * CH], start=True, stop=True)
                for c in range(NC):
                    pe.wait_ge(sem["l1_first"], at(pair, "l1_first", c + 1))
                    pe.wait_ge(sem["l1_second"], at(pair, "l1_second", c + 1))
                    for g in range(2):
                        m = mm(ps[D * g:D * g + D, 4 + c, :], foT, ffn_in(2, g)[:, c * CH:(c + 1) * CH],
                               start=False, stop=True, skip_group_check=True)
                    m.then_inc(sem["r_ready"], 1)
                norm(3)

        @block.scalar
        def _(act):
            act.wait_ge(mix_loaded, 16 * MIX_LOADS)
            for dst, src in [(wsT, i["wsT"]), (table, i["table"])]:
                act.dma_start(dst, src).then_inc(table_loaded, 16)
            for m, name in enumerate(("w1", "w2")):
                for a in range(2):
                    act.dma_start(w12[m][D * a:D * a + D], i[name]).then_inc(w12_loaded, 16)
            act.wait_ge(fold_ps, 1)
            count, per = [0], ACT_CHAIN
            act.activation(wvo_bd[0:D, 0:D], ps[0:D, 4, 0:D], ACT.Copy)
            act.activation(wvo_bd[D:P, D:P], ps[D:P, 4, 0:D], ACT.Copy)
            for g in range(2):
                act.activation(vo_row[:, g * D:(g + 1) * D], ps[:, 5, 0:D], ACT.Copy)
            act.activation(out_bias[:, :], ps[:, 6, 0:2], ACT.Copy)
            act.activation(w_dt[:, :], ps[:, 7, 0:E], ACT.Copy).then_inc(fold_sb, 1)
            with act.Fori(0, PAIRS) as pair:
                count[0] = 0

                def then(ins):
                    link(act, act_chain, per, pair, count, ins)

                def norm(k):
                    for c in range(NN):
                        if k == 1:
                            act.wait_ge(sem["summed"], at(pair, "summed", 2 * (2 * NX - 1 + c // (NN // NC))))
                        elif k == 2:
                            act.wait_ge(sem["proj_ps"], at(pair, "proj_ps", NW // 2))
                        else:
                            act.wait_ge(sem["r_ready"], at(pair, "r_ready", R_COUNT[k] + c // (NN // NC) + 1))
                        act.activation(sq[:, c * NCH:(c + 1) * NCH], res_chunk(k, c), ACT.Square,
                                       bias=res_bias(k) if k >= 2 else 0.0).then_inc(sem["squared"], 1)
                    before = count[0]
                    for c in range(NN + 1):
                        if c < NN:
                            act.wait_ge(sem["var_ps"], at(pair, "var_ps", NN * k + c + 1))
                            act.activation(rs[:, c * NCH:(c + 1) * NCH], ps[:, VAR_BANKS[k][c], 0:NCH], ACT.Ln,
                                           bias=v("eps")).then_inc(act_chain, 1)
                        if c:
                            cols = slice((c - 1) * NCH, c * NCH)
                            act.wait_ge(act_chain, pair * per + before + c)
                            act.activation(rs[:, cols], rs[:, cols], ACT.Exp, scale=-0.5).then_inc(sem["rstd"], 1)
                    count[0] += NN

                for c in range(NC):
                    act.wait_ge(sem["q_ps"], at(pair, "q_ps", c + 1))
                    act.activation(q_tok[:, c * CH:(c + 1) * CH], ps[:, c, :], ACT.Identity, bias=v("bq"))\
                       .then_inc(sem["qk_sb"], 1)
                for c in range(NC):
                    act.wait_ge(sem["k_ps"], at(pair, "k_ps", c + 1))
                    act.activation(k_tok[0][0:D, c * CH:(c + 1) * CH], ps[0:D, 2 + c, :], ACT.Identity, bias=v("bk")[0:D])\
                       .then_inc(sem["qk_sb"], 1)
                for g in range(2):
                    half = slice(D * g, D * g + D)
                    for c in range(NC):
                        act.wait_ge(sem["retained"], at(pair, "retained", NC * ((g + 1) * NT - 1) + c + 1))
                        act.activation(y_pos[half, c * CH:(c + 1) * CH], ps[half, 4 + c, :], ACT.Relu,
                                       bias=v("bo_tok")[half]).then_inc(sem["y_pos"], 1)

                for g in range(2):
                    act.wait_ge(sem["xin_ps"], at(pair, "xin_ps", g + 1))
                    act.activation(xc[:, g, :], banks(2 * g), ACT.Silu, bias=v("conv_b")).then_inc(sem["xc_ready"], 1)
                    act.wait_ge(sem["z_ps"], at(pair, "z_ps", g + 1))
                    act.activation(zs[:, g, :], banks(4 + 2 * g), ACT.Silu).then_inc(sem["z_ready"], 1)
                act.preload_act_table_set("natural_log_exp_and_others")
                act.wait_ge(w12_split, 10)

                def first_parts(g):
                    act.wait_ge(sem["sel_ps"], at(pair, "sel_ps", g + 1))
                    act.activation(bc[:, g, :], banks(SEL_BANK[g]), ACT.Copy).then_inc(sem["sel_hi"], 1)

                def dt_above(g):
                    act.wait_ge(sem["dt_ps"], at(pair, "dt_ps", g + 1))
                    act.activation(dt_pos(g), banks(DT_BANK[g]), ACT.Relu, bias=v("dt_b"))

                def dt_size(g):
                    act.activation(dt_neg(g), banks(DT_BANK[g]), ACT.Abs, bias=v("dt_b")).then_inc(sem["dt_read"], 1)

                def exp_dt(g):
                    act.wait_ge(sem["dt_read"], at(pair, "dt_read", g + 1))
                    act.activation(dt_neg(g), dt_neg(g), ACT.Exp, scale=-1.0).then_inc(sem["dt_exp"], 1)

                def log_dt(g):
                    act.wait_ge(sem["dt_exp"], at(pair, "dt_exp", g + 1))
                    act.activation(dt_neg(g), dt_neg(g), ACT.Ln, bias=v("one")).then_inc(sem["dt_ln"], 1)

                def decay(k):
                    if k >= 2:
                        act.wait_ge(sem["scanned"], at(pair, "scanned", k - 1))
                    name = "dt_late" if k >= NS else "dt_ready"
                    act.wait_ge(sem[name], at(pair, name, PER[name]))
                    act.activation(dA_slot(k), dt[:, k // NS, :], ACT.Exp, scale=v("A", k % NS))\
                       .then_inc(sem["dA_ready"], 1)

                def copy_c(k):
                    act.wait_ge(sem["c_ps"], at(pair, "c_ps", k + 1))
                    if k >= 2:
                        act.wait_ge(sem["hc_ready"], at(pair, "hc_ready", k - 1))
                    act.activation(c_slot(k), banks(4), ACT.Copy).then_inc(sem["c_sb"], 1)

                first_parts(0)
                dt_above(0)
                dt_size(0)
                exp_dt(0)
                log_dt(0)
                first_parts(1)
                dt_above(1)
                dt_size(1)
                decay(0)
                copy_c(0)
                decay(1)
                copy_c(1)
                for k in range(2, 2 * NS):
                    decay(k)
                    if k == 2:
                        exp_dt(1)
                    if k == 3:
                        log_dt(1)
                    if k == NS + 2:
                        act.wait_ge(sem["y_summed"], at(pair, "y_summed", NS))
                        act.activation(y_sum, banks(6), ACT.Copy).then_inc(sem["y_copied"], 1)
                    copy_c(k)
                norm(0)

                cols = slice(CH, T)
                act.wait_ge(sem["x_high"], at(pair, "x_high", NN))
                for g in range(2):
                    own = slice(D * g, D * g + D)
                    act.activation(x_a[own, g, cols], h[1][own, cols], ACT.Copy)
                    act.activation(x_b[own, g, cols], h[1][own, cols], ACT.Copy)
                act.wait_ge(sem["x_rest"], at(pair, "x_rest", NN))
                for g in range(2):
                    own, other = slice(D * g, D * g + D), slice(D * (1 - g), D * (1 - g) + D)
                    m = act.activation(x_a[other, g, cols], x_left[own, cols], ACT.Copy)
                m.then_inc(sem["x_copied"], 1)
                for j in range(STEPS):
                    if j == LEAD - 1:
                        act.wait_ge(sem["gatesT_ps"], at(pair, "gatesT_ps", 1))
                        act.activation(gatesT, banks(6), ACT.Copy).then_inc(sem["gates_hi"], 1)
                    for k in (2 * j, 2 * j + 1) if j < 2 * NX else ():
                        act.wait_ge(sem["hh_ps"], at(pair, "hh_ps", k + 1))
                        if k >= 2:
                            act.wait_ge(sem["hidden"], at(pair, "hidden", k - 1))
                        act.activation(scratch[:, 0, (k % 2) * CH:(k % 2 + 1) * CH], ps[:, k % 2, :], ACT.Silu)\
                           .then_inc(sem["silu_ready"], 1)
                        if k == 0:
                            act.wait_ge(sem["top_diff"], at(pair, "top_diff", 1))
                            act.activation(g2[:, :], g1[:, :], ACT.Silu).then_inc(sem["top_silu"], 1)
                    for i_ in OUT_STEPS[j]:
                        act.wait_ge(sem["gate_ps"], at(pair, "gate_ps", 2 * (i_ + 1)))
                        if i_ >= 2:
                            act.wait_ge(sem["gated"], at(pair, "gated", 2 * (i_ - 1)))
                        act.activation(gate_slot(i_), ps[:, 6 + i_ % 2, :], ACT.Copy).then_inc(sem["gate_sb"], 2)
                act.preload_act_table_set("natural_log_exp_and_others")
                norm(1)

                def q_blocks(c):
                    act.wait_ge(sem["aq_ps"], at(pair, "aq_ps", c + 1))
                    for g in range(2):
                        half = slice(D * g, D * g + D)
                        act.activation(qb[half, NW // NC * c:NW // NC * (c + 1), D * g:D * g + WS],
                                       ps[half, c, :].rearrange("p (a b) -> p a b", b=WS), ACT.Copy,
                                       scale=float(HD) ** -0.5).then_inc(sem["q_blocks"], 1)

                for c in range(NC):
                    act.wait_ge(sem["ak_ps"], at(pair, "ak_ps", c + 1))
                    act.activation(k_sb[:, c * CH:(c + 1) * CH], ps[:, 2 + c, :], ACT.Copy).then_inc(sem["k_copied"], 1)
                    if c:
                        q_blocks(c)
                    for hh in range(K_SPLIT):
                        act.activation(kb[:, NW // NC * c:NW // NC * (c + 1), hh, :],
                                       ps[:, 2 + c, :].rearrange("p (a b) -> p a b", b=WS), ACT.Copy,
                                       scale=head_mask[:, hh:hh + 1]).then_inc(sem["k_blocks"], 1)
                    if not c:
                        q_blocks(c)
                for s in range(NW + 4):
                    if s < NW:
                        act.wait_ge(sem["shifted"], at(pair, "shifted", s + 1))
                        if s >= 2:
                            act.wait_ge(sem["probT_ps"], at(pair, "probT_ps", s - 1))
                        act.activation(att_prob(s), att_shift(s), ACT.Exp).then_inc(sem["att_exp"], 1)
                    if 0 <= s - 1 < NW:
                        w = s - 1
                        act.wait_ge(sem["probT_ps"], at(pair, "probT_ps", w + 1))
                        if w >= 2:
                            act.wait_ge(sem["pv_ps"], at(pair, "pv_ps", w - 1))
                        act.activation(att_probT(w), ps[:, 2 + w % 2, :], ACT.Copy).then_inc(sem["probT_sb"], 1)
                    if s >= 3 and (s - 3) % 2 == 0 and (s - 3) // 2 < NW // 2:
                        m_ = (s - 3) // 2
                        act.wait_ge(sem["outT_ps"], at(pair, "outT_ps", m_ + 1))
                        if m_ >= 2:
                            act.wait_ge(sem["proj_ps"], at(pair, "proj_ps", m_ - 1))
                        act.activation(att_outT(m_), ps[:, 4 + m_ % 2, 3 * P:4 * P], ACT.Copy)\
                           .then_inc(sem["outT_sb"], 1)
                norm(2)

                for c in range(NC):
                    act.wait_ge(sem["f_in_ps"], at(pair, "f_in_ps", 2 * c + 1))
                    act.activation(ffn_in(0, 0)[:, c * CH:(c + 1) * CH], ps[:, c, :], ACT.Relu, bias=v("bi"))\
                       .then_inc(sem["f0_first"], 1)
                for l in range(LAYERS):
                    name = "l0_ps" if l == 0 else "l1_ps"
                    for c in range(NC):
                        act.wait_ge(sem[name], at(pair, name, 2 * c + 1))
                        for t in range(c * HT, (c + 1) * HT):
                            m = act.activation(ffn_in(l + 1, 0)[:, t * P:(t + 1) * P],
                                               ps[:, (4 if l == 0 else 0) + c, (t % HT) * P:(t % HT + 1) * P],
                                               ACT.Relu, bias=w_ring[:, l, 0, t, HID:HID + 1])
                        m.then_inc(sem["l0_first" if l == 0 else "l1_first"], 1)
                norm(3)
                assert count[0] == per, count[0]

        @block.vector
        def _(dve):
            def clear_k():
                for g in range(2):
                    dve.memset(k_tok[g][D * (1 - g):D * (1 - g) + D, :], 0.0).then_inc(sem["k_zero"], 1)

            dve.wait_ge(padded, 1)
            for a in range(2):
                dve.memset(vb[D * a:D * a + D, :, :, :, a, HD:HD + 1], 1.0)
            clear_k()
            dve.memset(m1[:, :], 0.0).then_inc(pair_done, 1)
            dve.wait_ge(mix_loaded, 16 * MIX_LOADS)
            with dve.Fori(0, PAIRS) as pair:
                count, per = [0], DVE_CHAIN

                def then(ins):
                    link(dve, dve_chain, per, pair, count, ins)

                def norm(k):
                    for c in range(NN):
                        cols = slice(c * NCH, (c + 1) * NCH)
                        r = res_chunk(k, c)
                        dve.wait_ge(sem["rstd"], at(pair, "rstd", NN * k + c + 1))
                        if k >= 2:
                            dve.scalar_tensor_tensor(out=h[k + 1][:, cols], in0=r, scalar=res_bias(k), in1=rs[:, cols],
                                                     op0=ALU.add, op1=ALU.mult).then_inc(sem["h_ready"], 1)
                        else:
                            dve.tensor_tensor(h[k + 1][:, cols], r, rs[:, cols], ALU.mult)\
                               .then_inc(sem["h_ready"], 1)
                        if k == 0:
                            if c:
                                rest(c - 1)
                            dve.wait_ge(sem["h_ready"], at(pair, "h_ready", c + 1))
                            dve.tensor_copy(x_part[:, 0, cols], h[1][:, cols]).then_inc(sem["x_high"], 1)
                    if k == 0:
                        rest(NN - 1)
                        dve.wait_ge(sem["x_rest"], at(pair, "x_rest", NN))
                        dve.tensor_copy(x_part[:, 1, :], x_left).then_inc(sem["x_low"], 1)

                def rest(c):
                    cols = slice(c * NCH, (c + 1) * NCH)
                    dve.wait_ge(sem["x_high"], at(pair, "x_high", c + 1))
                    dve.tensor_tensor(x_left[:, cols], h[1][:, cols], x_part[:, 0, cols],
                                      ALU.subtract).then_inc(sem["x_rest"], 1)

                for c in range(NC):
                    dve.wait_ge(sem["k_ps"], at(pair, "k_ps", c + 1))
                    dve.tensor_scalar(k_tok[1][D:P, c * CH:(c + 1) * CH], ps[D:P, 2 + c, :], v("bk")[D:P], None,
                                      ALU.add).then_inc(sem["k_late"], 1)
                for c in range(2):
                    dve.wait_ge(sem["vw_ps"], at(pair, "vw_ps", c + 1))
                    dve.tensor_tensor(vw[:, 4 * c:4 * c + 4, :], ps[:, 6 + c, :].rearrange("p (a b) -> p a b", a=4),
                                      vo_row[:, :].unsqueeze(1).to_broadcast([P, 4, P]), ALU.add)\
                       .then_inc(sem["vw_sb"], 1)
                def shrink(g, c):
                    half = slice(D * g, D * g + D)
                    cols = slice(c * CH, (c + 1) * CH)
                    dve.wait_ge(sem["y_pos"], at(pair, "y_pos", NC * g + c + 1))
                    dve.tensor_scalar(y_neg[half, cols], ps[half, 4 + c, :], v("bo_tok")[half], 0.0,
                                      ALU.add, ALU.min).then_inc(sem["y_neg"], 1)
                    dve.wait_ge(sem["y_neg"], at(pair, "y_neg", NC * g + c + 1))
                    if g == 0 and c == 0:
                        dve.wait_ge(sem["stored"], at(pair, "stored", 16))
                    dve.scalar_tensor_tensor(out=h[0][half, cols], in0=y_neg[half, cols], scalar=v("prelu")[half],
                                             in1=y_pos[half, cols], op0=ALU.mult, op1=ALU.add)\
                       .then_inc(sem["h0_ready"], 1)

                def taps_now(g):
                    own = slice(D * g, D * g + D)
                    dve.wait_ge(sem["h0_ready"], at(pair, "h0_ready", NC * (g + 1)))
                    dve.tensor_copy(taps[own, g, 3:3 + T], h[0][own, :]).then_inc(sem["taps_ready"], 1)

                def taps_before(g):
                    own, other = slice(D * g, D * g + D), slice(D * (1 - g), D * (1 - g) + D)
                    dve.tensor_copy(taps[other, g, 4:3 + T], h[0][own, 0:T - 1]).then_inc(sem["taps_ready"], 1)

                for k in range(2 * NT):
                    dve.wait_ge(decay_loaded[k % NT], 16)
                    dve.wait_ge(sem["scores"], at(pair, "scores", k + 1))
                    if k in (NT + 2, NT + 4):
                        shrink(0, (k - NT - 2) // 2)
                    if k == NT + 6:
                        taps_now(0)
                    if k == NT + 7:
                        taps_before(0)
                    if k >= 4:
                        dve.wait_ge(sem["retained"], at(pair, "retained", NC * (k - 3)))
                    dve.tensor_tensor(scratch[:, k % 4], banks(2 * (k % 2)), decayT[:, k % NT, :], ALU.mult)\
                       .then_inc(sem["masked"], 1)
                for c in range(NC):
                    shrink(1, c)
                taps_now(1)
                taps_before(1)

                def rest_of(g):
                    return scratch[:, 6] if g == 0 else y_sum

                def sel_rest(g):
                    dve.wait_ge(sem["sel_hi"], at(pair, "sel_hi", g + 1))
                    dve.tensor_tensor(rest_of(g)[D:P], banks(SEL_BANK[g])[D:P], bc[D:P, g, :], ALU.subtract)\
                       .then_inc(sem["sel_read"], 1)

                def split_middle(g):
                    dve.wait_ge(sem["sel_read"], at(pair, "sel_read", g + 1))
                    then(dve.tensor_copy(bc[D:P, g, :], rest_of(g)[D:P]))

                def split_low(g, cols):
                    dve.tensor_tensor(bc[96:P, g, cols], rest_of(g)[96:P, cols], bc[96:P, g, cols], ALU.subtract)\
                       .then_inc(sem["sel_split"], 1)

                dve.wait_ge(out_centred, SUM_STEPS + 2)
                dve.wait_ge(w12_split, 10)
                sel_rest(0)
                split_middle(0)
                split_low(0, slice(0, T))
                dve.wait_ge(sem["dt_ln"], at(pair, "dt_ln", 1))
                dve.tensor_tensor(dt[:, 0, :], dt_pos(0), dt_neg(0), ALU.add).then_inc(sem["dt_ready"], 1)
                dve.wait_ge(sem["dt_ready"], at(pair, "dt_ready", 1))
                dve.tensor_tensor(u[:, 0, :], dt[:, 0, :], xc[:, 0, :], ALU.mult).then_inc(sem["u_ready"], 1)
                dve.wait_ge(sem["u_ready"], at(pair, "u_ready", 1))

                def drive(k):
                    dve.wait_ge(sem["b_ps"], at(pair, "b_ps", k + 1))
                    if k >= 2:
                        dve.wait_ge(sem["scanned"], at(pair, "scanned", k - 1))
                    if k == NS:
                        dve.wait_ge(sem["u_late"], at(pair, "u_late", NN))
                    dve.tensor_tensor(dbu_slot(k), u[:, k // NS, :], banks(2 * (k % 2)), ALU.mult)\
                       .then_inc(sem["dbu_ready"], 1)

                def scan(k):
                    dve.wait_ge(sem["dA_ready"], at(pair, "dA_ready", k + 1))
                    dve.wait_ge(sem["dbu_ready"], at(pair, "dbu_ready", k + 1))
                    if k >= 3:
                        dve.wait_ge(sem["hc_ready"], at(pair, "hc_ready", k - 2))
                    dve.tensor_tensor_scan(hs_slot(k), dA_slot(k), dbu_slot(k), 0.0,
                                           ALU.mult, ALU.add).then_inc(sem["scanned"], 1)

                drive(0)
                scan(0)
                sel_rest(1)
                drive(1)
                for k in range(1, 2 * NS):
                    if k + 1 < 2 * NS:
                        drive(k + 1)
                    scan(k)
                    if k == MIDDLE_LATE:
                        split_middle(1)
                    if k in LOW_LATE:
                        c = LOW_LATE.index(k)
                        split_low(1, slice(c * CH, (c + 1) * CH))
                    if k in DT_LATE:
                        c = DT_LATE.index(k)
                        cols = slice(c * NCH, (c + 1) * NCH)
                        dve.wait_ge(sem["dt_ln"], at(pair, "dt_ln", 2))
                        dve.tensor_tensor(dt[:, 1, cols], dt_pos(1)[:, cols], dt_neg(1)[:, cols],
                                          ALU.add).then_inc(sem["dt_late"], 1)
                    if k in Y_LATE:
                        c = Y_LATE.index(k)
                        cols = slice(c * CH, (c + 1) * CH)
                        dve.wait_ge(sem["y_copied"], at(pair, "y_copied", 1))
                        dve.scalar_tensor_tensor(out=u[:, 0, cols], in0=xc[:, 0, cols], scalar=v("D"),
                                                 in1=y_sum[:, cols], op0=ALU.mult, op1=ALU.add)\
                           .then_inc(sem["y_read"], 1)
                    if k in Y_GATED:
                        c = Y_GATED.index(k)
                        cols = slice(c * CH, (c + 1) * CH)
                        dve.wait_ge(sem["y_read"], at(pair, "y_read", c + 1))
                        dve.tensor_tensor(u[:, 0, cols], u[:, 0, cols], zs[:, 0, cols], ALU.mult)\
                           .then_inc(sem["gated_y"], 1)
                for c in range(NC):
                    cols = slice(c * CH, (c + 1) * CH)
                    dve.wait_ge(sem["y_summed"], at(pair, "y_summed", 2 * NS + c))
                    dve.scalar_tensor_tensor(out=u[:, 1, cols], in0=xc[:, 1, cols], scalar=v("D"),
                                             in1=ps[:, 6 + c, :], op0=ALU.mult, op1=ALU.add).then_inc(sem["y_read"], 1)
                    dve.wait_ge(sem["y_read"], at(pair, "y_read", NC + 1 + c))
                    dve.tensor_tensor(u[:, 1, cols], u[:, 1, cols], zs[:, 1, cols], ALU.mult)\
                       .then_inc(sem["gated_y"], 1)
                norm(0)

                dve.wait_ge(sem["x_low"], at(pair, "x_low", 1))
                cols = slice(0, CH)
                for g in range(2):
                    own, other = slice(D * g, D * g + D), slice(D * (1 - g), D * (1 - g) + D)
                    dve.tensor_copy(x_a[own, g, cols], x_part[own, 0, cols])
                    dve.tensor_copy(x_b[own, g, cols], x_part[own, 0, cols])
                    m = dve.tensor_copy(x_a[other, g, cols], x_part[own, 1, cols])
                m.then_inc(sem["x_split"], 1)

                def multiply(k):
                    dve.wait_ge(sem["silu_ready"], at(pair, "silu_ready", k + 1))
                    if k >= HIDDEN_RING:
                        dve.wait_ge(sem["expert_ps"], at(pair, "expert_ps", k - HIDDEN_RING + 1))
                    dve.tensor_tensor(hidden_slot(k), scratch[:, 0, (k % 2) * CH:(k % 2 + 1) * CH], ps[:, 2 + k % 2, :],
                                      ALU.mult).then_inc(sem["hidden"], 1)

                dve.wait_ge(sem["logit_ps"], at(pair, "logit_ps", 1))
                G = NT * 2
                def wide(t):
                    return t[:, :].unsqueeze(2).to_broadcast([P, G, NX])
                order_b = order.unsqueeze(1).to_broadcast([P, G, NX])
                then(dve.tensor_tensor(logits[:, :, :], ps[:, 6, 0:G * NX].rearrange("p (a b) -> p a b", a=G),
                                       gate_row.unsqueeze(1).to_broadcast([P, G, NX]), ALU.add))
                then(dve.tensor_reduce(m1[:, :], logits[:, :, :], AX.X, ALU.max))
                then(dve.tensor_tensor(hit[:, :, :], logits[:, :, :], wide(m1), ALU.is_equal))
                then(dve.tensor_tensor(hit[:, :, :], hit[:, :, :], order_b, ALU.mult))
                then(dve.tensor_reduce(mo[:, :], hit[:, :, :], AX.X, ALU.max))
                then(dve.tensor_tensor(pick1[:, :, :], order_b, wide(mo), ALU.is_equal))
                then(dve.scalar_tensor_tensor(out=logits2[:, :, :], in0=pick1[:, :, :], scalar=-3.0e38,
                                              in1=logits[:, :, :], op0=ALU.mult, op1=ALU.add))
                then(dve.tensor_reduce(m2[:, :], logits2[:, :, :], AX.X, ALU.max))
                then(dve.tensor_tensor(g2[:, :], m2[:, :], m1[:, :], ALU.subtract))
                dve.tensor_scalar(g1[:, :], g2[:, :], -1e-10, None, ALU.min).then_inc(sem["top_diff"], 1)
                multiply(0)
                then(dve.tensor_tensor(hit[:, :, :], logits2[:, :, :], wide(m2), ALU.is_equal))
                then(dve.tensor_tensor(hit[:, :, :], hit[:, :, :], order_b, ALU.mult))
                multiply(1)
                then(dve.tensor_reduce(mo[:, :], hit[:, :, :], AX.X, ALU.max))
                then(dve.tensor_tensor(pick2[:, :, :], order_b, wide(mo), ALU.is_equal))

                dve.wait_ge(sem["top_silu"], at(pair, "top_silu", 1))
                multiply(2)
                then(dve.reciprocal(g1[:, :], g1[:, :]))
                then(dve.tensor_tensor(g2[:, :], g2[:, :], g1[:, :], ALU.mult))
                then(dve.tensor_scalar(g1[:, :], g2[:, :], -1.0, 1.0, ALU.mult, ALU.add))
                multiply(3)
                then(dve.tensor_tensor(pick1[:, :, :], pick1[:, :, :], wide(g1), ALU.mult))
                then(dve.tensor_tensor(pick2[:, :, :], pick2[:, :, :], wide(g2), ALU.mult))
                multiply(4)
                then(dve.tensor_tensor(gates[:, :, :], pick1[:, :, :], pick2[:, :, :], ALU.add))
                multiply(5)
                dve.tensor_copy(gates4, gates[:, :, :].rearrange("p (t g) e -> p t (g e)", g=2).unsqueeze(2)
                                .to_broadcast([P, NT, 4, 2 * NX])).then_inc(sem["gates_ready"], 1)
                multiply(6)
                multiply(7)
                dve.wait_ge(sem["gates_hi"], at(pair, "gates_hi", 1))
                then(dve.tensor_tensor(gates_left[D:P], banks(6)[D:P], gatesT[D:P], ALU.subtract))
                multiply(8)
                then(dve.tensor_copy(gatesT[D:P], gates_left[D:P]))
                multiply(9)
                dve.tensor_tensor(gatesT[96:P], gates_left[96:P], gatesT[96:P], ALU.subtract)\
                   .then_inc(sem["gates_split"], 1)

                def gate(j):
                    dve.wait_ge(sem["expert_ps"], at(pair, "expert_ps", 2 * (j + 1)))
                    dve.wait_ge(sem["gate_sb"], at(pair, "gate_sb", 2 * (j + 1)))
                    if j >= 2:
                        dve.wait_ge(sem["summed"], at(pair, "summed", 2 * (j - 1)))
                    dve.tensor_tensor(gated_out(j), gate_slot(j), ps[:, 4 + j % 2, :],
                                      ALU.mult).then_inc(sem["gated"], 2)
                    if j >= 2 * NX - 2:
                        dve.wait_ge(sem["gated"], at(pair, "gated", 2 * (j + 1)))
                        dve.wait_ge(sem["summed"], at(pair, "summed", 2 * j))
                        half = acc[:, (j % 2) * CH:(j % 2 + 1) * CH]
                        dve.tensor_tensor(half, gated_out(j), half, ALU.add).then_inc(sem["summed"], 2)

                for j in range(5, STEPS):
                    if j < 2 * NX:
                        multiply(2 * j)
                        multiply(2 * j + 1)
                    for o_ in OUT_STEPS[j]:
                        gate(o_)
                for g in range(2):
                    dve.wait_ge(sem["gated"], at(pair, "gated", 4 * NX))
                    dve.memset(qb[D * g:D * g + D, :, D * (1 - g):D * (1 - g) + D], 0.0).then_inc(sem["q_zero"], 1)
                norm(1)

                def k_blocks(c):
                    dve.wait_ge(sem["k_copied"], at(pair, "k_copied", c + 1))
                    for hh in range(K_SPLIT, H):
                        dve.tensor_scalar(kb[:, NW // NC * c:NW // NC * (c + 1), hh, :],
                                          k_sb[:, c * CH:(c + 1) * CH].rearrange("p (a b) -> p a b", b=WS),
                                          head_mask[:, hh:hh + 1], None, ALU.mult).then_inc(sem["k_blocks_dve"], 1)

                k_blocks(0)

                def att_norm(m_):
                    dve.wait_ge(sem["pv_ps"], at(pair, "pv_ps", 2 * m_ + 2))
                    if m_ >= 2:
                        dve.wait_ge(sem["outT_ps"], at(pair, "outT_ps", m_ - 1))
                    o = ps[:, 4 + m_ % 2, 0:288].rearrange("p (w g h d) -> p w g h d", w=2, g=2, h=H)
                    for g in range(2):
                        half = slice(D * g, D * g + D)
                        m = dve.reciprocal(rsum[half, :, :], o[half, :, g, :, HD])
                        if g:
                            then(m)
                    for g in range(2):
                        half = slice(D * g, D * g + D)
                        dve.tensor_tensor(att_out(m_)[half].rearrange("p (w h d) -> p w h d", w=2, h=H),
                                          o[half, :, g, :, 0:HD],
                                          rsum[half, :, :].unsqueeze(3).to_broadcast([D, 2, H, HD]), ALU.mult)\
                           .then_inc(sem["normed"], 1)

                for s in range(NW + 4):
                    if s < NW:
                        dve.wait_ge(sem["att_ps"], at(pair, "att_ps", s + 1))
                        if s >= 2:
                            dve.wait_ge(sem["shifted"], at(pair, "shifted", s - 1))
                        t1 = att_bias(s).rearrange("p (a b) -> p a b", a=H)
                        dve.tensor_tensor(t1, ps[:, s % 2, :].rearrange("p (a b) -> p a b", a=H),
                                          rel_row.unsqueeze(1).to_broadcast([P, H, WS]), ALU.add)\
                           .then_inc(sem["biased"], 1)
                        dve.wait_ge(sem["biased"], at(pair, "biased", s + 1))
                        dve.tensor_reduce(rmax[:, s % 2, :], t1, AX.X, ALU.max).then_inc(sem["row_max"], 1)
                    if s == 0:
                        k_blocks(1)
                    if s == 1:
                        dve.wait_ge(sem["av_ps"], at(pair, "av_ps", 2))
                        av = banks(4).rearrange("p (w g hp d) -> p w g hp d", w=NW, g=2, hp=H // 2)
                        for a in range(2):
                            half = slice(D * a, D * a + D)
                            for g in range(2):
                                dve.tensor_copy(vb[half, :, :, g, a, 0:HD], av[half, :, g, :, :]).then_inc(sem["v_blocks"], 1)
                    if s >= 4 and (s - 4) % 2 == 0 and (s - 4) // 2 < NW // 2:
                        att_norm((s - 4) // 2)
                norm(2)

                for c in range(NC):
                    dve.wait_ge(sem["f_in_ps"], at(pair, "f_in_ps", 2 * c + 2))
                    dve.tensor_scalar(ffn_in(0, 1)[:, c * CH:(c + 1) * CH], ps[:, 2 + c, :], v("bi"), 0.0,
                                      ALU.add, ALU.max).then_inc(sem["f0_second"], 1)
                for l in range(LAYERS):
                    name = "l0_ps" if l == 0 else "l1_ps"
                    for c in range(NC):
                        dve.wait_ge(sem[name], at(pair, name, 2 * c + 2))
                        for t in range(c * HT, (c + 1) * HT):
                            m = dve.tensor_scalar(ffn_in(l + 1, 1)[:, t * P:(t + 1) * P],
                                                  ps[:, (6 if l == 0 else 2) + c, (t % HT) * P:(t % HT + 1) * P],
                                                  w_ring[:, l, 1, t, HID:HID + 1], 0.0, ALU.add, ALU.max)
                        m.then_inc(sem["l0_second" if l == 0 else "l1_second"], 1)
                dve.wait_ge(sem["l1_first"], at(pair, "l1_first", NC))
                clear_k()
                norm(3)
                dve.memset(m1[:, :], 0.0).then_inc(pair_done, 1)
                assert count[0] == per, count[0]


MIX_LOADS = 11
LOADS = 23
ACT_CHAIN = 16
DVE_CHAIN = 31


def kernel(**a):
    import ml_dtypes
    import numpy as _np
    import concourse.bacc as _bacc
    from concourse import mybir as _mybir
    from concourse.bass_utils import run_bass_kernel_spmd as _run

    a = {k: _np.asarray(x) for k, x in a.items()}
    f32 = _np.float32

    def col(x):
        x = x.reshape(-1)
        return _np.concatenate([x] * (P // x.size)).reshape(P, 1)

    vecs = dict(
        bq=col(a["L0_tok_bq"]), bk=col(a["L0_tok_bk"]), bv=col(a["L0_tok_bv"]),
        prelu=_np.broadcast_to(a["L0_tok_prelu_a"], (P, 1)), bo_tok=col(a["L0_tok_bo"]),
        conv_b=col(a["L0_attn_conv_b"]), dt_b=col(a["L0_attn_dt_b"]), A=a["L0_attn_A"], D=col(a["L0_attn_D_param"]),
        b_proj=col(a["L1_attn_b_proj"]), bo=col(a["L1_ffn_bo"]), bi=col(a["L1_ffn_bi"]),
        bs=a["L1_ffn_bs"].reshape(LAYERS, HID).T, eps=_np.full((P, 1), EPS, f32), one=_np.ones((P, 1), f32),
    )
    names, columns = [], []
    for n, x in vecs.items():
        names += [n] + [f"{n}_{k}" for k in range(1, x.shape[1])]
        columns.append(x)
    windows = _np.lib.stride_tricks.sliding_window_view(a["L1_attn_rel_bias"], WS)[::-1]
    rows = _np.concatenate([
        _np.broadcast_to(a["L0_ffn_gate_b"], (P, NX)),
        _np.concatenate([windows, windows])], axis=1)
    part = _np.arange(P)
    same = (part[:, None] // D == part[None, :] // D).astype(f32)
    head = (part[:, None] % D // HD == _np.arange(H)[None, :]).astype(f32)
    consts = _np.concatenate([
        _np.eye(P, dtype=f32), _np.eye(P, dtype=f32) - same / D, same / D, head,
        _np.broadcast_to(NX - _np.arange(NX, dtype=f32), (P, NX))], axis=1)
    pick = _np.zeros((P, 2 * NS), ml_dtypes.bfloat16)
    for q in (0, 2, 3):
        pick[32 * q + _np.arange(2 * NS), _np.arange(2 * NS)] = 1
    in_projT = a["L0_attn_in_proj_w"].T
    conv_w = a["L0_attn_conv_w"].reshape(E, 4)
    taps = _np.empty((P, 2, 2, E), f32)
    for g in range(2):
        for lag in range(2):
            taps[D * g:D * g + D, g, lag] = conv_w[:, 3 - 2 * lag]
            taps[D * (1 - g):D * (1 - g) + D, g, lag] = conv_w[:, 2 - 2 * lag]
    sel = a["L0_attn_sel_w"]
    qkv = a["L1_attn_w_qkv"]
    wr = a["L1_ffn_Wr"].transpose(3, 0, 1, 2)
    br = a["L1_ffn_br"].transpose(2, 0, 1)[..., None]
    xT = a["x"].reshape(2, PAIRS, T, D).transpose(0, 3, 1, 2).reshape(P, PAIRS * T)
    arrays = dict(
        x_first=xT[:, 0:T], x_next=xT[:, T:],
        decayT=a["L0_tok_d_gamma_batched"].T.reshape(NT, P, T).transpose(1, 0, 2),
        wq=a["L0_tok_Wq"], wk=a["L0_tok_Wk"], wvT=a["L0_tok_Wv"].T, wo_tok=a["L0_tok_Wo"],
        vec=_np.concatenate(columns, axis=1), rows=rows, consts=consts, pick=pick,
        taps=taps, in_xT=in_projT[:, 0:E],
        in_zT=in_projT[:, E:], selT=_np.concatenate([sel[NS:]] * 4).T, sel_dt=sel[:NS],
        dt_wT=a["L0_attn_dt_w"].T, out_wT=a["L0_attn_out_w"].T, gate_w=a["L0_ffn_gate_w"],
        w1=a["L0_ffn_w1"].transpose(1, 0, 2).reshape(D, 2, T), w2=a["L0_ffn_w2"].transpose(1, 0, 2).reshape(D, 2, T),
        w3=a["L0_ffn_w3"].transpose(1, 0, 2),
        aqT=qkv[0:D].T, akT=qkv[D:2 * D].T, avT=qkv[2 * D:3 * D].T, projT=a["L1_attn_w_proj"].T,
        fiT=a["L1_ffn_Wi"].T, foT=a["L1_ffn_Wo"].T, wsT=a["L1_ffn_Ws"].reshape(LAYERS, HID, HID).transpose(2, 0, 1),
        table=_np.concatenate([wr, br], axis=3), route=a["L1_ffn_route_id"].reshape(2, PAIRS, NT)
        .transpose(1, 0, 2).reshape(1, B * NT),
    )
    nc = _bacc.Bacc("TRN2", target_bir_lowering=False, num_devices=1)
    maps, ins = {}, {}
    for name, x in arrays.items():
        x = _np.ascontiguousarray(x)
        maps[f"in_{name}"] = x
        ins[name] = nc.dram_tensor(f"in_{name}", x.shape, _mybir.dt.from_np(x.dtype), kind="ExternalInput").ap()
    ins["vec_names"] = names
    out = nc.dram_tensor("out_0", (P, PAIRS * T), F32, kind="ExternalOutput").ap()
    build_tower(nc, ins, out)
    r = _run(nc, [maps], core_ids=[0])
    y = r.results[0]["out_0"]
    return y.reshape(2, D, PAIRS, T).transpose(0, 2, 3, 1).reshape(B, T, D)
```
